# Optimizing a Trainium2 kernel written in Bass

```python
import numpy as np
import jax
import jax.numpy as jnp

def _softmax(x, axis=-1):
    return jax.nn.softmax(x, axis=axis)

def _gelu(x):
    return jax.nn.gelu(x, approximate=True)

def _silu(x):
    return jax.nn.silu(x)

def _sigmoid(x):
    return jax.nn.sigmoid(x)

def _layernorm(x, axis=-1, eps=1e-05):
    m = jnp.mean(x, axis=axis, keepdims=True)
    v = jnp.var(x, axis=axis, keepdims=True)
    return (x - m) / jnp.sqrt(v + eps)

def _scatter_add(tgt, idx, src, axis=0):
    return tgt.at[idx].add(src)

def _segment_sum(src, seg, n):
    return jax.ops.segment_sum(src, seg, n)
kernel_name = 'mk_xattn_ffn_d1_seqx_r2_45fa94'

def setup_inputs(seed: int=0):
    np.random.seed(seed)
    _w = jnp.asarray

    def _rec_inputs():
        import jax
        import jax.numpy as jnp
        _rk = jax.random.key(seed)
        x = -0.0002928 + 1 * jax.random.normal(jax.random.fold_in(_rk, 1), (8, 1024, 512), jnp.float32)
        _lenS = 1024 - jax.random.randint(jax.random.fold_in(_rk, 7), (8,), 0, max(1, 1024 // 4) + 1, jnp.int32)
        _lenS2 = 1024 - jax.random.randint(jax.random.fold_in(_rk, 8), (8,), 0, max(1, 1024 // 4) + 1, jnp.int32)
        _ctx_1024P = jax.random.normal(jax.random.fold_in(_rk, 11), (8, 16, 512), jnp.float32)
        _ctx_1024c = jax.random.dirichlet(jax.random.fold_in(_rk, 511), 0.3 * jnp.ones((16,), jnp.float32), (8, 1024))
        _ctx_1024t = jnp.einsum('bsk,bkd->bsd', _ctx_1024c, _ctx_1024P)
        _ctx_1024t = _ctx_1024t * jax.lax.rsqrt(jnp.mean(jnp.square(_ctx_1024t)) + 1e-12) * 0.953939
        ctx_1024 = -1.39393e-06 + 0.999914 * (_ctx_1024t + 0.3 * jax.random.normal(jax.random.fold_in(_rk, 611), (8, 1024, 512), jnp.float32))
        return (x, ctx_1024)
    x, ctx_1024 = _rec_inputs()

    def _L0_xattn_setup():
        import jax, jax.numpy as jnp
        import numpy as np
        EMBED_DIM = 512
        NUM_HEADS = 16
        PROJ_DIM = EMBED_DIM // NUM_HEADS

        def _split_heads(x, B):
            return x.reshape(B, -1, NUM_HEADS, PROJ_DIM).transpose(0, 2, 1, 3)
        key = jax.random.key(seed)
        ks = jax.random.split(key, 11)
        B, S, D = (2, 1024, EMBED_DIM)
        scale = 1.0 / np.sqrt(D)
        inp = {'q': jax.random.normal(ks[0], (B, S, D), jnp.float32), 'k': jax.random.normal(ks[1], (B, S, D), jnp.float32), 'v': jax.random.normal(ks[2], (B, S, D), jnp.float32), 'Wq': jax.random.normal(ks[3], (D, D), jnp.float32) * scale, 'bq': jnp.zeros((D,), jnp.float32), 'Wk': jax.random.normal(ks[4], (D, D), jnp.float32) * scale, 'bk': jnp.zeros((D,), jnp.float32), 'Wv': jax.random.normal(ks[5], (D, D), jnp.float32) * scale, 'bv': jnp.zeros((D,), jnp.float32), 'Wo': jax.random.normal(ks[6], (D, D), jnp.float32) * scale, 'bo': jnp.zeros((D,), jnp.float32), 'use_causal_mask': 1}
        return inp
    _L0_xattn_all = _L0_xattn_setup()
    _L0_xattn_in = {k: v for k, v in _L0_xattn_all.items() if k in ('Wq', 'bq', 'Wk', 'bk', 'Wv', 'bv', 'Wo', 'bo')}
    del _L0_xattn_all

    def _L0_ffn_setup():
        import jax, jax.numpy as jnp
        import numpy as np

        def _ste(w, w_q):
            return w + jax.lax.stop_gradient(w_q - w)

        def quantize_w8_per(w, axis):
            amax = jnp.clip(jnp.max(jnp.abs(w), axis=axis, keepdims=True), 1e-08, None)
            scale = 127.0 / amax
            w_q = jnp.clip(jnp.round(w * scale), -128.0, 127.0) / scale
            return _ste(w, w_q)

        def quantize_a16(x):
            amax = jnp.clip(jnp.max(jnp.abs(x)), 1e-08, None)
            scale = 32767.0 / amax
            x_q = jnp.clip(jnp.round(x * scale), -32768.0, 32767.0) / scale
            return _ste(x, x_q)
        key = jax.random.key(seed)
        k1, k2, k3 = jax.random.split(key, 3)
        d_model, d_ff = (512, 2048)
        x = jax.random.normal(k1, (4, 1024, d_model), dtype=jnp.float32)
        W_in = jax.random.normal(k2, (d_model, d_ff), dtype=jnp.float32) / np.sqrt(d_model)
        b_in = jnp.zeros((d_ff,), dtype=jnp.float32)
        W_out = jax.random.normal(k3, (d_ff, d_model), dtype=jnp.float32) / np.sqrt(d_ff)
        b_out = jnp.zeros((d_model,), dtype=jnp.float32)
        return {'x': x, 'W_in': W_in, 'b_in': b_in, 'W_out': W_out, 'b_out': b_out}
    _L0_ffn_all = _L0_ffn_setup()
    _L0_ffn_in = {k: v for k, v in _L0_ffn_all.items() if k in ('W_in', 'b_in', 'W_out', 'b_out')}
    del _L0_ffn_all
    return {'x': x, 'ctx_1024': ctx_1024, 'L0_xattn_Wq': _L0_xattn_in['Wq'], 'L0_xattn_bq': _L0_xattn_in['bq'], 'L0_xattn_Wk': _L0_xattn_in['Wk'], 'L0_xattn_bk': _L0_xattn_in['bk'], 'L0_xattn_Wv': _L0_xattn_in['Wv'], 'L0_xattn_bv': _L0_xattn_in['bv'], 'L0_xattn_Wo': _L0_xattn_in['Wo'], 'L0_xattn_bo': _L0_xattn_in['bo'], 'L0_ffn_W_in': _L0_ffn_in['W_in'], 'L0_ffn_b_in': _L0_ffn_in['b_in'], 'L0_ffn_W_out': _L0_ffn_in['W_out'], 'L0_ffn_b_out': _L0_ffn_in['b_out']}

def reference(x, ctx_1024, L0_xattn_Wq, L0_xattn_bq, L0_xattn_Wk, L0_xattn_bk, L0_xattn_Wv, L0_xattn_bv, L0_xattn_Wo, L0_xattn_bo, L0_ffn_W_in, L0_ffn_b_in, L0_ffn_W_out, L0_ffn_b_out):
    import jax
    import jax.numpy as jnp

    def _L0_xattn_ref(q, k, v, Wq, bq, Wk, bk, Wv, bv, Wo, bo, use_causal_mask):
        import jax, jax.numpy as jnp
        import numpy as np
        EMBED_DIM = 512
        NUM_HEADS = 16
        PROJ_DIM = EMBED_DIM // NUM_HEADS

        def _split_heads(x, B):
            return x.reshape(B, -1, NUM_HEADS, PROJ_DIM).transpose(0, 2, 1, 3)
        B, S, D = q.shape
        qh = _split_heads(q @ Wq + bq, B)
        kh = _split_heads(k @ Wk + bk, B)
        vh = _split_heads(v @ Wv + bv, B)
        logits = jnp.einsum('bhqd,bhkd->bhqk', qh, kh) / jnp.sqrt(jnp.asarray(PROJ_DIM, jnp.float32))
        if use_causal_mask:
            tril = jnp.tril(jnp.ones((S, S), dtype=logits.dtype))
            logits = logits + jnp.log(tril * 1e-09 + 1e-09)
        attn = jax.nn.softmax(logits, axis=-1)
        out = jnp.einsum('bhqk,bhkd->bhqd', attn, vh)
        out = out.transpose(0, 2, 1, 3).reshape(B, S, D)
        return out @ Wo + bo

    def _L0_ffn_ref(x, W_in, b_in, W_out, b_out):
        import jax, jax.numpy as jnp
        import numpy as np

        def _ste(w, w_q):
            return w + jax.lax.stop_gradient(w_q - w)

        def quantize_w8_per(w, axis):
            amax = jnp.clip(jnp.max(jnp.abs(w), axis=axis, keepdims=True), 1e-08, None)
            scale = 127.0 / amax
            w_q = jnp.clip(jnp.round(w * scale), -128.0, 127.0) / scale
            return _ste(w, w_q)

        def quantize_a16(x):
            amax = jnp.clip(jnp.max(jnp.abs(x)), 1e-08, None)
            scale = 32767.0 / amax
            x_q = jnp.clip(jnp.round(x * scale), -32768.0, 32767.0) / scale
            return _ste(x, x_q)
        W_in_sim = quantize_w8_per(W_in, axis=0)
        W_out_sim = quantize_w8_per(W_out, axis=1)
        x_sim = quantize_a16(x)
        hidden = jax.nn.gelu(x_sim @ W_in_sim + b_in, approximate=False)
        hidden_sim = quantize_a16(hidden)
        out = hidden_sim @ W_out_sim + b_out
        return out
    x = x + _L0_xattn_ref(_layernorm(x, axis=-1), ctx_1024, ctx_1024, L0_xattn_Wq, L0_xattn_bq, L0_xattn_Wk, L0_xattn_bk, L0_xattn_Wv, L0_xattn_bv, L0_xattn_Wo, L0_xattn_bo, 1)
    x = x + _L0_ffn_ref(_layernorm(x, axis=-1), L0_ffn_W_in, L0_ffn_b_in, L0_ffn_W_out, L0_ffn_b_out)
    return x

_drawn_inputs = setup_inputs


def setup_inputs(seed=0):
    import zlib

    import numpy as np

    out = dict(_drawn_inputs(seed))
    spreads = {'L0_xattn_bq': (0.0, 0.432),
     'L0_xattn_bk': (0.0, 0.8),
     'L0_xattn_bv': (0.0, 0.1),
     'L0_xattn_bo': (0.0, 0.1),
     'L0_ffn_b_in': (0.0, 0.1),
     'L0_ffn_b_out': (0.0, 0.1)}
    factors = {}
    for name, (base, spread) in spreads.items():
        noise = np.random.default_rng([zlib.crc32(name.encode()), seed]).standard_normal(out[name].shape)
        drawn = base * np.exp(spread * noise) if base else spread * noise
        out[name] = jnp.asarray(drawn.astype(out[name].dtype))
    for name, factor in factors.items():
        out[name] = (out[name] * factor).astype(out[name].dtype)
    return out
```

```python
import math
from contextlib import ExitStack

import concourse.bass as bass
from concourse import mybir

F32 = mybir.dt.float32
F16 = mybir.dt.float16
I32 = mybir.dt.int32
ALU = mybir.AluOpType
ACT = mybir.ActivationFunctionType
AX = mybir.AxisListType

P = 128
B, S, D, F = 8, 1024, 512, 2048
H, HD = 16, 32
KD = D // P
FT = F // P
KT = S // P
G = H // 4
CH = 512
CT = CH // P
NCH = B * S // CH
EPS = 1e-5
ROUND = 1.5 * 2.0 ** 23
STEP_ROWS = KT
QK_ROWS = 3 * HD + STEP_ROWS


class Space:

    def __init__(self, nc, ctx, tag):
        self.nc, self.ctx, self.tag = nc, ctx, tag

    def sb(self, name, shape, dt=F32):
        return self.ctx.enter_context(self.nc.sbuf_tensor(f"{self.tag}_{name}", shape, dt))

    def ps(self, name, shape):
        return self.ctx.enter_context(self.nc.psum_tensor(f"{self.tag}_{name}", shape, F32))

    def sem(self, name):
        return self.ctx.enter_context(self.nc.semaphore(f"{self.tag}_{name}"))

    def sems(self, name, n):
        return [self.sem(f"{name}{i}") for i in range(n)]


def project(nc, x, ctxT, wq, wk, wv, bq, bk, bv, ident_in, qT_s, kT_s, v_s, qk_max):
    with ExitStack() as ctx:
        m = Space(nc, ctx, "p1")
        w_q, w_k, w_v = (m.sb(n, [P, KD, D]) for n in ("wq", "wk", "wv"))
        ident = m.sb("ident", [P, P])
        bias_q, bias_k, bias_v = m.sb("bq", [P, G]), m.sb("bk", [P, G]), m.sb("bv", [P, D])
        xn = [m.sb(f"x{c}", [P, CT, D]) for c in range(2)]
        cT = [m.sb(f"cT{c}", [P, KD, CH]) for c in range(2)]
        xT = [m.sb(f"xT{c}", [P, KD, CH]) for c in range(2)]
        qo, ko = ([m.sb(f"{n}{c}", [P, G, CH]) for c in range(2)] for n in ("qo", "ko"))
        vo = [m.sb(f"vo{c}", [P, CT, D]) for c in range(2)]
        stats, mv = m.sb("stats", [P, CT, 6]), m.sb("mv", [P, CT, 2])
        std, rstd = m.sb("std", [P, CT]), m.sb("rstd", [P, CT])
        eps = m.sb("eps", [P, 1])
        part = m.sb("part", [P, 2])
        tr = m.ps("tr", [P, 2, CH])
        acc = m.ps("acc", [P, 4, CH])
        acc_v = m.ps("acc_v", [P, 2, CH])

        s_w = m.sem("weights_in")
        s_x, s_c = m.sems("x_in", 2), m.sems("ctx_in", 2)
        s_st, s_var, s_std, s_rstd, s_xn = (m.sem(n) for n in ("stats", "var", "std", "rstd", "xn"))
        s_eps, s_part = m.sem("eps"), m.sem("part")
        s_tr = m.sem("transposed")
        s_accv = m.sem("v_product")
        s_acc = m.sem("qk_product")
        s_max = m.sem("max")
        s_xt = m.sem("xT_evacuated")
        s_out = m.sem("qk_evacuated")
        s_vout = m.sem("v_evacuated")
        s_ks, s_vs, s_qs = (m.sems(n, 2) for n in ("k_stored", "v_stored", "q_stored"))
        block = ctx.enter_context(nc.Block())

        @block.sync
        def _(sync):
            for dst, src in ((w_k, wk), (w_v, wv), (w_q, wq)):
                sync.dma_start(dst[:, :, :], src.rearrange("(k p) n -> p k n", p=P)).then_inc(s_w, 16)
            for dst, src in ((ident, ident_in), (bias_q, bq), (bias_k, bk), (bias_v, bv)):
                sync.dma_start(dst[:, :], src).then_inc(s_w, 16)
            with sync.Fori(0, B) as b:
                for c in range(2):
                    n = b * 2 + c
                    sync.wait_ge(s_accv, n * CT + CT)
                    sync.dma_start(cT[c][:, :, :], ctxT.rearrange("(k p) t -> p k t", p=P)[:, :, bass.ds(n * CH, CH)]).then_inc(s_c[c], 16)
                    sync.wait_ge(s_tr, n * KD + KD)
                    sync.dma_start(xn[c][:, :, :], x[bass.ds(n * CH, CH), :].rearrange("(t p) d -> p t d", p=P)).then_inc(s_x[c], 16)

        @block.vector
        def _(dve):
            dve.sem_inc(s_vout, 2)
            dve.sem_inc(s_max, 8)
            dve.memset(eps[:, :], EPS).then_inc(s_eps, 1)
            dve.memset(qk_max[:, :], 0.0).then_inc(s_max, 1)
            dve.wait_ge(s_w, 7 * 16)
            with dve.Fori(0, B) as b:
                for c in range(2):
                    n = b * 2 + c
                    dve.wait_ge(s_x[c], b * 16 + 16)
                    for t in range(CT):
                        dve.bn_stats(stats[:, t, :], xn[c][:, t, :]).then_inc(s_st, 1)
                    dve.wait_ge(s_st, n * CT + CT)
                    dve.sem_inc(s_part, 1)
                    for t in range(CT):
                        dve.bn_aggr(mv[:, t, :], stats[:, t, :]).then_inc(s_var, 1)
                    dve.wait_ge(s_std, n + 1)
                    dve.reciprocal(rstd[:, :], std[:, :]).then_inc(s_rstd, 1)
                    dve.wait_ge(s_rstd, n + 1)
                    for t in range(CT):
                        dve.tensor_scalar(xn[c][:, t, :], xn[c][:, t, :], mv[:, t, 0:1], rstd[:, t:t + 1],
                                          ALU.subtract, ALU.mult).then_inc(s_xn, 1)
                    dve.wait_ge(s_vs[c], b * 16 + 16)
                    for t in range(CT):
                        dve.wait_ge(s_accv, n * CT + 2 * CT + t + 1)
                        dve.tensor_tensor(vo[c][:, t, :], acc_v[:, t % 2, :], bias_v[:, :], ALU.add).then_inc(s_vout, 1)
                    for o, buf in enumerate((ko, qo)):
                        dve.wait_ge(s_out, n * 2 * G + (o + 1) * G + 4)
                        dve.wait_ge(s_max, n * 4 + 2 * o + 9)
                        dve.tensor_reduce(part[:, o:o + 1], buf[c][:, :, :], axis=AX.XY, op=ALU.max,
                                          apply_absolute_value=True).then_inc(s_max, 1)
                        dve.wait_ge(s_max, n * 4 + 2 * o + 10)
                        dve.tensor_tensor(qk_max[:, o:o + 1], qk_max[:, o:o + 1], part[:, o:o + 1],
                                          ALU.max).then_inc(s_max, 1)

        @block.scalar
        def _(act):
            act.sem_inc(s_xt, 2)
            act.sem_inc(s_out, 4)
            for s_stored in (*s_ks, *s_vs, *s_qs):
                act.sem_inc(s_stored, 16)
            act.wait_ge(s_w, 7 * 16)
            act.wait_ge(s_eps, 1)
            with act.Fori(0, B) as b:
                for c in range(2):
                    n = b * 2 + c
                    act.wait_ge(s_var, n * CT + CT)
                    act.activation(std[:, :], mv[:, :, 1], ACT.Sqrt, bias=eps[:, 0:1]).then_inc(s_std, 1)

                    def evacuate(buf, bias, s_stored, first):
                        act.wait_ge(s_stored[c], b * 16 + 16)
                        act.wait_ge(s_max, n * 4 + 3 + 2 * (first // G))
                        for g in range(G):
                            act.wait_ge(s_acc, n * 2 * G + 4 * G + first + g + 1)
                            act.activation(buf[c][:, g, :], acc[:, g, :], ACT.Identity,
                                           bias=bias[:, g:g + 1]).then_inc(s_out, 1)

                    def store(dst, buf, s_evacuated, count, s_stored):
                        act.wait_ge(s_evacuated, count)
                        act.dma_start(dst, buf[c][:, :, :]).then_inc(s_stored[c], 16)

                    evacuate(ko, bias_k, s_ks, 0)
                    act.wait_ge(s_acc, n * 2 * G + 2 * G)
                    for k in range(KD):
                        act.wait_ge(s_tr, n * KD + 2 * KD + k + 1)
                        act.activation(xT[c][:, k, :], tr[:, k % 2, :], ACT.Copy).then_inc(s_xt, 1)
                    store(kT_s[bass.ds(b * P, P), :, c * CH:(c + 1) * CH], ko, s_out, n * 2 * G + G + 4, s_ks)
                    evacuate(qo, bias_q, s_qs, G)
                    store(v_s[bass.ds(b * P, P), c * CT:(c + 1) * CT, :], vo, s_vout, n * CT + CT + 2, s_vs)
                    store(qT_s[bass.ds(b * P, P), :, c * CH:(c + 1) * CH], qo, s_out, n * 2 * G + 2 * G + 4, s_qs)
            for c in range(2):
                for s_stored in (s_ks[c], s_vs[c], s_qs[c]):
                    act.wait_ge(s_stored, (B + 1) * 16)

        @block.tensor
        def _(pe):
            pe.sem_inc(s_tr, 2 * KD)
            pe.sem_inc(s_accv, 2 * CT)
            pe.sem_inc(s_acc, 4 * G)
            pe.wait_ge(s_w, 7 * 16)
            with pe.Fori(0, B) as b:
                for c in range(2):
                    n = b * 2 + c

                    def product(bank, lhs, rhs):
                        for k in range(KD):
                            last = pe.matmul(bank, lhs(k), rhs(k), start=(k == 0), stop=(k == KD - 1))
                        return last

                    pe.wait_ge(s_c[c], b * 16 + 16)
                    for g in range(G):
                        pe.wait_ge(s_out, n * 2 * G + g + 1)
                        product(acc[:, g, :], lambda k: w_k[:, k, g * P:(g + 1) * P], lambda k: cT[c][:, k, :]).then_inc(s_acc, 1)
                    pe.wait_ge(s_xn, n * CT + CT)
                    for k in range(KD):
                        pe.wait_ge(s_xt, n * KD + k + 1)
                        for t in range(CT):
                            last = pe.transpose(tr[:, k % 2, t * P:(t + 1) * P], xn[c][:, t, k * P:(k + 1) * P], ident[:, :])
                        last.then_inc(s_tr, 1)
                    for t in range(CT):
                        pe.wait_ge(s_vout, n * CT + t + 1)
                        product(acc_v[:, t % 2, :], lambda k: cT[c][:, k, t * P:(t + 1) * P], lambda k: w_v[:, k, :]).then_inc(s_accv, 1)
                    pe.wait_ge(s_xt, n * KD + KD + 2)
                    for g in range(G):
                        pe.wait_ge(s_out, n * 2 * G + G + g + 1)
                        product(acc[:, g, :], lambda k: w_q[:, k, g * P:(g + 1) * P], lambda k: xT[c][:, k, :]).then_inc(s_acc, 1)


def attend(nc, qT_s, kT_s, v_s, qk_max, ident_in, diag_in, tri_in, step_q, step_k, oT_s):
    with ExitStack() as ctx:
        m = Space(nc, ctx, "p2")
        NU = 2 * KT
        TURNS = B * G // 2
        ident, diag16, tri = m.sb("ident", [P, P]), m.sb("diag16", [P, P], F16), m.sb("tri", [P, P], F16)
        qs, ks = ([m.sb(f"{n}{p}", [QK_ROWS, 4, S], F16) for p in range(2)] for n in ("qs", "ks"))
        raw = [m.sb(f"raw{o}", [P, S]) for o in range(2)]
        scaled = m.sb("scaled", [P, S])
        hi, lo = ([m.sb(f"{n}{o}", [P, S], F16) for o in range(2)] for n in ("hi", "lo"))
        v = [m.sb(f"v{p}", [P, KT, P]) for p in range(2)]
        prob = m.sb("prob", [P, 2, 4, S])
        probT = m.sb("probT", [P, 2, 4, KT, P])
        oT = m.sb("oT", [P, 2, S])
        negmax, rsum, rinv = m.sb("negmax", [P, 2, 4]), m.sb("rsum", [P, 2, 4]), m.sb("rinv", [P, 2, 4, HD])
        recip = m.sb("recip", [P, 4])
        rows = m.sb("rows", [P, 2, P])
        sc, ones = m.sb("sc", [P, 16]), m.sb("ones", [2, P])
        top = m.sb("top", [2, 3])
        scores = m.ps("scores", [P, 2, 2, 512])
        tr = m.ps("tr", [P, 3, 512])
        acc = m.ps("acc", [P, 512])

        s_const, s_fill = m.sem("constants_in"), m.sem("step_rows_in")
        s_chain, s_pe0, s_scale = m.sem("chain"), m.sem("scale_products"), m.sem("scales")
        s_in, s_split = m.sem("qk_in"), m.sem("qk_split")
        s_qk = m.sems("qk_parts_in", 2)
        s_v = m.sems("v_in", 2)
        s_sc, s_max, s_exp = m.sem("scores"), m.sem("row_max"), m.sem("exp")
        s_tr, s_pv, s_zero, s_rec = m.sem("transposed"), m.sem("pv"), m.sem("zeroed"), m.sem("reciprocal")
        s_mark = m.sem("mark")
        s_ea = m.sem("evacuated_act")
        s_ed = m.sem("evacuated_dve")
        s_o = m.sems("oT_stored", 2)
        s_out = m.sem("oT_written")
        s_rinv = m.sem("rinv")
        block = ctx.enter_context(nc.Block())

        BY_ACT = (True, False, True, False, True, False, True, True, False)
        N_ACT, N_DVE = BY_ACT.count(True), BY_ACT.count(False)

        def evacuated(eng, unit, e):
            unit, e = (unit - 1, e + 9) if e < 0 else (unit, e)
            sem, n = (s_ea, N_ACT) if BY_ACT[e] else (s_ed, N_DVE)
            eng.wait_ge(sem, unit * n + (n + BY_ACT[:e + 1].count(BY_ACT[e])))

        def wait_apart(eng, sem, count):
            eng.wait_ge(sem, count)
            eng.sem_inc(s_mark, 1)

        @block.sync
        def _(sync):
            for dst, src in ((ident, ident_in), (diag16, diag_in), (tri, tri_in)):
                sync.dma_start(dst[:, :], src).then_inc(s_const, 16)
            for dst, src in (*((q, step_q) for q in qs), *((k, step_k) for k in ks)):
                sync.dma_start(dst[3 * HD:QK_ROWS, :, :], src).then_inc(s_fill, 16)

            def load_raw(b, g, count):
                wait_apart(sync, s_split, count)
                for buf, src in zip(raw, (kT_s, qT_s)):
                    sync.dma_start(buf[:, :].unsqueeze(1), src[bass.ds(b * P, P), bass.ds(g, 1), :]).then_inc(s_in, 16)

            def load_parts(par, count):
                wait_apart(sync, s_split, count)
                for o, (dst, parts) in enumerate(((ks[par], (hi, lo, hi)), (qs[par], (hi, hi, lo)))):
                    for r, part in enumerate(parts):
                        for j in range(4):
                            sync.dma_start(dst[r * HD:(r + 1) * HD, j, :],
                                           part[o][j * HD:(j + 1) * HD, :]).then_inc(s_qk[par], 16)

            def load_v(par, b, g):
                sync.dma_start(v[par][:, :, :], v_s[bass.ds(b * P, P), :, bass.ds(g * P, P)]).then_inc(s_v[par], 16)

            for par in range(2):
                load_raw(0, par, 6 * par + 6)
                load_parts(par, 6 * par + 12)
                load_v(par, 0, par)
            with sync.Fori(0, TURNS) as i:
                nxt = (i + 1) % TURNS
                for par in range(2):
                    b, g = nxt // 2, (nxt % 2) * 2 + par
                    load_raw(b, g, i * 12 + (6 * par + 18))
                    wait_apart(sync, s_sc, i * (4 * NU) + 4 * KT * (par + 1))
                    load_parts(par, i * 12 + (6 * par + 24))
                    wait_apart(sync, s_out, i * NU + (KT * (par + 1) + 2))
                    sync.dma_start(oT_s[bass.ds(i // 2 * P, P), bass.ds((i % 2) * 2 + par, 1), :], oT[:, par:par + 1, :]).then_inc(s_o[par], 16)
                    load_v(par, b, g)
            for par in range(2):
                sync.wait_ge(s_o[par], TURNS * 16 + 16)
                sync.wait_ge(s_v[par], TURNS * 16 + 16)
                sync.wait_ge(s_qk[par], (TURNS + 1) * 24 * 16)

        @block.gpsimd
        def _(pool):
            pool.sem_inc(s_split, 6)
            pool.memset(ones[:, :], 1.0).then_inc(s_scale, 1)
            pool.memset(probT[:, 1, :, :, :], 0.0).then_inc(s_zero, 1)
            pool.memset(rows[:, 1, :], 0.0).then_inc(s_zero, 1)
            pool.wait_ge(s_scale, 2)

            def split(n, wait_parts):
                wait_apart(pool, s_in, n * 32 + 32)
                for o in range(2):
                    step = n * 6 + 3 * o + 6
                    wait_apart(pool, s_split, step)
                    pool.tensor_scalar(scaled[:, :], raw[o][:, :], sc[:, 8 + o:9 + o], None, ALU.mult).then_inc(s_split, 1)
                    wait_apart(pool, s_split, step + 1)
                    if o == 0:
                        wait_parts()
                    pool.tensor_copy(hi[o][:, :], scaled[:, :]).then_inc(s_split, 1)
                    wait_apart(pool, s_split, step + 2)
                    pool.tensor_tensor(lo[o][:, :], scaled[:, :], hi[o][:, :], ALU.subtract).then_inc(s_split, 1)

            split(0, lambda: None)
            split(1, lambda: pool.wait_ge(s_qk[0], 24 * 16))
            with pool.Fori(0, TURNS) as i:
                for par in range(2):
                    def taken():
                        wait_apart(pool, s_qk[1 - par], i * (24 * 16) + (1 + par) * 24 * 16)
                    split(i * 2 + (2 + par), taken)

        @block.vector
        def _(dve):
            dve.sem_inc(s_ed, N_DVE)
            dve.sem_inc(s_out, 1)
            dve.sem_inc(s_rinv, 1)
            steps = [0]

            def link(ins):
                steps[0] += 1
                ins.then_inc(s_chain, 1)
                dve.wait_ge(s_chain, steps[0])

            dve.wait_ge(s_pe0, 1)
            link(dve.tensor_reduce(top[:, 0:1], acc[0:2, 0:P], axis=AX.X, op=ALU.max))
            link(dve.tensor_scalar(top[:, 1:3], ident[0:2, 0:2], top[:, 0:1], None, ALU.mult))
            dve.wait_ge(s_pe0, 2)
            link(dve.tensor_scalar(sc[:, 0:2], acc[:, P:P + 2], 1e-18, 1e18, ALU.max, ALU.min))
            link(dve.reciprocal(sc[:, 2:3], sc[:, 1:2]))
            link(dve.tensor_scalar(sc[:, 3:4], sc[:, 0:1], sc[:, 2:3], math.sqrt(HD), ALU.mult, ALU.mult))
            bits = sc[:, :].bitcast(I32)
            link(dve.tensor_scalar(bits[:, 4:5], bits[:, 3:4], 24, 23, ALU.logical_shift_right, ALU.logical_shift_left))
            link(dve.tensor_scalar(bits[:, 5:6], bits[:, 4:5], 64 << 23, None, ALU.add))
            link(dve.tensor_scalar(bits[:, 8:9], bits[:, 5:6], -1, 254 << 23, ALU.mult, ALU.add))
            dve.tensor_scalar(sc[:, 9:10], sc[:, 5:6], 1 / math.sqrt(HD), None, ALU.mult).then_inc(s_scale, 1)

            def row_max(unit, j, upar):
                n = unit * 4 + j
                dve.wait_ge(s_sc, n + 1)
                dve.tensor_reduce(negmax[:, upar, j:j + 1], scores[:, (4 * upar + j) % 2, :, :], axis=AX.XY, op=ALU.max,
                                  negate=True).then_inc(s_max, 1)

            def evacuate(unit, t, j):
                for e in (2 * j, 2 * j + 1):
                    if not BY_ACT[e]:
                        dve.wait_ge(s_tr, unit * 9 + e + 1)
                        dve.tensor_copy(probT[:, t % 2, j, 4 * (e % 2):4 * (e % 2) + 4, :], tr[:, (9 * t + e) % 3, :]).then_inc(s_ed, 1)

            def write_out(unit, t):
                par, qt = t // KT % 2, t % KT
                dve.wait_ge(s_ed, unit * N_DVE + 2 * N_DVE)
                dve.wait_ge(s_pv, unit + 2)
                dve.tensor_tensor(oT[:, par, qt * P:(qt + 1) * P], acc[:, 0:P], rows[:, t % 2, :], ALU.mult).then_inc(s_out, 1)

            for j in range(4):
                row_max(0, j, 0)
            dve.wait_ge(s_zero, 2)
            with dve.Fori(0, TURNS) as i:
                for t in range(NU):
                    unit = i * NU + t
                    for j in range(4):
                        row_max(unit + 1, j, (t + 1) % 2)
                        if j == 0:
                            dve.wait_ge(s_exp, unit * 4 + 4)
                            dve.reciprocal(recip[:, :], rsum[:, t % 2, :]).then_inc(s_rec, 1)
                            dve.wait_ge(s_rec, unit + 1)
                            dve.tensor_copy(rinv[:, t % 2, :, :], recip[:, :].unsqueeze(2).broadcast_to([P, 4, HD])).then_inc(s_rinv, 1)
                        evacuate(unit, t, j)
                    if t in (1, KT + 1):
                        dve.wait_ge(s_o[t // KT], i * 16 + 16)
                    write_out(unit - 1, t - 1)
                    dve.wait_ge(s_tr, unit * 9 + 9)
                    dve.tensor_copy(rows[:, t % 2, :], tr[:, (9 * t + 8) % 3, 0:P]).then_inc(s_ed, 1)
            write_out(TURNS * NU - 1, NU - 1)

        @block.scalar
        def _(act):
            act.sem_inc(s_ea, N_ACT)
            for par in range(2):
                act.sem_inc(s_o[par], 16)

            def softmax(unit, j, upar):
                n = unit * 4 + j
                act.wait_ge(s_max, n + 1)
                act.activation(prob[:, upar, j, :], scores[:, (4 * upar + j) % 2, :, :], ACT.Exp, bias=negmax[:, upar, j:j + 1],
                               accum_out=rsum[:, upar, j:j + 1]).then_inc(s_exp, 1)

            for j in range(4):
                softmax(0, j, 0)
            with act.Fori(0, TURNS) as i:
                for t in range(NU):
                    unit = i * NU + t
                    act.wait_ge(s_rinv, unit + 1)
                    for j in range(4):
                        for e in (2 * j, 2 * j + 1):
                            if BY_ACT[e]:
                                act.wait_ge(s_tr, unit * 9 + e + 1)
                                act.activation(probT[:, t % 2, j, 4 * (e % 2):4 * (e % 2) + 4, :], tr[:, (9 * t + e) % 3, :],
                                               ACT.Copy).then_inc(s_ea, 1)
                            if e % 2 == 0:
                                softmax(unit + 1, j, (t + 1) % 2)

        @block.tensor
        def _(pe):
            pe.wait_ge(s_const, 3 * 16)
            pe.transpose(acc[0:2, 0:P], qk_max[:, :], ident[:, :]).then_inc(s_pe0, 1)
            pe.wait_ge(s_chain, 2)
            pe.wait_ge(s_scale, 1)
            pe.matmul(acc[:, P:P + 2], ones[:, :], top[:, 1:3], start=True, stop=True).then_inc(s_pe0, 1)
            pe.wait_ge(s_fill, 4 * 16)

            def make_scores(unit, j, t, first):
                par, qt, buf = t // KT % 2, t % KT, (4 * t + j) % 2
                if not first:
                    pe.wait_ge(s_exp, unit * 4 + j - 1)
                q = qs[par][:, j, qt * P:(qt + 1) * P]
                for half in range(2):
                    bank = scores[:, buf, half, :]
                    diagonal = half == qt // 4
                    last = pe.matmul(bank, q, ks[par][:, j, half * 512:(half + 1) * 512], start=True, stop=not diagonal)
                    if diagonal:
                        last = pe.matmul(bank[:, (qt % 4) * P:(qt % 4 + 1) * P], tri[:, :], diag16[:, :], start=False, stop=True)
                last.then_inc(s_sc, 1)

            def transpose_tile(unit, t, e):
                evacuated(pe, unit, e - 3)
                for k in range(4):
                    kt = 4 * (e % 2) + k
                    last = pe.transpose(tr[:, (9 * t + e) % 3, k * P:(k + 1) * P],
                                        prob[:, t % 2, e // 2, kt * P:(kt + 1) * P], ident[:, :])
                last.then_inc(s_tr, 1)

            def pv(unit, t, kts):
                if 0 in kts:
                    pe.wait_ge(s_out, unit + 2)
                    for e in (5, 7):
                        evacuated(pe, unit, e)
                    if t in (0, KT):
                        pe.wait_ge(s_v[t // KT], i * 16 + 16)
                for kt in kts:
                    for j in range(4):
                        last = pe.matmul(acc[j * HD:(j + 1) * HD, 0:P], v[t // KT % 2][:, kt, j * HD:(j + 1) * HD],
                                         probT[:, t % 2, j, kt, :], start=(kt == 0), stop=(kt == KT - 1))
                if KT - 1 in kts:
                    last.then_inc(s_pv, 1)

            pe.wait_ge(s_qk[0], 24 * 16)
            pe.wait_ge(s_chain, 3)
            for j in range(4):
                make_scores(0, j, 0, j < 2)
            make_scores(1, 0, 1, False)
            pe.wait_ge(s_v[1], 16)
            pe.wait_ge(s_zero, 2)
            with pe.Fori(0, TURNS) as i:
                for t in range(NU):
                    unit = i * NU + t
                    for j in range(4):
                        pe.wait_ge(s_exp, unit * 4 + j + 1)
                        transpose_tile(unit, t, 2 * j)
                        if j > 0:
                            pv(unit - 1, t - 1, (2 * j,))
                        transpose_tile(unit, t, 2 * j + 1)
                        if j < 3:
                            make_scores(unit + 1, j + 1, t + 1, False)
                        else:
                            if t == KT - 2:
                                pe.wait_ge(s_qk[1], i * (24 * 16) + 24 * 16)
                            if t == NU - 2:
                                pe.wait_ge(s_qk[0], i * (24 * 16) + 48 * 16)
                            make_scores(unit + 2, 0, t + 2, False)
                        pv(unit - 1, t - 1, (0, 1) if j == 0 else (2 * j + 1,))
                    pe.wait_ge(s_rinv, unit + 2)
                    evacuated(pe, unit, 5)
                    pe.matmul(tr[:, (9 * t + 8) % 3, 0:P], rinv[:, t % 2, :, :], ident[:, :], start=True, stop=True).then_inc(s_tr, 1)
            pv(TURNS * NU - 1, NU - 1, range(KT))


def spread_max(nc, m, eng, stage, src, n, tile, bank, ident, ones, sem_pe, sem_dve):
    top, diag = tile[0:n, 0:1], tile[0:n, 1:1 + n]
    if stage == "pe":
        eng.transpose(bank[0:n, 0:P], src, ident[:, :]).then_inc(sem_pe, 1)
        eng.wait_ge(sem_dve, 2)
        eng.matmul(bank[:, P:P + n], ones[0:n, :], diag, start=True, stop=True).then_inc(sem_pe, 1)
    else:
        eng.wait_ge(sem_pe, 1)
        eng.tensor_reduce(top, bank[0:n, 0:P], axis=AX.X, op=ALU.max).then_inc(sem_dve, 1)
        eng.wait_ge(sem_dve, 1)
        eng.tensor_scalar(diag, ident[0:n, 0:n], top, None, ALU.mult).then_inc(sem_dve, 1)
        eng.wait_ge(sem_pe, 2)


def merge(nc, x, wo, bo, ident_in, oT_s, x1_s, xnT_s, xn_max):
    with ExitStack() as ctx:
        m = Space(nc, ctx, "p3")
        NT = 2 * CT
        w_o, ident, bias = m.sb("wo", [P, KD, D]), m.sb("ident", [P, P]), m.sb("bo", [P, D])
        oT = [m.sb(f"oT{c}", [P, G, CH]) for c in range(2)]
        xs = m.sb("x", [P, NT, D])
        xn = m.sb("xn", [P, NT, D])
        xT = m.sb("xT", [P, 2, KD, CH])
        stats, mv = m.sb("stats", [P, NT, 6]), m.sb("mv", [P, NT, 2])
        std, rstd, eps = m.sb("std", [P, NT]), m.sb("rstd", [P, NT]), m.sb("eps", [P, 1])
        high = m.sb("high", [P, NT + 1])
        acc, tr = m.ps("acc", [P, 4, D]), m.ps("tr", [P, 2, CH])

        s_w, s_x, s_oT = m.sem("weights_in"), m.sems("x_in", 2), m.sems("oT_in", 2)
        s_eps, s_var, s_std, s_rstd = m.sem("eps"), m.sem("var"), m.sem("std"), m.sem("rstd")
        s_st, s_high, s_mark = m.sem("stats"), m.sem("high"), m.sem("mark")
        s_xb = m.sem("bias_added")
        s_acc = m.sem("product")
        s_sum = m.sem("sum")
        s_tr = m.sem("transposed")
        s_xn = m.sem("xn")
        s_xt = m.sem("xT_evacuated")
        s_xs, s_xts = m.sems("x1_stored", 2), m.sems("xT_stored", 2)
        block = ctx.enter_context(nc.Block())

        @block.sync
        def _(sync):
            sync.dma_start(w_o[:, :, :], wo.rearrange("(k p) n -> p k n", p=P)).then_inc(s_w, 16)
            for dst, src in ((ident, ident_in), (bias, bo)):
                sync.dma_start(dst[:, :], src).then_inc(s_w, 16)
            with sync.Fori(0, B) as b:
                for c in range(2):
                    sync.wait_ge(s_acc, b * NT + CT * (c + 1))
                    sync.sem_inc(s_mark, 1)
                    sync.dma_start(oT[c][:, :, :], oT_s[bass.ds(b * P, P), :, c * CH:(c + 1) * CH]).then_inc(s_oT[c], 16)
                    sync.wait_ge(s_xs[c], b * 16 + 16)
                    sync.sem_inc(s_mark, 1)
                    sync.dma_start(xs[:, c * CT:(c + 1) * CT, :], x[bass.ds(b * S + c * CH, CH), :].rearrange("(t p) d -> p t d", p=P)).then_inc(s_x[c], 16)

        @block.gpsimd
        def _(pool):
            pool.wait_ge(s_w, 3 * 16)
            with pool.Fori(0, B) as b:
                for t in range(NT):
                    if t % CT == 0:
                        pool.wait_ge(s_x[t // CT], b * 16 + 16)
                    pool.tensor_tensor(xs[:, t, :], xs[:, t, :], bias[:, :], ALU.add).then_inc(s_xb, 1)

        @block.vector
        def _(dve):
            dve.memset(eps[:, :], EPS).then_inc(s_eps, 1)
            dve.memset(high[:, :], 0.0).then_inc(s_high, 1)
            dve.sem_inc(s_sum, 4)
            dve.sem_inc(s_xn, NT)
            with dve.Fori(0, B) as b:
                for t in range(NT):
                    n = b * NT + t
                    dve.wait_ge(s_xb, n + 1)
                    dve.wait_ge(s_acc, n + NT + 1)
                    dve.tensor_tensor(xs[:, t, :], acc[:, t % 4, :], xs[:, t, :], ALU.add).then_inc(s_sum, 1)
                    dve.wait_ge(s_sum, n + 5)
                    dve.bn_stats(stats[:, t, :], xs[:, t, :]).then_inc(s_st, 1)
                    dve.wait_ge(s_st, n + 1)
                    dve.sem_inc(s_mark, 1)
                    dve.bn_aggr(mv[:, t, :], stats[:, t, :]).then_inc(s_var, 1)
                    dve.wait_ge(s_std, n + 1)
                    dve.reciprocal(rstd[:, t:t + 1], std[:, t:t + 1]).then_inc(s_rstd, 1)
                    dve.wait_ge(s_rstd, n + 1)
                    dve.wait_ge(s_tr, n + 1)
                    dve.tensor_scalar(xn[:, t, :], xs[:, t, :], mv[:, t, 0:1], rstd[:, t:t + 1], ALU.subtract, ALU.mult).then_inc(s_xn, 1)
                    dve.wait_ge(s_xn, n + NT + 1)
                    if t == 0:
                        dve.wait_ge(s_high, b * (NT + 1) + 1)
                    dve.tensor_reduce(high[:, t:t + 1], xn[:, t, :], axis=AX.X, op=ALU.max, apply_absolute_value=True).then_inc(s_high, 1)
                dve.wait_ge(s_high, b * (NT + 1) + (NT + 1))
                dve.tensor_reduce(high[:, NT:NT + 1], high[:, :], axis=AX.X, op=ALU.max).then_inc(s_high, 1)
            dve.wait_ge(s_high, B * (NT + 1) + 1)
            dve.tensor_copy(xn_max[:, :], high[:, NT:NT + 1]).then_inc(s_high, 1)

        @block.scalar
        def _(act):
            act.sem_inc(s_xt, 2)
            for s_stored in (*s_xs, *s_xts):
                act.sem_inc(s_stored, 16)
            act.wait_ge(s_eps, 1)

            def square_root(b, t):
                act.wait_ge(s_var, b * NT + t + 1)
                act.activation(std[:, t:t + 1], mv[:, t, 1:2], ACT.Sqrt, bias=eps[:, 0:1]).then_inc(s_std, 1)

            with act.Fori(0, B) as b:
                square_root(b, 0)
                for t in range(NT):
                    c = t // CT
                    if t + 1 < NT:
                        square_root(b, t + 1)
                    if t % CT == 0:
                        act.wait_ge(s_xts[c], b * 16 + 16)
                    act.wait_ge(s_tr, b * NT + NT + t + 1)
                    act.activation(xT[:, c, :, (t % CT) * P:(t % CT + 1) * P], tr[:, t % 2, :], ACT.Copy).then_inc(s_xt, 1)
                    if t % CT == CT - 1:
                        act.wait_ge(s_xn, b * NT + NT + t + 1)
                        act.dma_start(x1_s[bass.ds((b * 2 + c) * P, P), :, :], xs[:, c * CT:(c + 1) * CT, :]).then_inc(s_xs[c], 16)
                        act.wait_ge(s_xt, b * NT + t + 3)
                        act.dma_start(xnT_s[bass.ds((b * 2 + c) * P, P), :, :], xT[:, c, :, :]).then_inc(s_xts[c], 16)
            for s_stored in (*s_xs, *s_xts):
                act.wait_ge(s_stored, B * 16 + 16)

        @block.tensor
        def _(pe):
            pe.sem_inc(s_acc, NT)
            pe.sem_inc(s_tr, NT)
            pe.wait_ge(s_w, 3 * 16)

            def transposes(b, t):
                pe.wait_ge(s_xn, b * NT + NT + t + 1)
                pe.wait_ge(s_xt, b * NT + t + 1)
                for k in range(KD):
                    last = pe.transpose(tr[:, t % 2, k * P:(k + 1) * P], xn[:, t, k * P:(k + 1) * P], ident[:, :])
                last.then_inc(s_tr, 1)

            with pe.Fori(0, B) as b:
                for t in range(NT):
                    if t % CT == 0:
                        pe.wait_ge(s_oT[t // CT], b * 16 + 16)
                    pe.wait_ge(s_sum, b * NT + t + 1)
                    for k in range(KD):
                        last = pe.matmul(acc[:, t % 4, :], oT[t // CT][:, k, (t % CT) * P:(t % CT + 1) * P], w_o[:, k, :],
                                         start=(k == 0), stop=(k == KD - 1))
                    last.then_inc(s_acc, 1)
                    if t > 0:
                        transposes(b, t - 1)
                transposes(b, NT - 1)


def expand(nc, w_inT, b_in, ident_in, ident16_in, xnT_s, xn_max, h_s, h_max):
    with ExitStack() as ctx:
        m = Space(nc, ctx, "p4")
        HP = 4
        NP = 2 * FT // HP
        w = m.sb("w", [P, FT, D])
        w16 = m.sb("w16", [P, FT, D], F16)
        wq = m.sb("wq", [P, KD, F], F16)
        ident, ident16, bias = m.sb("ident", [P, P]), m.sb("ident16", [P, P], F16), m.sb("b_in", [P, FT])
        high_w, scale_w, alpha = m.sb("high_w", [P, FT]), m.sb("scale_w", [P, FT]), m.sb("alpha", [P, FT])
        scale_x, tops, ones = m.sb("scale_x", [P, 3]), m.sb("tops", [1, 2]), m.sb("ones", [1, P])
        raw = m.sb("raw", [P, 2, KD, CH])
        hi, lo = (m.sb(n, [P, 2, KD, CH], F16) for n in ("hi", "lo"))
        g = m.sb("g", [P, 4, HP, CH])
        high = m.sb("high", [P, NP + 1])
        acc = m.ps("acc", [P, 8, CH])

        s_w, s_chain, s_pe0, s_top = m.sem("weights_in"), m.sem("chain"), m.sem("max_products"), m.sem("max_steps")
        s_w16, s_wt, s_wq, s_mark = m.sem("w_integers"), m.sem("w_transposed"), m.sem("w_evacuated"), m.sem("mark")
        s_x, s_r, s_q, s_hi, s_high, s_scale = m.sems("x_in", 2), m.sem("rounding"), m.sem("x_integers"), m.sem("x_hi"), m.sem("high"), m.sem("scales")
        s_lo = m.sem("x_lo")
        s_acc = m.sem("product")
        s_g = m.sem("gelu")
        s_read = m.sem("g_read")
        s_gs = m.sems("g_stored", 4)
        block = ctx.enter_context(nc.Block())

        @block.sync
        def _(sync):
            sync.dma_start(w[:, :, :], w_inT.rearrange("(f p) d -> p f d", p=P)).then_inc(s_w, 16)
            for dst, src in ((ident, ident_in), (ident16, ident16_in), (bias, b_in)):
                sync.dma_start(dst[:, :], src).then_inc(s_w, 16)

            def load(n, c):
                sync.wait_ge(s_lo, n + 1)
                sync.sem_inc(s_mark, 1)
                sync.dma_start(raw[:, c, :, :], xnT_s[bass.ds(n % NCH * P, P), :, :]).then_inc(s_x[c], 16)

            load(0, 0)
            with sync.Fori(0, NCH // 2) as i:
                load(i * 2 + 1, 1)
                for p in range(NP):
                    if p == 2:
                        load(i * 2 + 2, 0)
                    sync.wait_ge(s_g, i * (2 * FT) + (HP * (p + 1) + 8))
                    sync.sem_inc(s_mark, 1)
                    sync.dma_start(h_s[bass.ds((i * 2 + p // 4) * P, P), (p % 4) * HP:(p % 4 + 1) * HP, :], g[:, p % 4, :, :]).then_inc(s_gs[p % 4], 16)
            for s_stored in s_gs:
                sync.wait_ge(s_stored, NCH * 16 + 16)
            sync.wait_ge(s_x[0], (NCH // 2 + 1) * 16)

        @block.gpsimd
        def _(pool):
            pool.memset(ones[:, :], 1.0).then_inc(s_scale, 1)
            pool.sem_inc(s_lo, 2)

            def second_part(n, c):
                pool.wait_ge(s_acc, n * FT + FT)
                pool.wait_ge(s_hi, n + 1)
                pool.tensor_tensor(lo[:, c, :, :], raw[:, c, :, :], hi[:, c, :, :], ALU.subtract).then_inc(s_lo, 1)

            second_part(0, 0)
            with pool.Fori(0, NCH // 2) as i:
                second_part(i * 2 + 1, 1)
                second_part(i * 2 + 2, 0)

        @block.vector
        def _(dve):
            steps = [0]

            def link(ins):
                steps[0] += 1
                ins.then_inc(s_chain, 1)
                dve.wait_ge(s_chain, steps[0])

            dve.sem_inc(s_read, 4)
            dve.memset(high[:, :], 0.0).then_inc(s_high, 1)
            dve.wait_ge(s_w, 4 * 16)
            dve.tensor_reduce(high_w[:, :], w[:, :, :], axis=AX.X, op=ALU.max, apply_absolute_value=True).then_inc(s_chain, 1)
            steps[0] += 1
            spread_max(nc, m, dve, "dve", xn_max[:, :], 1, tops, acc[:, 0, :], ident, ones, s_pe0, s_top)
            link(dve.tensor_scalar(high_w[:, :], high_w[:, :], 1e-8, None, ALU.max))
            link(dve.reciprocal(scale_w[:, :], high_w[:, :]))
            link(dve.tensor_scalar(scale_w[:, :], scale_w[:, :], 127.0, None, ALU.mult))
            link(dve.tensor_scalar(scale_x[:, 0:1], acc[:, 0, P:P + 1], 1e-8, None, ALU.max))
            link(dve.reciprocal(scale_x[:, 1:2], scale_x[:, 0:1]))
            link(dve.tensor_scalar(scale_x[:, 2:3], scale_x[:, 1:2], 32767.0, None, ALU.mult))
            dve.tensor_scalar(alpha[:, :], high_w[:, :], scale_x[:, 0:1], 1 / (127.0 * 32767.0), ALU.mult, ALU.mult).then_inc(s_scale, 1)
            for f in range(FT):
                link(dve.tensor_scalar(w[:, f, :], w[:, f, :], scale_w[:, f:f + 1], 127.0, ALU.mult, ALU.min))
                link(dve.tensor_scalar(w[:, f, :], w[:, f, :], -128.0, ROUND, ALU.max, ALU.add))
                dve.tensor_scalar(w16[:, f, :], w[:, f, :], ROUND, None, ALU.subtract).then_inc(s_w16, 1)

            def integers(n, c):
                x = raw[:, c, :, :]
                dve.tensor_scalar(x, x, scale_x[:, 2:3], 32767.0, ALU.mult, ALU.min).then_inc(s_r, 1)
                dve.wait_ge(s_r, n * 2 + 1)
                dve.tensor_scalar(x, x, -32768.0, ROUND, ALU.max, ALU.add).then_inc(s_r, 1)
                dve.wait_ge(s_r, n * 2 + 2)
                dve.tensor_scalar(x, x, ROUND, None, ALU.subtract).then_inc(s_q, 1)

            dve.wait_ge(s_x[0], 16)
            integers(0, 0)
            with dve.Fori(0, NCH // 2) as i:
                for p in range(NP):
                    if p in (1, 5):
                        c = 1 if p == 1 else 0
                        n = i * 2 + 2 - c
                        dve.wait_ge(s_x[c], (i + 2 - c) * 16)
                        integers(n, c)
                    dve.wait_ge(s_g, i * (2 * FT) + (HP * (p + 1) + 8))
                    if p == 0:
                        dve.wait_ge(s_high, i * (NP + 1) + 1)
                    dve.tensor_reduce(high[:, p:p + 1], g[:, p % 4, :, :], axis=AX.XY, op=ALU.max,
                                      apply_absolute_value=True).then_inc(s_read, 1)
                dve.wait_ge(s_read, i * NP + (NP + 4))
                dve.tensor_reduce(high[:, NP:NP + 1], high[:, :], axis=AX.X, op=ALU.max).then_inc(s_high, NP + 1)
            dve.wait_ge(s_high, NCH // 2 * (NP + 1) + 1)
            dve.tensor_copy(h_max[:, :], high[:, NP:NP + 1]).then_inc(s_high, 1)

        @block.scalar
        def _(act):
            act.sem_inc(s_g, 8)
            for s_stored in s_gs:
                act.sem_inc(s_stored, 16)
            for f in range(FT):
                act.wait_ge(s_wt, f + 1)
                src = acc[:, 1 + f % 2, :].bitcast(F16)[:, 0:KD * P].rearrange("p (k f) -> p k f", k=KD)
                act.activation(wq[:, :, f * P:(f + 1) * P], src, ACT.Copy).then_inc(s_wq, 1)

            def first_part(n, c):
                act.wait_ge(s_acc, n * FT + FT)
                act.wait_ge(s_q, n + 1)
                act.activation(hi[:, c, :, :], raw[:, c, :, :], ACT.Copy).then_inc(s_hi, 1)

            first_part(0, 0)
            act.wait_ge(s_scale, 2)
            with act.Fori(0, NCH // 2) as i:
                for o in range(2 * FT):
                    f, p = o % FT, o // HP
                    if o == 6:
                        first_part(i * 2 + 1, 1)
                    if o == FT + 6:
                        first_part(i * 2 + 2, 0)
                    if o % HP == 0:
                        act.wait_ge(s_gs[p % 4], (i * 2 + p // 4) * 16 + 16)
                        act.wait_ge(s_read, i * NP + p + 1)
                    act.wait_ge(s_acc, i * (2 * FT) + (2 * FT + o + 1))
                    act.activation(g[:, p % 4, o % HP, :], acc[:, o % 8, :], ACT.Gelu, bias=bias[:, f:f + 1],
                                   scale=alpha[:, f:f + 1]).then_inc(s_g, 1)

        @block.tensor
        def _(pe):
            pe.sem_inc(s_acc, 2 * FT)
            pe.wait_ge(s_w, 4 * 16)
            pe.wait_ge(s_scale, 1)
            spread_max(nc, m, pe, "pe", xn_max[:, :], 1, tops, acc[:, 0, :], ident, ones, s_pe0, s_top)
            for f in range(FT):
                if f >= 2:
                    pe.wait_ge(s_wq, f - 1)
                pe.wait_ge(s_w16, f + 1)
                bank = acc[:, 1 + f % 2, :].bitcast(F16)
                for k in range(KD):
                    last = pe.transpose(bank[:, k * P:(k + 1) * P], w16[:, f, k * P:(k + 1) * P], ident16[:, :])
                last.then_inc(s_wt, 1)
            pe.wait_ge(s_wq, FT)
            with pe.Fori(0, NCH // 2) as i:
                for o in range(2 * FT):
                    c, f = o // FT, o % FT
                    if f == 0:
                        pe.wait_ge(s_lo, i * 2 + c + 3)
                    pe.wait_ge(s_g, i * (2 * FT) + o + 1)
                    for k in range(KD):
                        for part in (hi, lo):
                            last = pe.matmul(acc[:, o % 8, :], wq[:, k, f * P:(f + 1) * P], part[:, c, k, :],
                                             start=(k == 0 and part is hi), stop=(k == KD - 1 and part is lo))
                    last.then_inc(s_acc, 1)


def contract(nc, w_out, b_out, ident_in, h_s, h_max, x1_s, out):
    with ExitStack() as ctx:
        m = Space(nc, ctx, "p5")
        HP = 4
        NP = FT // HP
        w, wq = m.sb("w", [P, 4, D]), m.sb("wq", [P, FT, D], F16)
        ident, bias = m.sb("ident", [P, P]), m.sb("b_out", [P, D])
        high_w, scale_w, rel = m.sb("high_w", [P, FT]), m.sb("scale_w", [P, FT]), m.sb("rel", [P, FT])
        both, tops, ones, sc = m.sb("both", [P, 2]), m.sb("tops", [2, 3]), m.sb("ones", [2, P]), m.sb("sc", [P, 4])
        h = m.sb("h", [P, 8, HP, CH])
        hi, lo = (m.sb(n, [P, 4, HP, CH], F16) for n in ("hi", "lo"))
        x1, y = m.sb("x1", [P, 2, CT, D]), m.sb("y", [P, CT, D])
        acc = m.ps("acc", [P, 8, D])

        s_c, s_w, s_chain, s_pe0, s_top = m.sem("constants_in"), m.sems("weights_in", 4), m.sem("chain"), m.sem("max_products"), m.sem("max_steps")
        s_ones, s_mark, s_wq = m.sem("ones"), m.sem("mark"), m.sem("w_integers")
        s_h = m.sems("h_in", 8)
        s_x = m.sems("x1_in", 2)
        s_ab, s_u, s_hi, s_xb = m.sem("rounding"), m.sem("scaled"), m.sem("h_hi"), m.sem("bias_added")
        s_lo = m.sem("h_lo")
        s_mm = m.sem("piece_product")
        s_y = m.sem("y")
        s_ys = m.sem("y_stored")
        block = ctx.enter_context(nc.Block())

        @block.sync
        def _(sync):
            for dst, src in ((ident, ident_in), (bias, b_out)):
                sync.dma_start(dst[:, :], src).then_inc(s_c, 16)
            for q in range(FT):
                if q >= 4:
                    sync.wait_ge(s_wq, q - 3)
                sync.dma_start(w[:, q % 4, :], w_out[q * P:(q + 1) * P, :]).then_inc(s_w[q % 4], 16)

            def load(n, c):
                for p in range(NP):
                    slot = c * NP + p
                    sync.wait_ge(s_lo, n * NP + p + 1)
                    sync.sem_inc(s_mark, 1)
                    sync.dma_start(h[:, slot, :, :], h_s[bass.ds(n % NCH * P, P), p * HP:(p + 1) * HP, :]).then_inc(s_h[slot], 16)

            load(0, 0)
            with sync.Fori(0, NCH // 2) as i:
                for c in range(2):
                    n = i * 2 + c
                    sync.wait_ge(s_y, n * CT + CT)
                    sync.sem_inc(s_mark, 1)
                    sync.dma_start(x1[:, c, :, :], x1_s[bass.ds(n * P, P), :, :]).then_inc(s_x[c], 16)
                    load(n + 1, 1 - c)

        @block.gpsimd
        def _(pool):
            pool.memset(ones[:, :], 1.0).then_inc(s_ones, 1)
            pool.sem_inc(s_lo, 8)
            pool.wait_ge(s_c, 2 * 16)

            def low_parts(n, c):
                for p in range(NP):
                    pool.wait_ge(s_hi, n * NP + p + 1)
                    pool.wait_ge(s_mm, n * NP + p + 1)
                    pool.tensor_tensor(lo[:, p, :, :], h[:, c * NP + p, :, :], hi[:, p, :, :], ALU.subtract).then_inc(s_lo, 1)

            low_parts(0, 0)
            with pool.Fori(0, NCH // 2) as i:
                for c in range(2):
                    low_parts(i * 2 + (c + 1), 1 - c)
                    pool.wait_ge(s_x[c], i * 16 + 16)
                    for t in range(CT):
                        pool.tensor_tensor(x1[:, c, t, :], x1[:, c, t, :], bias[:, :], ALU.add).then_inc(s_xb, 1)

        @block.vector
        def _(dve):
            steps = [0]

            def link(ins):
                steps[0] += 1
                ins.then_inc(s_chain, 1)
                dve.wait_ge(s_chain, steps[0])

            dve.sem_inc(s_y, 2 * CT)
            for q in range(FT):
                dve.wait_ge(s_w[q % 4], (q // 4 + 1) * 16)
                one, scale = high_w[:, q:q + 1], scale_w[:, q:q + 1]
                link(dve.tensor_reduce(one, w[:, q % 4, :], axis=AX.X, op=ALU.max, apply_absolute_value=True))
                link(dve.tensor_scalar(one, one, 1e-8, None, ALU.max))
                link(dve.reciprocal(scale, one))
                link(dve.tensor_scalar(scale, scale, 127.0, None, ALU.mult))
                link(dve.tensor_scalar(w[:, q % 4, :], w[:, q % 4, :], scale, 127.0, ALU.mult, ALU.min))
                link(dve.tensor_scalar(w[:, q % 4, :], w[:, q % 4, :], -128.0, ROUND, ALU.max, ALU.add))
                dve.tensor_scalar(wq[:, q, :], w[:, q % 4, :], ROUND, None, ALU.subtract).then_inc(s_wq, 1)
            link(dve.tensor_reduce(both[:, 0:1], high_w[:, :], axis=AX.X, op=ALU.max))
            dve.tensor_scalar(both[:, 1:2], h_max[:, :], 1e-8, None, ALU.max).then_inc(s_ones, 1)
            dve.wait_ge(s_ones, 2)
            spread_max(nc, m, dve, "dve", both[:, :], 2, tops, acc[:, 0, :], ident, ones, s_pe0, s_top)
            link(dve.tensor_copy(sc[:, 0:2], acc[:, 0, P:P + 2]))
            link(dve.reciprocal(sc[:, 2:4], sc[:, 0:2]))
            link(dve.tensor_scalar(rel[:, :], high_w[:, :], sc[:, 2:3], None, ALU.mult))
            link(dve.tensor_scalar(sc[:, 3:4], sc[:, 3:4], 32767.0, None, ALU.mult))
            link(dve.tensor_scalar(sc[:, 2:3], sc[:, 0:1], sc[:, 1:2], 1 / (127.0 * 32767.0), ALU.mult, ALU.mult))

            def integers(chunk, c, turn):
                for p in range(NP):
                    slot = c * NP + p
                    n = chunk * NP + p
                    v = h[:, slot, :, :]
                    dve.wait_ge(s_h[slot], turn * 16 + 16)
                    dve.tensor_scalar(v, v, sc[:, 3:4], 32767.0, ALU.mult, ALU.min).then_inc(s_ab, 1)
                    dve.wait_ge(s_ab, n * 2 + 1)
                    dve.tensor_scalar(v, v, -32768.0, ROUND, ALU.max, ALU.add).then_inc(s_ab, 1)
                    dve.wait_ge(s_ab, n * 2 + 2)
                    for f in range(HP):
                        dve.tensor_scalar(h[:, slot, f, :], h[:, slot, f, :], ROUND, rel[:, p * HP + f:p * HP + f + 1],
                                          ALU.subtract, ALU.mult).then_inc(s_u, 1)

            integers(0, 0, 0)
            with dve.Fori(0, NCH // 2) as i:
                for c in range(2):
                    integers(i * 2 + (c + 1), 1 - c, i + c)
                    dve.wait_ge(s_mm, (i * 2 + c) * NP + (NP + 4))
                    dve.wait_ge(s_xb, (i * 2 + c) * CT + CT)
                    dve.wait_ge(s_ys, (i * 2 + c) * 16 + 16)
                    for t in range(CT):
                        dve.scalar_tensor_tensor(y[:, t, :], acc[:, c * 4 + t, :], sc[:, 2:3], x1[:, c, t, :], ALU.mult, ALU.add).then_inc(s_y, 1)

        @block.scalar
        def _(act):
            act.sem_inc(s_ys, 16)

            def high_parts(chunk, c):
                for p in range(NP):
                    n = chunk * NP + p
                    act.wait_ge(s_u, n * HP + HP)
                    act.wait_ge(s_mm, n + 1)
                    act.activation(hi[:, p, :, :], h[:, c * NP + p, :, :], ACT.Copy).then_inc(s_hi, 1)

            high_parts(0, 0)
            with act.Fori(0, NCH // 2) as i:
                for c in range(2):
                    high_parts(i * 2 + (c + 1), 1 - c)
                    act.wait_ge(s_y, (i * 2 + c) * CT + (3 * CT))
                    act.dma_start(out[bass.ds((i * 2 + c) * CH, CH), :].rearrange("(t p) d -> p t d", p=P), y[:, :, :]).then_inc(s_ys, 16)
            act.wait_ge(s_ys, NCH * 16 + 16)

        @block.tensor
        def _(pe):
            pe.sem_inc(s_mm, 4)
            pe.wait_ge(s_c, 2 * 16)
            pe.wait_ge(s_ones, 2)
            spread_max(nc, m, pe, "pe", both[:, :], 2, tops, acc[:, 0, :], ident, ones, s_pe0, s_top)
            pe.wait_ge(s_chain, 6 * FT + 2)
            with pe.Fori(0, NCH // 2) as i:
                for c in range(2):
                    pe.wait_ge(s_y, (i * 2 + c) * CT + CT)
                    for p in range(NP):
                        pe.wait_ge(s_lo, i * 8 + (c * NP + p) + 9)
                        for f in range(HP):
                            for part in (hi, lo):
                                for t in range(CT):
                                    last = pe.matmul(acc[:, c * 4 + t, :], part[:, p, f, t * P:(t + 1) * P], wq[:, p * HP + f, :],
                                                     start=(p == 0 and f == 0 and part is hi),
                                                     stop=(p == NP - 1 and f == HP - 1 and part is lo))
                        last.then_inc(s_mm, 1)


def constants(np):
    left = np.arange(1024, 2048) / 1024
    right = (math.log(2.0) / left).astype(np.float16)
    best = np.argmin(np.abs(left * right.astype(np.float64) - math.log(2.0)))
    left, right = np.float16(left[best]), right[best]
    key, tile = np.arange(S)[None, :], np.arange(KT)[:, None]
    below = key < P * tile
    within = key // P == tile
    tri = np.arange(P)[:, None] <= np.arange(P)[None, :]
    zero = np.float16(0)
    return {
        "step_q": np.repeat(np.where(within, left, zero)[:, None, :], 4, axis=1),
        "step_k": np.repeat(np.where(below, right, zero)[:, None, :], 4, axis=1),
        "tri": np.where(tri, left, zero),
        "diag16": np.where(np.eye(P, dtype=bool), right, zero),
        "ident": np.eye(P, dtype=np.float32),
        "ident16": np.eye(P, dtype=np.float16),
    }



def build(nc, a, out):
    def dram(name, shape, dt=F32):
        return nc.dram_tensor(name, shape, dt, kind="Internal").ap()

    qT_s, kT_s, oT_s = (dram(n, [B * P, G, S]) for n in ("qT_s", "kT_s", "oT_s"))
    v_s = dram("v_s", [B * P, KT, D])
    x1_s = dram("x1_s", [NCH * P, CT, D])
    xnT_s = dram("xnT_s", [NCH * P, KD, CH])
    h_s = dram("h_s", [NCH * P, FT, CH])
    with (nc.sbuf_tensor("qk_max", [P, 2], F32) as qk_max, nc.sbuf_tensor("xn_max", [P, 1], F32) as xn_max,
          nc.sbuf_tensor("h_max", [P, 1], F32) as h_max):
        project(nc, a["x"], a["ctxT"], a["wq"], a["wk"], a["wv"], a["bq"], a["bk"], a["bv"], a["ident"], qT_s, kT_s, v_s, qk_max)
        attend(nc, qT_s, kT_s, v_s, qk_max, a["ident"], a["diag16"], a["tri"], a["step_q"], a["step_k"], oT_s)
        merge(nc, a["x"], a["wo"], a["bo"], a["ident"], oT_s, x1_s, xnT_s, xn_max)
        expand(nc, a["w_inT"], a["b_in"], a["ident"], a["ident16"], xnT_s, xn_max, h_s, h_max)
        contract(nc, a["w_out"], a["b_out"], a["ident"], h_s, h_max, x1_s, out)


def kernel(x, ctx_1024, L0_xattn_Wq, L0_xattn_bq, L0_xattn_Wk, L0_xattn_bk, L0_xattn_Wv, L0_xattn_bv,
           L0_xattn_Wo, L0_xattn_bo, L0_ffn_W_in, L0_ffn_b_in, L0_ffn_W_out, L0_ffn_b_out):
    import numpy as np
    import concourse.bacc as bacc
    from concourse.bass_utils import run_bass_kernel_spmd

    def rows(v):
        return np.ascontiguousarray(np.broadcast_to(np.asarray(v)[None, :], (P, len(v))))

    def cols(v):
        return np.ascontiguousarray(np.asarray(v).reshape(-1, P).T)

    arrays = {
        "x": np.ascontiguousarray(np.asarray(x).reshape(B * S, D)),
        "ctxT": np.ascontiguousarray(np.asarray(ctx_1024).reshape(B * S, D).T),
        "wq": np.asarray(L0_xattn_Wq), "wk": np.asarray(L0_xattn_Wk), "wv": np.asarray(L0_xattn_Wv), "wo": np.asarray(L0_xattn_Wo),
        "bq": cols(L0_xattn_bq), "bk": cols(L0_xattn_bk), "bv": rows(L0_xattn_bv), "bo": rows(L0_xattn_bo),
        "w_inT": np.ascontiguousarray(np.asarray(L0_ffn_W_in).T), "b_in": cols(L0_ffn_b_in),
        "w_out": np.asarray(L0_ffn_W_out), "b_out": rows(L0_ffn_b_out),
        **constants(np),
    }
    nc = bacc.Bacc("TRN2", target_bir_lowering=False, num_devices=1)
    a = {n: nc.dram_tensor(n, v.shape, mybir.dt.from_np(v.dtype), kind="ExternalInput").ap() for n, v in arrays.items()}
    out = nc.dram_tensor("out", (B * S, D), F32, kind="ExternalOutput").ap()
    build(nc, a, out)
    r = run_bass_kernel_spmd(nc, [arrays], core_ids=[0])
    return r.results[0]["out"].reshape(B, S, D)
```

```python
import math
from contextlib import ExitStack

import concourse.bass as bass
from concourse import mybir

F32 = mybir.dt.float32
F16 = mybir.dt.float16
I32 = mybir.dt.int32
ALU = mybir.AluOpType
ACT = mybir.ActivationFunctionType
AX = mybir.AxisListType

P = 128
B, S, D, F = 8, 1024, 512, 2048
H, HD = 16, 32
KD = D // P
FT = F // P
KT = S // P
G = H // 4
CH = 512
CT = CH // P
NCH = B * S // CH
EPS = 1e-5
ROUND = 1.5 * 2.0 ** 23
MAX_ROW = 2.0 ** 15
QK_ROWS = 3 * HD + 2 + KT
LN_SCALE = 2.0 ** 11


class Space:

    def __init__(self, nc, ctx, tag):
        self.nc, self.ctx, self.tag = nc, ctx, tag

    def sb(self, name, shape, dt=F32):
        return self.ctx.enter_context(self.nc.sbuf_tensor(f"{self.tag}_{name}", shape, dt))

    def ps(self, name, shape):
        return self.ctx.enter_context(self.nc.psum_tensor(f"{self.tag}_{name}", shape, F32))

    def sem(self, name):
        return self.ctx.enter_context(self.nc.semaphore(f"{self.tag}_{name}"))

    def sems(self, name, n):
        return [self.sem(f"{name}{i}") for i in range(n)]


def spread_max(eng, stage, src, n, tile, bank, ident, ones, sem_pe, sem_dve):
    top, diag = tile[0:n, 0:1], tile[0:n, 1:1 + n]
    if stage == "pe":
        eng.transpose(bank[0:n, 0:P], src, ident[:, :]).then_inc(sem_pe, 1)
        eng.wait_ge(sem_dve, 2)
        eng.matmul(bank[:, P:P + n], ones[0:n, :], diag, start=True, stop=True).then_inc(sem_pe, 1)
    else:
        eng.wait_ge(sem_pe, 1)
        eng.tensor_reduce(top, bank[0:n, 0:P], axis=AX.X, op=ALU.max).then_inc(sem_dve, 1)
        eng.wait_ge(sem_dve, 1)
        eng.tensor_scalar(diag, ident[0:n, 0:n], top, None, ALU.mult).then_inc(sem_dve, 1)
        eng.wait_ge(sem_pe, 2)


def flat(tiles):
    return tiles.rearrange("p k t -> p (k t)")


def power_scales(dve, link, scale, inverse, top):
    bits, inv = scale.bitcast(I32), inverse.bitcast(I32)
    link(dve.tensor_scalar(scale, top, 1e-30, 1e30, ALU.max, ALU.min))
    link(dve.tensor_scalar(bits, bits, 23, 23, ALU.logical_shift_right, ALU.logical_shift_left))
    link(dve.tensor_scalar(inv, bits, -(11 << 23), None, ALU.add))
    link(dve.tensor_scalar(bits, inv, -1, 254 << 23, ALU.mult, ALU.add))


def project_queries(nc, x, ctxT, wq, wk, wv, bq, ident_in, qT_s, w_hi, w_lo, w_inv, q_max, ctx_max):
    with ExitStack() as ctx:
        m = Space(nc, ctx, "p1")
        w32 = m.sb("w", [P, 3, KD, D])
        ident, bias, ones = m.sb("ident", [P, P]), m.sb("bq", [P, G]), m.sb("ones", [3, P])
        xn = m.sb("x", [P, 2, CT, D])
        cx = m.sb("ctx", [P, 2, KD, CH])
        hi, lo = (m.sb(n, [P, 2, KD, CH], F16) for n in ("hi", "lo"))
        qo = m.sb("qo", [P, 2, G, CH])
        stats, mv = m.sb("stats", [P, CT, 6]), m.sb("mv", [P, CT, 2])
        std, rstd, shift, eps = m.sb("std", [P, CT]), m.sb("rstd", [P, CT]), m.sb("shift", [P, CT]), m.sb("eps", [P, 1])
        factor = m.sb("factor", [P, 1])
        tops, w_top, w_scale = m.sb("tops", [3, 4]), m.sb("w_top", [P, 3]), m.sb("w_scale", [P, 3])
        high = m.sb("high", [P, 4])
        tr, acc = m.ps("tr", [P, KD, CH]), m.ps("acc", [P, G, CH])

        s_w, s_chain, s_pe0, s_top, s_parts = m.sem("weights_in"), m.sem("chain"), m.sem("max_products"), m.sem("max_steps"), m.sem("w_low_parts")
        s_wh = m.sem("w_high_parts")
        s_x, s_c, s_k0 = m.sems("x_in", 2), m.sems("ctx_in", 2), m.sem("constants_in")
        s_st, s_var, s_std, s_rstd = (m.sem(n) for n in ("stats", "var", "std", "rstd"))
        s_init, s_mark, s_hi, s_scale = m.sem("initial_values"), m.sem("mark"), m.sem("hi"), m.sem("w_scales")
        s_tr = m.sem("transposed")
        s_lo = m.sem("lo")
        s_acc = m.sem("q_product")
        s_q = m.sem("q_evacuated")
        s_cmax = m.sem("ctx_read")
        s_qmax = m.sem("q_read")
        s_high = m.sem("high")
        s_shift = m.sem("shift")
        s_xn = m.sem("xn")
        s_qs = m.sems("q_stored", 2)
        block = ctx.enter_context(nc.Block())

        @block.sync
        def _(sync):
            def load_x(n, c):
                sync.wait_ge(s_tr, n * KD + KD)
                sync.sem_inc(s_mark, 1)
                sync.dma_start(xn[:, c, :, :], x[bass.ds(n % NCH * CH, CH), :].rearrange("(t p) d -> p t d", p=P)).then_inc(s_x[c], 16)

            load_x(0, 0)
            for dst, src in ((ident, ident_in), (bias, bq)):
                sync.dma_start(dst[:, :], src).then_inc(s_k0, 16)
            for o, src in enumerate((wq, wk, wv)):
                sync.dma_start(w32[:, o, :, :], src.rearrange("(k p) n -> p k n", p=P)).then_inc(s_w, 16)
            load_x(1, 1)
            with sync.Fori(0, NCH // 2) as i:
                for c in range(2):
                    n = i * 2 + c
                    sync.wait_ge(s_cmax, n + 1)
                    sync.dma_start(cx[:, c, :, :], ctxT.rearrange("(k p) t -> p k t", p=P)[:, :, bass.ds(n * CH, CH)]).then_inc(s_c[c], 16)
                    load_x(n + 2, c)
            for c in range(2):
                sync.wait_ge(s_x[c], (NCH // 2 + 1) * 16)

        @block.gpsimd
        def _(pool):
            pool.memset(eps[:, :], EPS).then_inc(s_init, 1)
            pool.memset(ones[:, :], 1.0).then_inc(s_init, 1)
            pool.memset(high[:, :], 0.0).then_inc(s_init, 1)
            pool.memset(qo[:, 1, :, :], 0.0).then_inc(s_init, 1)

        @block.vector
        def _(dve):
            steps = [0]

            def link(ins):
                steps[0] += 1
                ins.then_inc(s_chain, 1)
                dve.wait_ge(s_chain, steps[0])

            def layernorm(n, c):
                dve.wait_ge(s_x[c], (n - c) * 8 + 16)
                for t in range(CT):
                    dve.bn_stats(stats[:, t, :], xn[:, c, t, :]).then_inc(s_st, 1)
                dve.wait_ge(s_st, n * CT + CT)
                dve.wait_ge(s_shift, n + 1)
                dve.sem_inc(s_mark, 1)
                for t in range(CT):
                    dve.bn_aggr(mv[:, t, :], stats[:, t, :]).then_inc(s_var, 1)
                dve.wait_ge(s_std, n + 1)
                dve.wait_ge(s_xn, n * CT + CT)
                dve.reciprocal(rstd[:, :], std[:, :]).then_inc(s_rstd, 1)
                dve.wait_ge(s_rstd, n + 1)
                dve.scalar_tensor_tensor(shift[:, :], mv[:, :, 0], -1.0, rstd[:, :], ALU.mult, ALU.mult).then_inc(s_shift, 1)

            def low_parts(n, c):
                dve.wait_ge(s_acc, n * G + G)
                for k in range(KD):
                    dve.wait_ge(s_hi, n * KD + k + 1)
                    dve.scalar_tensor_tensor(lo[:, c, k, :], tr[:, k, :], LN_SCALE, hi[:, c, k, :], ALU.mult, ALU.subtract).then_inc(s_lo, 1)

            def low_weights(o):
                dve.wait_ge(s_wh, o + 1)
                dve.scalar_tensor_tensor(flat(w_lo[:, o, :, :]), flat(w32[:, o, :, :]), w_scale[:, o:o + 1], flat(w_hi[:, o, :, :]),
                                         ALU.mult, ALU.subtract).then_inc(s_parts, 1)

            dve.sem_inc(s_lo, KD)
            dve.sem_inc(s_cmax, 2)
            dve.sem_inc(s_qmax, 1)
            dve.sem_inc(s_high, 1)
            dve.sem_inc(s_shift, 1)
            dve.wait_ge(s_init, 4)
            layernorm(0, 0)
            dve.wait_ge(s_w, 3 * 16)
            for o in range(3):
                link(dve.tensor_reduce(w_top[:, o:o + 1], w32[:, o, :, :], axis=AX.XY, op=ALU.max, apply_absolute_value=True))
            spread_max(dve, "dve", w_top[:, :], 3, tops, acc[:, 0, :], ident, ones, s_pe0, s_top)
            power_scales(dve, link, w_scale[:, :], w_inv[:, :], acc[:, 0, P:P + 3])
            dve.tensor_scalar(factor[:, :], w_inv[:, 0:1], 1 / LN_SCALE, None, ALU.mult).then_inc(s_scale, 1)
            low_weights(0)
            low_parts(0, 0)
            layernorm(1, 1)
            low_weights(1)
            low_weights(2)
            with dve.Fori(0, NCH // 2) as i:
                for c in range(2):
                    n = i * 2 + c
                    low_parts(n + 1, 1 - c)
                    layernorm(n + 2, c)
                    dve.wait_ge(s_c[c], i * 16 + 16)
                    dve.wait_ge(s_high, n + 1)
                    dve.tensor_reduce(high[:, 1:2], cx[:, c, :, :], axis=AX.XY, op=ALU.max, apply_absolute_value=True).then_inc(s_cmax, 1)
                    dve.wait_ge(s_q, n * G + G)
                    dve.tensor_reduce(high[:, 0:1], qo[:, 1 - c, :, :], axis=AX.XY, op=ALU.max, apply_absolute_value=True).then_inc(s_qmax, 1)
                    dve.wait_ge(s_cmax, n + 3)
                    dve.wait_ge(s_qmax, n + 2)
                    dve.tensor_tensor(high[:, 2:4], high[:, 2:4], high[:, 0:2], ALU.max).then_inc(s_high, 1)
            dve.wait_ge(s_q, NCH * G + G)
            dve.wait_ge(s_high, NCH + 1)
            link(dve.tensor_reduce(high[:, 0:1], qo[:, 1, :, :], axis=AX.XY, op=ALU.max, apply_absolute_value=True))
            dve.tensor_tensor(q_max[:, :], high[:, 2:3], high[:, 0:1], ALU.max).then_inc(s_high, 1)
            dve.tensor_copy(ctx_max[:, :], high[:, 3:4]).then_inc(s_high, 1)

        @block.scalar
        def _(act):
            act.sem_inc(s_q, G)
            for s_stored in s_qs:
                act.sem_inc(s_stored, 16)
            act.sem_inc(s_xn, CT)
            act.wait_ge(s_init, 4)

            def layernorm(n, c):
                act.wait_ge(s_var, n * CT + CT)
                act.activation(std[:, :], mv[:, :, 1], ACT.Sqrt, bias=eps[:, 0:1]).then_inc(s_std, 1)
                act.wait_ge(s_shift, n + 2)
                for t in range(CT):
                    act.activation(xn[:, c, t, :], xn[:, c, t, :], ACT.Identity, bias=shift[:, t:t + 1],
                                   scale=rstd[:, t:t + 1]).then_inc(s_xn, 1)

            def high_parts(n, c):
                act.wait_ge(s_acc, n * G + G)
                for k in range(KD):
                    act.wait_ge(s_tr, n * KD + (2 * KD + k + 1))
                    act.activation(hi[:, c, k, :], tr[:, k, :], ACT.Copy, scale=LN_SCALE).then_inc(s_hi, 1)

            def high_weights(o):
                act.activation(w_hi[:, o, :, :], w32[:, o, :, :], ACT.Identity, scale=w_scale[:, o:o + 1]).then_inc(s_wh, 1)

            layernorm(0, 0)
            act.wait_ge(s_k0, 2 * 16)
            act.wait_ge(s_scale, 1)
            high_weights(0)
            high_parts(0, 0)
            layernorm(1, 1)
            high_weights(1)
            high_weights(2)
            with act.Fori(0, NCH // 2) as i:
                for c in range(2):
                    n = i * 2 + c
                    high_parts(n + 1, 1 - c)
                    layernorm(n + 2, c)
                    act.wait_ge(s_qs[c], i * 16 + 16)
                    act.wait_ge(s_qmax, n + 1)
                    for g in range(G):
                        act.wait_ge(s_acc, n * G + (2 * G + g + 1))
                        act.activation(qo[:, c, g, :], acc[:, g, :], ACT.Identity, bias=bias[:, g:g + 1], scale=factor[:, 0:1]).then_inc(s_q, 1)
                    act.wait_ge(s_q, n * G + 2 * G)
                    act.dma_start(qT_s[bass.ds(i * P, P), :, c * CH:(c + 1) * CH], qo[:, c, :, :]).then_inc(s_qs[c], 16)
            for s_stored in s_qs:
                act.wait_ge(s_stored, (NCH // 2 + 1) * 16)

        @block.tensor
        def _(pe):
            pe.sem_inc(s_tr, 2 * KD)
            pe.sem_inc(s_acc, 2 * G)
            pe.wait_ge(s_k0, 2 * 16)
            pe.wait_ge(s_init, 4)

            def transposes(n, c):
                pe.wait_ge(s_xn, n * CT + 2 * CT)
                for k in range(KD):
                    pe.wait_ge(s_lo, n * KD + k + 1)
                    for t in range(CT):
                        last = pe.transpose(tr[:, k, t * P:(t + 1) * P], xn[:, c, t, k * P:(k + 1) * P], ident[:, :])
                    last.then_inc(s_tr, 1)

            transposes(0, 0)
            pe.wait_ge(s_chain, 3)
            spread_max(pe, "pe", w_top[:, :], 3, tops, acc[:, 0, :], ident, ones, s_pe0, s_top)
            pe.wait_ge(s_chain, 4)
            pe.wait_ge(s_parts, 1)
            with pe.Fori(0, NCH // 2) as i:
                for c in range(2):
                    n = i * 2 + c
                    transposes(n + 1, 1 - c)
                    pe.wait_ge(s_lo, n * KD + 2 * KD)
                    for g in range(G):
                        pe.wait_ge(s_q, n * G + g + 1)
                        three_products(pe, acc[:, g, :], lambda part, k: part[:, 0, k, g * P:(g + 1) * P],
                                       lambda part, k: part[:, c, k, :], (w_hi, w_lo), (hi, lo)).then_inc(s_acc, 1)


def three_products(pe, bank, stationary, moving, left, right):
    pairs = ((left[0], right[0]), (left[0], right[1]), (left[1], right[0]))
    for k in range(KD):
        for n, (a, b) in enumerate(pairs):
            last = pe.matmul(bank, stationary(a, k), moving(b, k), start=(k == 0 and n == 0), stop=(k == KD - 1 and n == 2))
    return last


def quantise_tile(dve, w, out, high, top, scale, sem_step, first, sem_done):
    dve.tensor_reduce(top, w, axis=AX.X, op=ALU.max, apply_absolute_value=True).then_inc(sem_step, 1)
    dve.wait_ge(sem_step, first + 1)
    dve.tensor_scalar(top, top, 1e-8, None, ALU.max).then_inc(sem_step, 1)
    dve.wait_ge(sem_step, first + 2)
    dve.reciprocal(scale, top).then_inc(sem_step, 1)
    dve.tensor_scalar(high, top, 1e-8, None, ALU.max).then_inc(sem_step, 1)
    dve.wait_ge(sem_step, first + 4)
    dve.tensor_scalar(scale, scale, 127.0, None, ALU.mult).then_inc(sem_step, 1)
    dve.wait_ge(sem_step, first + 5)
    dve.tensor_scalar(w, w, scale, 127.0, ALU.mult, ALU.min).then_inc(sem_step, 1)
    dve.wait_ge(sem_step, first + 6)
    dve.tensor_scalar(w, w, -128.0, ROUND, ALU.max, ALU.add).then_inc(sem_step, 1)
    dve.wait_ge(sem_step, first + 7)
    dve.tensor_scalar(out, w, ROUND, None, ALU.subtract).then_inc(sem_done, 1)


def project_context(nc, ctxT, bk, bv, w_inT, w_out, ident_in, ident16_in, kT_s, v_s, w_hi, w_lo, w_inv, ctx_max,
                    k_max, win16, win_high, wout16, wout_high):
    assert FT == NCH
    with ExitStack() as ctx:
        m = Space(nc, ctx, "p2")
        ident, ident16, ones = m.sb("ident", [P, P]), m.sb("ident16", [P, P], F16), m.sb("ones", [3, P])
        bias_k, bias_v = m.sb("bk", [P, G]), m.sb("bv", [P, D])
        cx = m.sb("ctx", [P, 2, KD, CH])
        hi, lo = (m.sb(n, [P, 2, KD, CH], F16) for n in ("hi", "lo"))
        ko, vo = m.sb("ko", [P, 2, G, CH]), m.sb("vo", [P, 2, CT, D])
        tops, sc = m.sb("tops", [3, 4]), m.sb("sc", [P, 4])
        wi, wo = m.sb("wi", [P, 2, D]), m.sb("wo", [P, 2, D])
        wi_int, row = m.sb("wi_int", [P, 2, D], F16), m.sb("row", [P, 4])
        high = m.sb("high", [P, 2])
        acc, acc_v, tr = m.ps("acc", [P, G, CH]), m.ps("acc_v", [P, 2, D]), m.ps("tr", [P, CH])

        s_c0, s_chain, s_pe0, s_top, s_init = m.sem("constants_in"), m.sem("chain"), m.sem("max_products"), m.sem("max_steps"), m.sem("initial_values")
        s_c, s_w = m.sems("ctx_in", 2), m.sems("w_in", 2)
        s_mark, s_hi, s_scale = m.sem("mark"), m.sem("hi"), m.sem("scales")
        s_step, s_wt = m.sem("rounding"), m.sem("w_transposed")
        s_lo = m.sem("lo")
        s_acc = m.sem("k_product")
        s_accv = m.sem("v_product")
        s_k, s_v = m.sem("k_evacuated"), m.sem("v_evacuated")
        s_kmax = m.sem("k_read")
        s_high = m.sem("high")
        s_wi, s_wo = m.sem("w_in_integers"), m.sem("w_out_integers")
        s_wd = m.sem("w_transpose_evacuated")
        s_ks, s_vs = m.sems("k_stored", 2), m.sems("v_stored", 2)
        block = ctx.enter_context(nc.Block())

        @block.sync
        def _(sync):
            for dst, src in ((ident, ident_in), (ident16, ident16_in), (bias_k, bk), (bias_v, bv)):
                sync.dma_start(dst[:, :], src).then_inc(s_c0, 16)

            def load(n, c):
                sync.wait_ge(s_lo, n + 1)
                sync.sem_inc(s_mark, 1)
                sync.dma_start(cx[:, c, :, :], ctxT.rearrange("(k p) t -> p k t", p=P)[:, :, bass.ds(n % NCH * CH, CH)]).then_inc(s_c[c], 16)

            load(0, 0)
            with sync.Fori(0, NCH // 2) as i:
                for c in range(2):
                    n = i * 2 + c
                    load(n + 1, 1 - c)
                    sync.wait_ge(s_wi, n + 1)
                    sync.sem_inc(s_mark, 1)
                    sync.dma_start(wi[:, c, :], w_inT[bass.ds(n * P, P), :]).then_inc(s_w[c], 16)
                    sync.wait_ge(s_wo, n + 1)
                    sync.sem_inc(s_mark, 1)
                    sync.dma_start(wo[:, c, :], w_out[bass.ds(n * P, P), :]).then_inc(s_w[c], 16)
            sync.wait_ge(s_c[0], (NCH // 2 + 1) * 16)

        @block.gpsimd
        def _(pool):
            pool.memset(ones[:, :], 1.0).then_inc(s_init, 1)
            pool.memset(high[:, :], 0.0).then_inc(s_init, 1)
            pool.memset(ko[:, 1, :, :], 0.0).then_inc(s_init, 1)

        @block.vector
        def _(dve):
            steps = [0]

            def link(ins):
                steps[0] += 1
                ins.then_inc(s_chain, 1)
                dve.wait_ge(s_chain, steps[0])

            def low_part(n, c):
                dve.wait_ge(s_hi, n + 1)
                dve.scalar_tensor_tensor(flat(lo[:, c, :, :]), flat(cx[:, c, :, :]), sc[:, 0:1],
                                         flat(hi[:, c, :, :]), ALU.mult, ALU.subtract).then_inc(s_lo, 1)

            dve.sem_inc(s_lo, 2)
            dve.sem_inc(s_v, 2)
            dve.sem_inc(s_wi, 2)
            dve.sem_inc(s_kmax, 1)
            dve.sem_inc(s_high, 1)
            dve.sem_inc(s_wo, 2)
            dve.wait_ge(s_init, 3)
            dve.wait_ge(s_c0, 4 * 16)
            spread_max(dve, "dve", ctx_max[:, :], 1, tops, acc[:, 0, :], ident, ones, s_pe0, s_top)
            power_scales(dve, link, sc[:, 0:1], sc[:, 1:2], acc[:, 0, P:P + 1])
            dve.tensor_scalar(sc[:, 2:4], w_inv[:, 1:3], sc[:, 1:2], None, ALU.mult).then_inc(s_scale, 1)
            low_part(0, 0)
            with dve.Fori(0, NCH // 2) as i:
                for c in range(2):
                    n = i * 2 + c
                    dve.wait_ge(s_vs[c], i * 16 + 16)
                    for t in range(CT):
                        dve.wait_ge(s_accv, n * CT + t + 1)
                        dve.scalar_tensor_tensor(vo[:, c, t, :], acc_v[:, t % 2, :], sc[:, 3:4], bias_v[:, :], ALU.mult, ALU.add).then_inc(s_v, 1)
                    low_part(n + 1, 1 - c)
                    dve.wait_ge(s_k, n * G + G)
                    dve.wait_ge(s_high, n + 1)
                    dve.tensor_reduce(high[:, 0:1], ko[:, 1 - c, :, :], axis=AX.XY, op=ALU.max, apply_absolute_value=True).then_inc(s_kmax, 1)
                    dve.wait_ge(s_kmax, n + 2)
                    dve.tensor_tensor(high[:, 1:2], high[:, 0:1], high[:, 1:2], ALU.max).then_inc(s_high, 1)
                    dve.wait_ge(s_w[c], i * 32 + 32)
                    dve.wait_ge(s_wd, n + 1)
                    quantise_tile(dve, wi[:, c, :], wi_int[:, c, :], win_high[:, bass.ds(n, 1)], row[:, 0:1], row[:, 1:2], s_step, n * 14, s_wi)
                    quantise_tile(dve, wo[:, c, :], wout16[:, bass.ds(n, 1), :].rearrange("p a d -> p (a d)"), wout_high[:, bass.ds(n, 1)],
                                  row[:, 2:3], row[:, 3:4], s_step, n * 14 + 7, s_wo)
            dve.wait_ge(s_k, NCH * G + G)
            dve.wait_ge(s_high, NCH + 1)
            link(dve.tensor_reduce(high[:, 0:1], ko[:, 1, :, :], axis=AX.XY, op=ALU.max, apply_absolute_value=True))
            dve.tensor_tensor(k_max[:, :], high[:, 1:2], high[:, 0:1], ALU.max).then_inc(s_high, 1)

        @block.scalar
        def _(act):
            act.sem_inc(s_k, G)
            act.sem_inc(s_wd, 2)
            for s_stored in (*s_ks, *s_vs):
                act.sem_inc(s_stored, 16)

            def high_part(n, c):
                act.wait_ge(s_acc, n * G + G)
                act.wait_ge(s_c[c], (n - c) * 8 + 16)
                act.activation(hi[:, c, :, :], cx[:, c, :, :], ACT.Identity, scale=sc[:, 0:1]).then_inc(s_hi, 1)

            act.wait_ge(s_scale, 1)
            high_part(0, 0)
            with act.Fori(0, NCH // 2) as i:
                for c in range(2):
                    n = i * 2 + c
                    high_part(n + 1, 1 - c)
                    act.wait_ge(s_ks[c], i * 16 + 16)
                    act.wait_ge(s_kmax, n + 1)
                    for g in range(G):
                        act.wait_ge(s_acc, n * G + (2 * G + g + 1))
                        act.activation(ko[:, c, g, :], acc[:, g, :], ACT.Identity, bias=bias_k[:, g:g + 1], scale=sc[:, 2:3]).then_inc(s_k, 1)
                    act.wait_ge(s_v, n * CT + (CT + 2))
                    act.dma_start(v_s[bass.ds(i * P, P), c * CT:(c + 1) * CT, :], vo[:, c, :, :]).then_inc(s_vs[c], 16)
                    act.wait_ge(s_k, n * G + 2 * G)
                    act.dma_start(kT_s[bass.ds(i * P, P), :, c * CH:(c + 1) * CH], ko[:, c, :, :]).then_inc(s_ks[c], 16)
                    act.wait_ge(s_wt, n + 1)
                    act.activation(win16[:, :, bass.ds(n * P, P)], tr[:, :].bitcast(F16)[:, 0:KD * P].rearrange("p (k f) -> p k f", k=KD),
                                   ACT.Copy).then_inc(s_wd, 1)
            for s_stored in (*s_ks, *s_vs):
                act.wait_ge(s_stored, (NCH // 2 + 1) * 16)

        @block.tensor
        def _(pe):
            pe.sem_inc(s_acc, 2 * G)
            pe.wait_ge(s_c0, 4 * 16)
            pe.wait_ge(s_init, 3)
            spread_max(pe, "pe", ctx_max[:, :], 1, tops, acc[:, 0, :], ident, ones, s_pe0, s_top)
            pe.wait_ge(s_chain, 1)
            with pe.Fori(0, NCH // 2) as i:
                for c in range(2):
                    n = i * 2 + c
                    pe.wait_ge(s_lo, n + 3)
                    for t in range(CT):
                        pe.wait_ge(s_v, n * CT + t + 1)
                        three_products(pe, acc_v[:, t % 2, :], lambda part, k: part[:, c, k, t * P:(t + 1) * P],
                                       lambda part, k: part[:, 2, k, :], (hi, lo), (w_hi, w_lo)).then_inc(s_accv, 1)
                    for g in range(G):
                        pe.wait_ge(s_k, n * G + g + 1)
                        three_products(pe, acc[:, g, :], lambda part, k: part[:, 1, k, g * P:(g + 1) * P],
                                       lambda part, k: part[:, c, k, :], (w_hi, w_lo), (hi, lo)).then_inc(s_acc, 1)
                    pe.wait_ge(s_wi, n + 3)
                    pe.wait_ge(s_wd, n + 2)
                    for k in range(KD):
                        last = pe.transpose(tr[:, :].bitcast(F16)[:, k * P:(k + 1) * P], wi_int[:, c, k * P:(k + 1) * P], ident16[:, :])
                    last.then_inc(s_wt, 1)


def attend(nc, qT_s, kT_s, v_s, qk_max, ident_in, ident16_in, diag_in, tri_in, step_q, step_k, oT_s):
    with ExitStack() as ctx:
        m = Space(nc, ctx, "p3")
        TURNS = B * G // 2
        NB = 4
        QK = 3 * HD
        ident, ident16, diag16, tri = m.sb("ident", [P, P]), m.sb("ident16", [P, P], F16), m.sb("diag16", [P, P], F16), m.sb("tri", [P, P], F16)
        qs, ks = ([m.sb(f"{n}{p}", [QK_ROWS, 4, S], F16) for p in range(2)] for n in ("qs", "ks"))
        raw, scaled = ([m.sb(f"{n}{o}", [P, S]) for o in range(2)] for n in ("raw", "scaled"))
        hi, lo = ([m.sb(f"{n}{o}", [P, S], F16) for o in range(2)] for n in ("hi", "lo"))
        v = [m.sb(f"v{p}", [P, KT, P]) for p in range(2)]
        probT = m.sb("probT", [P, 2, 4, 2, CH])
        pair_sum = m.sb("pair_sum", [P, 2, 4, CH])
        oT = m.sb("oT", [P, 2, S])
        pv_out, sum_out, recip = m.sb("pv_out", [P, CH]), m.sb("sum_out", [P, CH]), m.sb("recip", [P, CH])
        half_max, negmax = m.sb("half_max", [P, 2, 4, 2]), m.sb("negmax", [P, 4])
        max_parts = m.sb("max_parts", [P, 2, 4, 2], F16)
        sc, ones = m.sb("sc", [P, 16]), m.sb("ones", [P, P])
        top = m.sb("top", [2, 3])
        scoresT = m.ps("scoresT", [P, 2, 2, CH])
        scores = m.ps("scores", [P, 2, CH])
        acc, acc_sum = m.ps("acc", [P, CH]), m.ps("acc_sum", [P, CH])

        s_const, s_fill = m.sem("constants_in"), m.sem("step_rows_in")
        s_chain, s_pe0, s_scale = m.sem("chain"), m.sem("scale_products"), m.sem("scales")
        s_in, s_qk, s_v = m.sem("qk_in"), m.sems("qk_parts_in", 2), m.sems("v_in", 2)
        s_init, s_mark = m.sem("initial_values"), m.sem("mark")
        s_st, s_mx = m.sem("scoresT"), m.sem("scores")
        s_cmb, s_mp, s_rc = m.sem("max_combined"), m.sem("max_parts"), m.sem("max_rows_written")
        s_split = m.sem("split")
        s_lo = m.sem("lo")
        s_exp = m.sem("exp")
        s_pre = m.sem("pair_sum")
        s_pv, s_sum = m.sem("pv"), m.sem("sums")
        s_red = m.sem("reduced")
        s_rows = m.sem("max_rows")
        s_raw = m.sem("evacuated")
        s_rec = m.sem("reciprocal")
        s_out = m.sem("oT_written")
        s_o = m.sems("oT_stored", 2)
        block = ctx.enter_context(nc.Block())

        def bank_of(j, n):
            return (j + n + (n >= 2)) % 2

        def rows_bank(j):
            return j % 2

        def wait_apart(eng, sem, count):
            eng.wait_ge(sem, count)
            eng.sem_inc(s_mark, 1)

        @block.sync
        def _(sync):
            for dst, src in ((ident, ident_in), (ident16, ident16_in), (diag16, diag_in), (tri, tri_in)):
                sync.dma_start(dst[:, :], src).then_inc(s_const, 16)

            def load_raw(n, b, g):
                wait_apart(sync, s_split, n * 4 + 4)
                for buf, src in zip(raw, (kT_s, qT_s)):
                    sync.dma_start(buf[:, :].unsqueeze(1), src[bass.ds(b * P, P), bass.ds(g, 1), :]).then_inc(s_in, 16)

            def load_parts(n, par):
                wait_apart(sync, s_lo, n * 2 + 4)
                for o, (dst, parts) in enumerate(((ks[par], (hi, lo, hi)), (qs[par], (hi, hi, lo)))):
                    for r, part in enumerate(parts):
                        for j in range(4):
                            sync.dma_start(dst[r * HD:(r + 1) * HD, j, :],
                                           part[o][j * HD:(j + 1) * HD, :]).then_inc(s_qk[par], 16)

            def load_v(par, b, g):
                sync.dma_start(v[par][:, :, :], v_s[bass.ds(b * P, P), :, bass.ds(g * P, P)]).then_inc(s_v[par], 16)

            for par in range(2):
                load_raw(par, 0, par)
                if par == 0:
                    load_v(1, 0, 1)
                    load_v(0, 0, 0)
                    for q in qs:
                        sync.dma_start(q[QK + 2:QK_ROWS, :, :], step_q).then_inc(s_fill, 16)
                    for k in ks:
                        sync.dma_start(k[QK:QK_ROWS, :, :], step_k).then_inc(s_fill, 16)
                load_parts(par, par)
            load_raw(2, 0, 2)
            with sync.Fori(0, TURNS) as i:
                nxt, after = (i + 1) % TURNS, (i + 2) % TURNS
                for par in range(2):
                    b, g, n = nxt // 2, (nxt % 2) * 2 + par, i * 2 + (2 + par)
                    wait_apart(sync, s_st, i * (16 * NB) + 32 * (par + 1))
                    load_parts(n, par)
                    if par == 0:
                        load_raw(n + 1, nxt // 2, (nxt % 2) * 2 + 1)
                    else:
                        load_raw(n + 1, after // 2, (after % 2) * 2)
                    wait_apart(sync, s_out, i * NB + (2 * (par + 1) + 2))
                    sync.dma_start(oT_s[bass.ds(i // 2 * P, P), bass.ds((i % 2) * 2 + par, 1), :], oT[:, par:par + 1, :]).then_inc(s_o[par], 16)
                    load_v(par, b, g)
            sync.wait_ge(s_in, (2 * TURNS + 3) * 32)
            for par in range(2):
                sync.wait_ge(s_o[par], TURNS * 16 + 16)
                sync.wait_ge(s_v[par], TURNS * 16 + 16)
                sync.wait_ge(s_qk[par], (TURNS + 1) * 24 * 16)

        @block.gpsimd
        def _(pool):
            pool.memset(ones[:, :], 1.0).then_inc(s_scale, 1)
            pool.sem_inc(s_lo, 2)
            pool.sem_inc(s_pre, 8)
            pool.sem_inc(s_out, 1)

            def low_part(n, o):
                pool.wait_ge(s_split, n * 4 + (2 * o + 6))
                pool.tensor_tensor(lo[o][:, :], scaled[o][:, :], hi[o][:, :], ALU.subtract).then_inc(s_lo, 1)

            low_part(0, 0)
            low_part(0, 1)
            pool.memset(probT[:, 1, :, :, :], 0.0).then_inc(s_init, 1)
            pool.memset(pair_sum[:, 1, :, :], 1.0).then_inc(s_init, 1)
            low_part(1, 0)
            low_part(1, 1)
            pool.wait_ge(s_init, 2)
            with pool.Fori(0, TURNS) as i:
                for t in range(NB):
                    blk = i * NB + t
                    for p in range(4):
                        for j in range(4):
                            pair, step = blk * 4 + p, p * 4 + j
                            if j == 0:
                                pool.wait_ge(s_sum, pair + 1)
                            pool.wait_ge(s_exp, blk * 16 + (step + 3))
                            pool.tensor_tensor(pair_sum[:, p % 2, j, :], probT[:, p % 2, j, 0, :], probT[:, p % 2, j, 1, :],
                                               ALU.add).then_inc(s_pre, 1)
                            if t % 2 == 1 and step in (8, 15):
                                low_part(i * 2 + (2 + t // 2), 0 if step == 8 else 1)
                            if step == 15:
                                par, half = (t - 1) // 2 % 2, (t - 1) % 2
                                if half == 0:
                                    pool.wait_ge(s_o[par], i * 16 + 16)
                                pool.wait_ge(s_rec, blk * 8 + 16)
                                pool.tensor_tensor(oT[:, par, half * CH:(half + 1) * CH], pv_out[:, :], recip[:, :],
                                                   ALU.mult).then_inc(s_out, 1)
            pool.wait_ge(s_rec, TURNS * NB * 8 + 16)
            pool.tensor_tensor(oT[:, 1, CH:2 * CH], pv_out[:, :], recip[:, :], ALU.mult).then_inc(s_out, 1)

        @block.vector
        def _(dve):
            dve.sem_inc(s_red, 2)
            dve.sem_inc(s_rec, 8)
            steps = [0]

            def link(ins):
                steps[0] += 1
                ins.then_inc(s_chain, 1)
                dve.wait_ge(s_chain, steps[0])

            dve.wait_ge(s_pe0, 1)
            link(dve.tensor_reduce(top[:, 0:1], acc[0:2, 0:P], axis=AX.X, op=ALU.max))
            link(dve.tensor_scalar(top[:, 1:3], ident[0:2, 0:2], top[:, 0:1], None, ALU.mult))
            dve.wait_ge(s_pe0, 2)
            link(dve.tensor_scalar(sc[:, 0:2], acc[:, P:P + 2], 1e-18, 1e18, ALU.max, ALU.min))
            link(dve.reciprocal(sc[:, 2:3], sc[:, 1:2]))
            link(dve.tensor_scalar(sc[:, 3:4], sc[:, 0:1], sc[:, 2:3], math.sqrt(HD), ALU.mult, ALU.mult))
            bits = sc[:, :].bitcast(I32)
            link(dve.tensor_scalar(bits[:, 4:5], bits[:, 3:4], 24, 23, ALU.logical_shift_right, ALU.logical_shift_left))
            link(dve.tensor_scalar(bits[:, 5:6], bits[:, 4:5], 64 << 23, None, ALU.add))
            link(dve.tensor_scalar(bits[:, 8:9], bits[:, 5:6], -1, 254 << 23, ALU.mult, ALU.add))
            dve.tensor_scalar(sc[:, 9:10], sc[:, 5:6], 1 / math.sqrt(HD), None, ALU.mult).then_inc(s_scale, 1)

            def maxima(head, par, n):
                dve.wait_ge(s_mx, head * 8 + (n + 1))
                dve.tensor_reduce(half_max[:, par, n // 2, n % 2:n % 2 + 1], scores[:, bank_of(par, n), :], axis=AX.X, op=ALU.max,
                                  negate=True).then_inc(s_red, 1)

            def combine(head, par):
                dve.wait_ge(s_red, head * 8 + 10)
                dve.tensor_tensor(negmax[:, :], half_max[:, par, :, 0], half_max[:, par, :, 1], ALU.min).then_inc(s_cmb, 1)
                dve.wait_ge(s_rows, head + 1)
                dve.wait_ge(s_cmb, head * 2 + 1)
                dve.tensor_scalar(max_parts[:, par, :, 0], negmax[:, :], 1 / MAX_ROW, None, ALU.mult).then_inc(s_cmb, 1)
                dve.wait_ge(s_cmb, head * 2 + 2)
                dve.scalar_tensor_tensor(max_parts[:, par, :, 1], negmax[:, :], 1 / MAX_ROW, max_parts[:, par, :, 0],
                                         ALU.mult, ALU.subtract).then_inc(s_mp, 1)
                dve.wait_ge(s_mp, head + 1)

            def reciprocals(blk, e):
                if e == 0:
                    dve.wait_ge(s_raw, blk * 2 + 2)
                    dve.wait_ge(s_out, blk + 1)
                    dve.sem_inc(s_mark, 1)
                dve.reciprocal(recip[:, e * 64:(e + 1) * 64], sum_out[:, e * 64:(e + 1) * 64]).then_inc(s_rec, 1)

            for p in range(4):
                for n in range(8):
                    maxima(p, p % 2, n)
                    if n == 0 and p > 0:
                        combine(p - 1, (p - 1) % 2)
            with dve.Fori(0, TURNS) as i:
                for t in range(NB):
                    blk = i * NB + t
                    eighth = 0
                    for p in range(4):
                        for n in range(8):
                            maxima(blk * 4 + (4 + p), p % 2, n)
                            if n == 0:
                                combine(blk * 4 + (3 + p), (p + 3) % 2)
                            if p > 0 and n in (1, 3, 5) and eighth < 8:
                                reciprocals(blk, eighth)
                                eighth += 1
            for e in range(8):
                reciprocals(TURNS * NB, e)

        @block.scalar
        def _(act):
            act.sem_inc(s_split, 4)
            act.sem_inc(s_exp, 2)
            for par in range(2):
                act.sem_inc(s_o[par], 16)

            def split(n, o, part):
                out = (scaled, hi)[part][o]
                act.activation(out[:, :], raw[o][:, :], ACT.Identity, scale=sc[:, 8 + o:9 + o]).then_inc(s_split, 1)

            def write_max_rows(head, par, half, j):
                act.wait_ge(s_rows, head + 3)
                act.activation(qs[par][QK:QK + 2, j, half * CH:(half + 1) * CH], scores[QK:QK + 2, rows_bank(j + 1), :],
                               ACT.Copy).then_inc(s_rc, 1)

            def evacuate(blk, out, src, sem):
                act.wait_ge(sem, blk * 4 + 2)
                act.wait_ge(s_out, blk + 1)
                act.wait_ge(s_rec, blk * 8 + 8)
                act.activation(out[:, :], src[:, :], ACT.Copy).then_inc(s_raw, 1)

            act.wait_ge(s_scale, 2)
            for n in range(2):
                act.wait_ge(s_in, n * 32 + 32)
                act.wait_ge(s_lo, n * 2 + 2)
                if n == 1:
                    act.wait_ge(s_qk[0], 24 * 16)
                for o in range(2):
                    split(n, o, 0)
                    split(n, o, 1)
            for head in range(3):
                write_max_rows(head, 0, 0, head)
            with act.Fori(0, TURNS) as i:
                for t in range(NB):
                    blk = i * NB + t
                    for p in range(4):
                        for j in range(4):
                            pair, step = blk * 4 + p, p * 4 + j
                            if j == 2:
                                other = (t + (p > 0)) % NB
                                write_max_rows(pair + 3, other // 2, other % 2, (p + 3) % 4)
                            if j == 0:
                                act.wait_ge(s_pv, pair + 1)
                            act.wait_ge(s_pre, blk * 16 + (step + 1))
                            act.wait_ge(s_st, blk * 16 + (step + 1))
                            act.activation(probT[:, p % 2, j, :, :], scoresT[:, j % 2, :, :], ACT.Exp).then_inc(s_exp, 1)
                            if step == 3:
                                evacuate(blk, pv_out, acc, s_pv)
                            if step == 4:
                                evacuate(blk, sum_out, acc_sum, s_sum)
                            if t % 2 == 1 and j == 2:
                                n, q = i * 2 + (2 + t // 2), t // 2
                                if p == 0:
                                    act.wait_ge(s_in, n * 32 + 32)
                                    act.wait_ge(s_lo, n * 2 + 2)
                                    act.wait_ge(s_qk[1 - q], (i + 1 + q) * (24 * 16))
                                    act.sem_inc(s_mark, 1)
                                split(n, p // 2, p % 2)
            evacuate(TURNS * NB, pv_out, acc, s_pv)
            evacuate(TURNS * NB, sum_out, acc_sum, s_sum)

        @block.tensor
        def _(pe):
            pe.sem_inc(s_pv, 1)
            pe.sem_inc(s_sum, 1)
            pe.sem_inc(s_rows, 2)
            pe.wait_ge(s_const, 4 * 16)
            pe.transpose(acc[0:2, 0:P], qk_max[:, :], ident[:, :]).then_inc(s_pe0, 1)
            pe.wait_ge(s_chain, 2)
            pe.wait_ge(s_scale, 1)
            pe.matmul(acc[:, P:P + 2], ones[0:2, :], top[:, 1:3], start=True, stop=True).then_inc(s_pe0, 1)

            def make_scores(head, t, p, n):
                par, qt, half = t // 2 % 2, t % 2 * 4 + n // 2, n % 2
                if n == 3:
                    if t > 0 or p > 0:
                        pe.wait_ge(s_rc, head)
                elif n == 2:
                    pe.wait_ge(s_red, head * 8 + 4)
                else:
                    pe.wait_ge(s_red, head * 8 + (n + 1))
                pe.matmul(scores[:, bank_of(p, n), :], qs[par][0:QK, p, qt * P:(qt + 1) * P],
                          ks[par][0:QK, p, half * CH:(half + 1) * CH], start=True, stop=True).then_inc(s_mx, 1)

            def make_max_rows(head, p):
                pe.wait_ge(s_mp, head + 1)
                pe.wait_ge(s_red, head * 8 + 11)
                for qt in range(4):
                    last = pe.matmul(scores[QK:QK + 2, rows_bank(p), qt * P:(qt + 1) * P], max_parts[:, (p - 1) % 2, qt, :],
                                     ident16[:, :], start=True, stop=True)
                last.then_inc(s_rows, 1)

            def make_scoresT(blk, t, p, j):
                step = p * 4 + j
                par, half = t // 2, t % 2
                pe.wait_ge(s_exp, blk * 16 + (step + 1))
                if p == 0:
                    pe.wait_ge(s_rc, blk * 4 + (j + 1))
                for k in range(2):
                    kt = 2 * p + k
                    bank = scoresT[:, j % 2, k, :]
                    diagonal = kt // 4 == half
                    last = pe.matmul(bank, ks[par][:, j, kt * P:(kt + 1) * P], qs[par][:, j, half * CH:(half + 1) * CH],
                                     start=True, stop=not diagonal)
                    if diagonal:
                        last = pe.matmul(bank[:, (kt % 4) * P:(kt % 4 + 1) * P], diag16[:, :], tri[:, :], start=False, stop=True)
                last.then_inc(s_st, 1)

            def pv(par, p, k):
                for j in range(4):
                    last = pe.matmul(acc[j * HD:(j + 1) * HD, :], v[par][:, 2 * p + k, j * HD:(j + 1) * HD],
                                     probT[:, p % 2, j, k, :], start=(p == 0 and k == 0), stop=(p == 3 and k == 1))
                return last

            def sums(p):
                for j in range(4):
                    last = pe.matmul(acc_sum[j * HD:(j + 1) * HD, :], ones[:, 0:HD], pair_sum[:, p % 2, j, :],
                                     start=(p == 0), stop=(p == 3))
                return last

            pe.wait_ge(s_qk[0], 24 * 16)
            for p in range(4):
                for n in range(8):
                    if p > 0 and n == 2:
                        make_max_rows(p - 1, p)
                    make_scores(p, 0, p, n)
            pe.wait_ge(s_fill, 4 * 16)
            pe.wait_ge(s_v[1], 16)
            pe.wait_ge(s_init, 2)
            for j in range(4):
                pe.matmul(acc[j * HD:(j + 1) * HD, :], v[1][:, 0, j * HD:(j + 1) * HD], probT[:, 1, j, 0, :], start=True, stop=False)
                pe.matmul(acc_sum[j * HD:(j + 1) * HD, :], ones[:, 0:HD], pair_sum[:, 1, j, :], start=True, stop=False)
            with pe.Fori(0, TURNS) as i:
                for t in range(NB):
                    blk = i * NB + t
                    for p in range(4):
                        pair, last_p = blk * 4 + p, (p + 3) % 4
                        v_par = (t - (p == 0)) // 2 % 2
                        if p == 0 and t == 1:
                            pe.wait_ge(s_qk[1], i * (24 * 16) + 24 * 16)
                        if p == 0 and t == NB - 1:
                            pe.wait_ge(s_qk[0], i * (24 * 16) + 48 * 16)

                        def tile(n):
                            make_scores(pair + 4, t + 1, p, n)

                        make_scoresT(blk, t, p, 0)
                        tile(0)
                        make_scoresT(blk, t, p, 1)
                        tile(1)
                        pe.wait_ge(s_exp, blk * 16 + (p * 4 + 2))
                        if p == 1:
                            pe.wait_ge(s_raw, blk * 2 + 1)
                            if t % 2 == 0:
                                pe.wait_ge(s_v[t // 2], i * 16 + 16)
                        pv(v_par, last_p, 0)
                        make_max_rows(pair + 3, p)
                        make_scoresT(blk, t, p, 2)
                        tile(2)
                        make_scoresT(blk, t, p, 3)
                        tile(3)
                        pv(v_par, last_p, 1).then_inc(s_pv, 1)
                        tile(4)
                        tile(5)
                        pe.wait_ge(s_pre, blk * 16 + (p * 4 + 8))
                        if p == 1:
                            pe.wait_ge(s_raw, blk * 2 + 2)
                        sums(last_p).then_inc(s_sum, 1)
                        tile(6)
                        tile(7)
            pe.wait_ge(s_exp, TURNS * NB * 16 + 2)
            pv(1, 3, 0)
            pv(1, 3, 1).then_inc(s_pv, 1)
            pe.wait_ge(s_pre, TURNS * NB * 16 + 8)
            sums(3).then_inc(s_sum, 1)


def merge(nc, x, wo, bo, ident_in, oT_s, x1_s, xnT_s, xn_max):
    with ExitStack() as ctx:
        m = Space(nc, ctx, "p4")
        NT = 2 * CT
        w_o, ident, bias = m.sb("wo", [P, KD, D]), m.sb("ident", [P, P]), m.sb("bo", [P, D])
        oT = [m.sb(f"oT{c}", [P, G, CH]) for c in range(2)]
        xs = m.sb("x", [P, NT, D])
        xn = m.sb("xn", [P, NT, D])
        xT = m.sb("xT", [P, 2, KD, CH])
        stats, mv = m.sb("stats", [P, NT, 6]), m.sb("mv", [P, NT, 2])
        std, rstd, eps = m.sb("std", [P, NT]), m.sb("rstd", [P, NT]), m.sb("eps", [P, 1])
        high = m.sb("high", [P, NT + 1])
        acc, tr = m.ps("acc", [P, 4, D]), m.ps("tr", [P, 2, CH])

        s_w, s_x, s_oT = m.sem("weights_in"), m.sems("x_in", 2), m.sems("oT_in", 2)
        s_eps, s_var, s_std, s_rstd = m.sem("eps"), m.sem("var"), m.sem("std"), m.sem("rstd")
        s_st, s_high, s_mark = m.sem("stats"), m.sem("high"), m.sem("mark")
        s_xb = m.sem("bias_added")
        s_acc = m.sem("product")
        s_sum = m.sem("sum")
        s_tr = m.sem("transposed")
        s_xn = m.sem("xn")
        s_xt = m.sem("xT_evacuated")
        s_xs, s_xts = m.sems("x1_stored", 2), m.sems("xT_stored", 2)
        block = ctx.enter_context(nc.Block())

        @block.sync
        def _(sync):
            sync.dma_start(w_o[:, :, :], wo.rearrange("(k p) n -> p k n", p=P)).then_inc(s_w, 16)
            for dst, src in ((ident, ident_in), (bias, bo)):
                sync.dma_start(dst[:, :], src).then_inc(s_w, 16)
            with sync.Fori(0, B) as b:
                for c in range(2):
                    sync.wait_ge(s_acc, b * NT + CT * (c + 1))
                    sync.sem_inc(s_mark, 1)
                    sync.dma_start(oT[c][:, :, :], oT_s[bass.ds(b * P, P), :, c * CH:(c + 1) * CH]).then_inc(s_oT[c], 16)
                    sync.wait_ge(s_xs[c], b * 16 + 16)
                    sync.sem_inc(s_mark, 1)
                    sync.dma_start(xs[:, c * CT:(c + 1) * CT, :], x[bass.ds(b * S + c * CH, CH), :].rearrange("(t p) d -> p t d", p=P)).then_inc(s_x[c], 16)

        @block.gpsimd
        def _(pool):
            pool.wait_ge(s_w, 3 * 16)
            with pool.Fori(0, B) as b:
                for t in range(NT):
                    if t % CT == 0:
                        pool.wait_ge(s_x[t // CT], b * 16 + 16)
                    pool.tensor_tensor(xs[:, t, :], xs[:, t, :], bias[:, :], ALU.add).then_inc(s_xb, 1)

        @block.vector
        def _(dve):
            dve.memset(eps[:, :], EPS).then_inc(s_eps, 1)
            dve.memset(high[:, :], 0.0).then_inc(s_high, 1)
            dve.sem_inc(s_sum, 4)
            dve.sem_inc(s_xn, NT)
            with dve.Fori(0, B) as b:
                for t in range(NT):
                    n = b * NT + t
                    dve.wait_ge(s_xb, n + 1)
                    dve.wait_ge(s_acc, n + NT + 1)
                    dve.tensor_tensor(xs[:, t, :], acc[:, t % 4, :], xs[:, t, :], ALU.add).then_inc(s_sum, 1)
                    dve.wait_ge(s_sum, n + 5)
                    dve.bn_stats(stats[:, t, :], xs[:, t, :]).then_inc(s_st, 1)
                    dve.wait_ge(s_st, n + 1)
                    dve.sem_inc(s_mark, 1)
                    dve.bn_aggr(mv[:, t, :], stats[:, t, :]).then_inc(s_var, 1)
                    dve.wait_ge(s_std, n + 1)
                    dve.reciprocal(rstd[:, t:t + 1], std[:, t:t + 1]).then_inc(s_rstd, 1)
                    dve.wait_ge(s_rstd, n + 1)
                    dve.wait_ge(s_tr, n + 1)
                    dve.tensor_scalar(xn[:, t, :], xs[:, t, :], mv[:, t, 0:1], rstd[:, t:t + 1], ALU.subtract, ALU.mult).then_inc(s_xn, 1)
                    dve.wait_ge(s_xn, n + NT + 1)
                    if t == 0:
                        dve.wait_ge(s_high, b * (NT + 1) + 1)
                    dve.tensor_reduce(high[:, t:t + 1], xn[:, t, :], axis=AX.X, op=ALU.max, apply_absolute_value=True).then_inc(s_high, 1)
                dve.wait_ge(s_high, b * (NT + 1) + (NT + 1))
                dve.tensor_reduce(high[:, NT:NT + 1], high[:, :], axis=AX.X, op=ALU.max).then_inc(s_high, 1)
            dve.wait_ge(s_high, B * (NT + 1) + 1)
            dve.tensor_copy(xn_max[:, :], high[:, NT:NT + 1]).then_inc(s_high, 1)

        @block.scalar
        def _(act):
            act.sem_inc(s_xt, 2)
            for s_stored in (*s_xs, *s_xts):
                act.sem_inc(s_stored, 16)
            act.wait_ge(s_eps, 1)

            def square_root(b, t):
                act.wait_ge(s_var, b * NT + t + 1)
                act.activation(std[:, t:t + 1], mv[:, t, 1:2], ACT.Sqrt, bias=eps[:, 0:1]).then_inc(s_std, 1)

            with act.Fori(0, B) as b:
                square_root(b, 0)
                for t in range(NT):
                    c = t // CT
                    if t + 1 < NT:
                        square_root(b, t + 1)
                    if t % CT == 0:
                        act.wait_ge(s_xts[c], b * 16 + 16)
                    act.wait_ge(s_tr, b * NT + NT + t + 1)
                    act.activation(xT[:, c, :, (t % CT) * P:(t % CT + 1) * P], tr[:, t % 2, :], ACT.Copy).then_inc(s_xt, 1)
                    if t % CT == CT - 1:
                        act.wait_ge(s_xn, b * NT + NT + t + 1)
                        act.dma_start(x1_s[bass.ds((b * 2 + c) * P, P), :, :], xs[:, c * CT:(c + 1) * CT, :]).then_inc(s_xs[c], 16)
                        act.wait_ge(s_xt, b * NT + t + 3)
                        act.dma_start(xnT_s[bass.ds((b * 2 + c) * P, P), :, :], xT[:, c, :, :]).then_inc(s_xts[c], 16)
            for s_stored in (*s_xs, *s_xts):
                act.wait_ge(s_stored, B * 16 + 16)

        @block.tensor
        def _(pe):
            pe.sem_inc(s_acc, NT)
            pe.sem_inc(s_tr, NT)
            pe.wait_ge(s_w, 3 * 16)

            def transposes(b, t):
                pe.wait_ge(s_xn, b * NT + NT + t + 1)
                pe.wait_ge(s_xt, b * NT + t + 1)
                for k in range(KD):
                    last = pe.transpose(tr[:, t % 2, k * P:(k + 1) * P], xn[:, t, k * P:(k + 1) * P], ident[:, :])
                last.then_inc(s_tr, 1)

            with pe.Fori(0, B) as b:
                for t in range(NT):
                    if t % CT == 0:
                        pe.wait_ge(s_oT[t // CT], b * 16 + 16)
                    pe.wait_ge(s_sum, b * NT + t + 1)
                    for k in range(KD):
                        last = pe.matmul(acc[:, t % 4, :], oT[t // CT][:, k, (t % CT) * P:(t % CT + 1) * P], w_o[:, k, :],
                                         start=(k == 0), stop=(k == KD - 1))
                    last.then_inc(s_acc, 1)
                    if t > 0:
                        transposes(b, t - 1)
                transposes(b, NT - 1)


def expand(nc, b_in, ident_in, win16, win_high, xnT_s, xn_max, h_s, h_max):
    with ExitStack() as ctx:
        m = Space(nc, ctx, "p5")
        HP = 4
        NP = 2 * FT // HP
        ident, bias, alpha = m.sb("ident", [P, P]), m.sb("b_in", [P, FT]), m.sb("alpha", [P, FT])
        scale_x, tops, ones = m.sb("scale_x", [P, 3]), m.sb("tops", [1, 2]), m.sb("ones", [1, P])
        raw = m.sb("raw", [P, 2, KD, CH])
        hi, lo = (m.sb(n, [P, 2, KD, CH], F16) for n in ("hi", "lo"))
        g = m.sb("g", [P, 4, HP, CH])
        high = m.sb("high", [P, NP + 1])
        acc = m.ps("acc", [P, 8, CH])

        s_k0, s_chain, s_pe0, s_top, s_mark = m.sem("constants_in"), m.sem("chain"), m.sem("max_products"), m.sem("max_steps"), m.sem("mark")
        s_x, s_r, s_q, s_hi, s_high, s_scale = m.sems("x_in", 2), m.sem("rounding"), m.sem("x_integers"), m.sem("x_hi"), m.sem("high"), m.sem("scales")
        s_lo = m.sem("x_lo")
        s_acc = m.sem("product")
        s_g = m.sem("gelu")
        s_read = m.sem("g_read")
        s_gs = m.sems("g_stored", 4)
        block = ctx.enter_context(nc.Block())

        @block.sync
        def _(sync):
            for dst, src in ((ident, ident_in), (bias, b_in)):
                sync.dma_start(dst[:, :], src).then_inc(s_k0, 16)

            def load(n, c):
                sync.wait_ge(s_lo, n + 1)
                sync.sem_inc(s_mark, 1)
                sync.dma_start(raw[:, c, :, :], xnT_s[bass.ds(n % NCH * P, P), :, :]).then_inc(s_x[c], 16)

            load(0, 0)
            with sync.Fori(0, NCH // 2) as i:
                load(i * 2 + 1, 1)
                for p in range(NP):
                    if p == 2:
                        load(i * 2 + 2, 0)
                    sync.wait_ge(s_g, i * (2 * FT) + (HP * (p + 1) + 8))
                    sync.sem_inc(s_mark, 1)
                    sync.dma_start(h_s[bass.ds((i * 2 + p // 4) * P, P), (p % 4) * HP:(p % 4 + 1) * HP, :], g[:, p % 4, :, :]).then_inc(s_gs[p % 4], 16)
            for s_stored in s_gs:
                sync.wait_ge(s_stored, NCH * 16 + 16)
            sync.wait_ge(s_x[0], (NCH // 2 + 1) * 16)

        @block.gpsimd
        def _(pool):
            pool.memset(ones[:, :], 1.0).then_inc(s_scale, 1)
            pool.sem_inc(s_lo, 2)

            def second_part(n, c):
                pool.wait_ge(s_acc, n * FT + FT)
                pool.wait_ge(s_hi, n + 1)
                pool.tensor_tensor(lo[:, c, :, :], raw[:, c, :, :], hi[:, c, :, :], ALU.subtract).then_inc(s_lo, 1)

            second_part(0, 0)
            with pool.Fori(0, NCH // 2) as i:
                second_part(i * 2 + 1, 1)
                second_part(i * 2 + 2, 0)

        @block.vector
        def _(dve):
            steps = [0]

            def link(ins):
                steps[0] += 1
                ins.then_inc(s_chain, 1)
                dve.wait_ge(s_chain, steps[0])

            dve.sem_inc(s_read, 4)
            dve.memset(high[:, :], 0.0).then_inc(s_high, 1)
            dve.wait_ge(s_k0, 2 * 16)
            spread_max(dve, "dve", xn_max[:, :], 1, tops, acc[:, 0, :], ident, ones, s_pe0, s_top)
            link(dve.tensor_scalar(scale_x[:, 0:1], acc[:, 0, P:P + 1], 1e-8, None, ALU.max))
            link(dve.reciprocal(scale_x[:, 1:2], scale_x[:, 0:1]))
            link(dve.tensor_scalar(scale_x[:, 2:3], scale_x[:, 1:2], 32767.0, None, ALU.mult))
            dve.tensor_scalar(alpha[:, :], win_high[:, :], scale_x[:, 0:1], 1 / (127.0 * 32767.0), ALU.mult, ALU.mult).then_inc(s_scale, 1)

            def integers(n, c):
                x = raw[:, c, :, :]
                dve.tensor_scalar(x, x, scale_x[:, 2:3], 32767.0, ALU.mult, ALU.min).then_inc(s_r, 1)
                dve.wait_ge(s_r, n * 2 + 1)
                dve.tensor_scalar(x, x, -32768.0, ROUND, ALU.max, ALU.add).then_inc(s_r, 1)
                dve.wait_ge(s_r, n * 2 + 2)
                dve.tensor_scalar(x, x, ROUND, None, ALU.subtract).then_inc(s_q, 1)

            dve.wait_ge(s_x[0], 16)
            integers(0, 0)
            with dve.Fori(0, NCH // 2) as i:
                for p in range(NP):
                    if p in (1, 5):
                        c = 1 if p == 1 else 0
                        n = i * 2 + 2 - c
                        dve.wait_ge(s_x[c], (i + 2 - c) * 16)
                        integers(n, c)
                    dve.wait_ge(s_g, i * (2 * FT) + (HP * (p + 1) + 8))
                    if p == 0:
                        dve.wait_ge(s_high, i * (NP + 1) + 1)
                    dve.tensor_reduce(high[:, p:p + 1], g[:, p % 4, :, :], axis=AX.XY, op=ALU.max,
                                      apply_absolute_value=True).then_inc(s_read, 1)
                dve.wait_ge(s_read, i * NP + (NP + 4))
                dve.tensor_reduce(high[:, NP:NP + 1], high[:, :], axis=AX.X, op=ALU.max).then_inc(s_high, NP + 1)
            dve.wait_ge(s_high, NCH // 2 * (NP + 1) + 1)
            dve.tensor_copy(h_max[:, :], high[:, NP:NP + 1]).then_inc(s_high, 1)

        @block.scalar
        def _(act):
            act.sem_inc(s_g, 8)
            for s_stored in s_gs:
                act.sem_inc(s_stored, 16)

            def first_part(n, c):
                act.wait_ge(s_acc, n * FT + FT)
                act.wait_ge(s_q, n + 1)
                act.activation(hi[:, c, :, :], raw[:, c, :, :], ACT.Copy).then_inc(s_hi, 1)

            first_part(0, 0)
            act.wait_ge(s_scale, 2)
            with act.Fori(0, NCH // 2) as i:
                for o in range(2 * FT):
                    f, p = o % FT, o // HP
                    if o == 6:
                        first_part(i * 2 + 1, 1)
                    if o == FT + 6:
                        first_part(i * 2 + 2, 0)
                    if o % HP == 0:
                        act.wait_ge(s_gs[p % 4], (i * 2 + p // 4) * 16 + 16)
                        act.wait_ge(s_read, i * NP + p + 1)
                    act.wait_ge(s_acc, i * (2 * FT) + (2 * FT + o + 1))
                    act.activation(g[:, p % 4, o % HP, :], acc[:, o % 8, :], ACT.Gelu, bias=bias[:, f:f + 1],
                                   scale=alpha[:, f:f + 1]).then_inc(s_g, 1)

        @block.tensor
        def _(pe):
            pe.sem_inc(s_acc, 2 * FT)
            pe.wait_ge(s_k0, 2 * 16)
            pe.wait_ge(s_scale, 1)
            spread_max(pe, "pe", xn_max[:, :], 1, tops, acc[:, 0, :], ident, ones, s_pe0, s_top)
            pe.wait_ge(s_chain, 1)
            with pe.Fori(0, NCH // 2) as i:
                for o in range(2 * FT):
                    c, f = o // FT, o % FT
                    if f == 0:
                        pe.wait_ge(s_lo, i * 2 + c + 3)
                    pe.wait_ge(s_g, i * (2 * FT) + o + 1)
                    for k in range(KD):
                        for part in (hi, lo):
                            last = pe.matmul(acc[:, o % 8, :], win16[:, k, f * P:(f + 1) * P], part[:, c, k, :],
                                             start=(k == 0 and part is hi), stop=(k == KD - 1 and part is lo))
                    last.then_inc(s_acc, 1)


def contract(nc, b_out, ident_in, wout16, wout_high, h_s, h_max, x1_s, out):
    with ExitStack() as ctx:
        m = Space(nc, ctx, "p6")
        HP = 4
        NP = FT // HP
        ident, bias = m.sb("ident", [P, P]), m.sb("b_out", [P, D])
        rel = m.sb("rel", [P, FT])
        both, tops, ones, sc = m.sb("both", [P, 2]), m.sb("tops", [2, 3]), m.sb("ones", [2, P]), m.sb("sc", [P, 4])
        h = m.sb("h", [P, 8, HP, CH])
        hi, lo = (m.sb(n, [P, 4, HP, CH], F16) for n in ("hi", "lo"))
        x1, y = m.sb("x1", [P, 2, CT, D]), m.sb("y", [P, CT, D])
        acc = m.ps("acc", [P, 8, D])

        s_c, s_chain, s_pe0, s_top = m.sem("constants_in"), m.sem("chain"), m.sem("max_products"), m.sem("max_steps")
        s_ones, s_mark = m.sem("ones"), m.sem("mark")
        s_h = m.sems("h_in", 8)
        s_x = m.sems("x1_in", 2)
        s_ab, s_u, s_hi, s_xb = m.sem("rounding"), m.sem("scaled"), m.sem("h_hi"), m.sem("bias_added")
        s_lo = m.sem("h_lo")
        s_mm = m.sem("piece_product")
        s_y = m.sem("y")
        s_ys = m.sem("y_stored")
        block = ctx.enter_context(nc.Block())

        @block.sync
        def _(sync):
            for dst, src in ((ident, ident_in), (bias, b_out)):
                sync.dma_start(dst[:, :], src).then_inc(s_c, 16)

            def load(n, c):
                for p in range(NP):
                    slot = c * NP + p
                    sync.wait_ge(s_lo, n * NP + p + 1)
                    sync.sem_inc(s_mark, 1)
                    sync.dma_start(h[:, slot, :, :], h_s[bass.ds(n % NCH * P, P), p * HP:(p + 1) * HP, :]).then_inc(s_h[slot], 16)

            load(0, 0)
            with sync.Fori(0, NCH // 2) as i:
                for c in range(2):
                    n = i * 2 + c
                    sync.wait_ge(s_y, n * CT + CT)
                    sync.sem_inc(s_mark, 1)
                    sync.dma_start(x1[:, c, :, :], x1_s[bass.ds(n * P, P), :, :]).then_inc(s_x[c], 16)
                    load(n + 1, 1 - c)

        @block.gpsimd
        def _(pool):
            pool.memset(ones[:, :], 1.0).then_inc(s_ones, 1)
            pool.sem_inc(s_lo, 8)
            pool.wait_ge(s_c, 2 * 16)

            def low_parts(n, c):
                for p in range(NP):
                    pool.wait_ge(s_hi, n * NP + p + 1)
                    pool.wait_ge(s_mm, n * NP + p + 1)
                    pool.tensor_tensor(lo[:, p, :, :], h[:, c * NP + p, :, :], hi[:, p, :, :], ALU.subtract).then_inc(s_lo, 1)

            low_parts(0, 0)
            with pool.Fori(0, NCH // 2) as i:
                for c in range(2):
                    low_parts(i * 2 + (c + 1), 1 - c)
                    pool.wait_ge(s_x[c], i * 16 + 16)
                    for t in range(CT):
                        pool.tensor_tensor(x1[:, c, t, :], x1[:, c, t, :], bias[:, :], ALU.add).then_inc(s_xb, 1)

        @block.vector
        def _(dve):
            steps = [0]

            def link(ins):
                steps[0] += 1
                ins.then_inc(s_chain, 1)
                dve.wait_ge(s_chain, steps[0])

            dve.sem_inc(s_y, 2 * CT)
            link(dve.tensor_reduce(both[:, 0:1], wout_high[:, :], axis=AX.X, op=ALU.max))
            dve.tensor_scalar(both[:, 1:2], h_max[:, :], 1e-8, None, ALU.max).then_inc(s_ones, 1)
            dve.wait_ge(s_ones, 2)
            spread_max(dve, "dve", both[:, :], 2, tops, acc[:, 0, :], ident, ones, s_pe0, s_top)
            link(dve.tensor_copy(sc[:, 0:2], acc[:, 0, P:P + 2]))
            link(dve.reciprocal(sc[:, 2:4], sc[:, 0:2]))
            link(dve.tensor_scalar(rel[:, :], wout_high[:, :], sc[:, 2:3], None, ALU.mult))
            link(dve.tensor_scalar(sc[:, 3:4], sc[:, 3:4], 32767.0, None, ALU.mult))
            link(dve.tensor_scalar(sc[:, 2:3], sc[:, 0:1], sc[:, 1:2], 1 / (127.0 * 32767.0), ALU.mult, ALU.mult))

            def integers(chunk, c, turn):
                for p in range(NP):
                    slot = c * NP + p
                    n = chunk * NP + p
                    v = h[:, slot, :, :]
                    dve.wait_ge(s_h[slot], turn * 16 + 16)
                    dve.tensor_scalar(v, v, sc[:, 3:4], 32767.0, ALU.mult, ALU.min).then_inc(s_ab, 1)
                    dve.wait_ge(s_ab, n * 2 + 1)
                    dve.tensor_scalar(v, v, -32768.0, ROUND, ALU.max, ALU.add).then_inc(s_ab, 1)
                    dve.wait_ge(s_ab, n * 2 + 2)
                    for f in range(HP):
                        dve.tensor_scalar(h[:, slot, f, :], h[:, slot, f, :], ROUND, rel[:, p * HP + f:p * HP + f + 1],
                                          ALU.subtract, ALU.mult).then_inc(s_u, 1)

            integers(0, 0, 0)
            with dve.Fori(0, NCH // 2) as i:
                for c in range(2):
                    integers(i * 2 + (c + 1), 1 - c, i + c)
                    dve.wait_ge(s_mm, (i * 2 + c) * NP + (NP + 4))
                    dve.wait_ge(s_xb, (i * 2 + c) * CT + CT)
                    dve.wait_ge(s_ys, (i * 2 + c) * 16 + 16)
                    for t in range(CT):
                        dve.scalar_tensor_tensor(y[:, t, :], acc[:, c * 4 + t, :], sc[:, 2:3], x1[:, c, t, :], ALU.mult, ALU.add).then_inc(s_y, 1)

        @block.scalar
        def _(act):
            act.sem_inc(s_ys, 16)

            def high_parts(chunk, c):
                for p in range(NP):
                    n = chunk * NP + p
                    act.wait_ge(s_u, n * HP + HP)
                    act.wait_ge(s_mm, n + 1)
                    act.activation(hi[:, p, :, :], h[:, c * NP + p, :, :], ACT.Copy).then_inc(s_hi, 1)

            high_parts(0, 0)
            with act.Fori(0, NCH // 2) as i:
                for c in range(2):
                    high_parts(i * 2 + (c + 1), 1 - c)
                    act.wait_ge(s_y, (i * 2 + c) * CT + (3 * CT))
                    act.dma_start(out[bass.ds((i * 2 + c) * CH, CH), :].rearrange("(t p) d -> p t d", p=P), y[:, :, :]).then_inc(s_ys, 16)
            act.wait_ge(s_ys, NCH * 16 + 16)

        @block.tensor
        def _(pe):
            pe.sem_inc(s_mm, 4)
            pe.wait_ge(s_c, 2 * 16)
            pe.wait_ge(s_ones, 2)
            spread_max(pe, "pe", both[:, :], 2, tops, acc[:, 0, :], ident, ones, s_pe0, s_top)
            pe.wait_ge(s_chain, 2)
            with pe.Fori(0, NCH // 2) as i:
                for c in range(2):
                    pe.wait_ge(s_y, (i * 2 + c) * CT + CT)
                    for p in range(NP):
                        pe.wait_ge(s_lo, i * 8 + (c * NP + p) + 9)
                        for f in range(HP):
                            for part in (hi, lo):
                                for t in range(CT):
                                    last = pe.matmul(acc[:, c * 4 + t, :], part[:, p, f, t * P:(t + 1) * P], wout16[:, p * HP + f, :],
                                                     start=(p == 0 and f == 0 and part is hi),
                                                     stop=(p == NP - 1 and f == HP - 1 and part is lo))
                        last.then_inc(s_mm, 1)


def constants(np):
    left = np.arange(1024, 2048) / 1024
    right = (math.log(2.0) / left).astype(np.float16)
    best = np.argmin(np.abs(left * right.astype(np.float64) - math.log(2.0)))
    left, right = np.float16(left[best]), right[best]
    key, tile = np.arange(S)[None, :], np.arange(KT)[:, None]
    below = key < P * tile
    within = key // P == tile
    tri = np.arange(P)[:, None] <= np.arange(P)[None, :]
    zero = np.float16(0)
    return {
        "step_q": np.repeat(np.where(within, left, zero)[:, None, :], 4, axis=1),
        "step_k": np.repeat(np.concatenate([np.full((2, S), MAX_ROW, np.float16), np.where(below, right, zero)])[:, None, :], 4, axis=1),
        "tri": np.where(tri, left, zero),
        "diag16": np.where(np.eye(P, dtype=bool), right, zero),
        "ident": np.eye(P, dtype=np.float32),
        "ident16": np.eye(P, dtype=np.float16),
    }



def build(nc, a, out):
    def dram(name, shape, dt=F32):
        return nc.dram_tensor(name, shape, dt, kind="Internal").ap()

    qT_s, kT_s, oT_s = (dram(n, [B * P, G, S]) for n in ("qT_s", "kT_s", "oT_s"))
    v_s = dram("v_s", [B * P, KT, D])
    x1_s = dram("x1_s", [NCH * P, CT, D])
    xnT_s = dram("xnT_s", [NCH * P, KD, CH])
    h_s = dram("h_s", [NCH * P, FT, CH])
    with ExitStack() as ctx:
        m = Space(nc, ctx, "all")
        qk_max, xn_max, h_max = m.sb("qk_max", [P, 2]), m.sb("xn_max", [P, 1]), m.sb("h_max", [P, 1])
        win16, win_high = m.sb("win16", [P, KD, F], F16), m.sb("win_high", [P, FT])
        wout16, wout_high = m.sb("wout16", [P, FT, D], F16), m.sb("wout_high", [P, FT])
        with ExitStack() as ctx_qkv:
            m = Space(nc, ctx_qkv, "qkv")
            w_hi, w_lo = m.sb("w_hi", [P, 3, KD, D], F16), m.sb("w_lo", [P, 3, KD, D], F16)
            w_inv, ctx_max = m.sb("w_inv", [P, 3]), m.sb("ctx_max", [P, 1])
            project_queries(nc, a["x"], a["ctxT"], a["wq"], a["wk"], a["wv"], a["bq"], a["ident"], qT_s,
                            w_hi, w_lo, w_inv, qk_max[:, 1:2], ctx_max)
            project_context(nc, a["ctxT"], a["bk"], a["bv"], a["w_inT"], a["w_out"], a["ident"], a["ident16"], kT_s, v_s,
                            w_hi, w_lo, w_inv, ctx_max, qk_max[:, 0:1], win16, win_high, wout16, wout_high)
        attend(nc, qT_s, kT_s, v_s, qk_max, a["ident"], a["ident16"], a["diag16"], a["tri"], a["step_q"], a["step_k"], oT_s)
        merge(nc, a["x"], a["wo"], a["bo"], a["ident"], oT_s, x1_s, xnT_s, xn_max)
        expand(nc, a["b_in"], a["ident"], win16, win_high, xnT_s, xn_max, h_s, h_max)
        contract(nc, a["b_out"], a["ident"], wout16, wout_high, h_s, h_max, x1_s, out)


def kernel(x, ctx_1024, L0_xattn_Wq, L0_xattn_bq, L0_xattn_Wk, L0_xattn_bk, L0_xattn_Wv, L0_xattn_bv,
           L0_xattn_Wo, L0_xattn_bo, L0_ffn_W_in, L0_ffn_b_in, L0_ffn_W_out, L0_ffn_b_out):
    import numpy as np
    import concourse.bacc as bacc
    from concourse.bass_utils import run_bass_kernel_spmd

    def rows(v):
        return np.ascontiguousarray(np.broadcast_to(np.asarray(v)[None, :], (P, len(v))))

    def cols(v):
        return np.ascontiguousarray(np.asarray(v).reshape(-1, P).T)

    arrays = {
        "x": np.ascontiguousarray(np.asarray(x).reshape(B * S, D)),
        "ctxT": np.ascontiguousarray(np.asarray(ctx_1024).reshape(B * S, D).T),
        "wq": np.asarray(L0_xattn_Wq), "wk": np.asarray(L0_xattn_Wk), "wv": np.asarray(L0_xattn_Wv), "wo": np.asarray(L0_xattn_Wo),
        "bq": cols(L0_xattn_bq), "bk": cols(L0_xattn_bk), "bv": rows(L0_xattn_bv), "bo": rows(L0_xattn_bo),
        "w_inT": np.ascontiguousarray(np.asarray(L0_ffn_W_in).T), "b_in": cols(L0_ffn_b_in),
        "w_out": np.asarray(L0_ffn_W_out), "b_out": rows(L0_ffn_b_out),
        **constants(np),
    }
    nc = bacc.Bacc("TRN2", target_bir_lowering=False, num_devices=1)
    a = {n: nc.dram_tensor(n, v.shape, mybir.dt.from_np(v.dtype), kind="ExternalInput").ap() for n, v in arrays.items()}
    out = nc.dram_tensor("out", (B * S, D), F32, kind="ExternalOutput").ap()
    build(nc, a, out)
    r = run_bass_kernel_spmd(nc, [arrays], core_ids=[0])
    return r.results[0]["out"].reshape(B, S, D)
```

```python
import math
from contextlib import ExitStack

import concourse.bass as bass
from concourse import mybir

F32 = mybir.dt.float32
F16 = mybir.dt.float16
I32 = mybir.dt.int32
ALU = mybir.AluOpType
ACT = mybir.ActivationFunctionType
AX = mybir.AxisListType

P = 128
B, S, D, F = 8, 1024, 512, 2048
H, HD = 16, 32
KD = D // P
FT = F // P
KT = S // P
G = H // 4
CH = 512
CT = CH // P
NCH = B * S // CH
EPS = 1e-5
ROUND = 1.5 * 2.0 ** 23
MAX_ROW = 2.0 ** 15
QK_ROWS = 3 * HD + 2 + KT
LN_SCALE = 2.0 ** 11


class Space:

    def __init__(self, nc, ctx, tag):
        self.nc, self.ctx, self.tag = nc, ctx, tag

    def sb(self, name, shape, dt=F32):
        return self.ctx.enter_context(self.nc.sbuf_tensor(f"{self.tag}_{name}", shape, dt))

    def ps(self, name, shape):
        return self.ctx.enter_context(self.nc.psum_tensor(f"{self.tag}_{name}", shape, F32))

    def sem(self, name):
        return self.ctx.enter_context(self.nc.semaphore(f"{self.tag}_{name}"))

    def sems(self, name, n):
        return [self.sem(f"{name}{i}") for i in range(n)]


def spread_max(eng, stage, src, n, tile, bank, ident, ones, sem_pe, sem_dve):
    top, diag = tile[0:n, 0:1], tile[0:n, 1:1 + n]
    if stage == "pe":
        eng.transpose(bank[0:n, 0:P], src, ident[:, :]).then_inc(sem_pe, 1)
        eng.wait_ge(sem_dve, 2)
        eng.matmul(bank[:, P:P + n], ones[0:n, :], diag, start=True, stop=True).then_inc(sem_pe, 1)
    else:
        eng.wait_ge(sem_pe, 1)
        eng.tensor_reduce(top, bank[0:n, 0:P], axis=AX.X, op=ALU.max).then_inc(sem_dve, 1)
        eng.wait_ge(sem_dve, 1)
        eng.tensor_scalar(diag, ident[0:n, 0:n], top, None, ALU.mult).then_inc(sem_dve, 1)
        eng.wait_ge(sem_pe, 2)


def flat(tiles):
    return tiles.rearrange("p k t -> p (k t)")


def power_scales(dve, link, scale, inverse, top):
    bits, inv = scale.bitcast(I32), inverse.bitcast(I32)
    link(dve.tensor_scalar(scale, top, 1e-30, 1e30, ALU.max, ALU.min))
    link(dve.tensor_scalar(bits, bits, 23, 23, ALU.logical_shift_right, ALU.logical_shift_left))
    link(dve.tensor_scalar(inv, bits, -(11 << 23), None, ALU.add))
    link(dve.tensor_scalar(bits, inv, -1, 254 << 23, ALU.mult, ALU.add))


def project_queries(nc, s_mark, x, ctxT, wq, wk, wv, wo, bq, ident_in, qT_s, w_hi, w_lo, wo_hi, wo_lo, w_inv, q_max, ctx_max):
    with ExitStack() as ctx:
        m = Space(nc, ctx, "p1")
        w32 = m.sb("w", [P, 4, KD, D])
        highs = [w_hi[:, o, :, :] for o in range(3)] + [wo_hi[:, :, :]]
        lows = [w_lo[:, o, :, :] for o in range(3)] + [wo_lo[:, :, :]]
        ident, bias, ones = m.sb("ident", [P, P]), m.sb("bq", [P, G]), m.sb("ones", [4, P])
        xn = m.sb("x", [P, 2, CT, D])
        cx = m.sb("ctx", [P, 2, KD, CH])
        hi, lo = (m.sb(n, [P, 2, KD, CH], F16) for n in ("hi", "lo"))
        qo = m.sb("qo", [P, 2, G, CH])
        stats, mv = m.sb("stats", [P, CT, 6]), m.sb("mv", [P, CT, 2])
        std, rstd, shift, eps = m.sb("std", [P, CT]), m.sb("rstd", [P, CT]), m.sb("shift", [P, CT]), m.sb("eps", [P, 1])
        factor = m.sb("factor", [P, 1])
        tops, w_top, w_scale = m.sb("tops", [4, 5]), m.sb("w_top", [P, 4]), m.sb("w_scale", [P, 4])
        high = m.sb("high", [P, 4])
        tr, acc = m.ps("tr", [P, KD, CH]), m.ps("acc", [P, G, CH])

        s_w, s_chain, s_pe0, s_top, s_parts = m.sem("weights_in"), m.sem("chain"), m.sem("max_products"), m.sem("max_steps"), m.sem("w_low_parts")
        s_wh = m.sem("w_high_parts")
        s_x, s_c, s_k0 = m.sems("x_in", 2), m.sems("ctx_in", 2), m.sem("constants_in")
        s_st, s_var, s_std, s_rstd = (m.sem(n) for n in ("stats", "var", "std", "rstd"))
        s_init, s_hi, s_scale = m.sem("initial_values"), m.sem("hi"), m.sem("w_scales")
        s_tr = m.sem("transposed")
        s_lo = m.sem("lo")
        s_acc = m.sem("q_product")
        s_q = m.sem("q_evacuated")
        s_cmax = m.sem("ctx_read")
        s_qmax = m.sem("q_read")
        s_high = m.sem("high")
        s_shift = m.sem("shift")
        s_xn = m.sem("xn")
        s_qs = m.sems("q_stored", 2)
        block = ctx.enter_context(nc.Block())

        @block.sync
        def _(sync):
            def load_x(n, c):
                sync.wait_ge(s_tr, n * KD + KD)
                sync.sem_inc(s_mark, 1)
                sync.dma_start(xn[:, c, :, :], x[bass.ds(n % NCH * CH, CH), :].rearrange("(t p) d -> p t d", p=P)).then_inc(s_x[c], 16)

            load_x(0, 0)
            for dst, src in ((ident, ident_in), (bias, bq)):
                sync.dma_start(dst[:, :], src).then_inc(s_k0, 16)
            for o, src in enumerate((wq, wk, wv, wo)):
                sync.dma_start(w32[:, o, :, :], src.rearrange("(k p) n -> p k n", p=P)).then_inc(s_w, 16)
            load_x(1, 1)
            with sync.Fori(0, NCH // 2) as i:
                for c in range(2):
                    n = i * 2 + c
                    sync.wait_ge(s_cmax, n + 1)
                    sync.dma_start(cx[:, c, :, :], ctxT.rearrange("(k p) t -> p k t", p=P)[:, :, bass.ds(n * CH, CH)]).then_inc(s_c[c], 16)
                    load_x(n + 2, c)
            for c in range(2):
                sync.wait_ge(s_x[c], (NCH // 2 + 1) * 16)

        @block.gpsimd
        def _(pool):
            pool.memset(eps[:, :], EPS).then_inc(s_init, 1)
            pool.memset(ones[:, :], 1.0).then_inc(s_init, 1)
            pool.memset(high[:, :], 0.0).then_inc(s_init, 1)
            pool.memset(qo[:, 1, :, :], 0.0).then_inc(s_init, 1)

        @block.vector
        def _(dve):
            steps = [0]

            def link(ins):
                steps[0] += 1
                ins.then_inc(s_chain, 1)
                dve.wait_ge(s_chain, steps[0])

            def layernorm(n, c):
                dve.wait_ge(s_x[c], (n - c) * 8 + 16)
                for t in range(CT):
                    dve.bn_stats(stats[:, t, :], xn[:, c, t, :]).then_inc(s_st, 1)
                dve.wait_ge(s_st, n * CT + CT)
                dve.wait_ge(s_shift, n + 1)
                dve.sem_inc(s_mark, 1)
                for t in range(CT):
                    dve.bn_aggr(mv[:, t, :], stats[:, t, :]).then_inc(s_var, 1)
                dve.wait_ge(s_std, n + 1)
                dve.wait_ge(s_xn, n * CT + CT)
                dve.reciprocal(rstd[:, :], std[:, :]).then_inc(s_rstd, 1)
                dve.wait_ge(s_rstd, n + 1)
                dve.scalar_tensor_tensor(shift[:, :], mv[:, :, 0], -1.0, rstd[:, :], ALU.mult, ALU.mult).then_inc(s_shift, 1)

            def low_parts(n, c):
                dve.wait_ge(s_acc, n * G + G)
                for k in range(KD):
                    dve.wait_ge(s_hi, n * KD + k + 1)
                    dve.scalar_tensor_tensor(lo[:, c, k, :], tr[:, k, :], LN_SCALE, hi[:, c, k, :], ALU.mult, ALU.subtract).then_inc(s_lo, 1)

            def low_weights(o):
                dve.wait_ge(s_wh, o + 1)
                dve.scalar_tensor_tensor(flat(lows[o]), flat(w32[:, o, :, :]), w_scale[:, o:o + 1], flat(highs[o]),
                                         ALU.mult, ALU.subtract).then_inc(s_parts, 1)

            dve.sem_inc(s_lo, KD)
            dve.sem_inc(s_cmax, 2)
            dve.sem_inc(s_qmax, 1)
            dve.sem_inc(s_high, 1)
            dve.sem_inc(s_shift, 1)
            dve.wait_ge(s_init, 4)
            layernorm(0, 0)
            dve.wait_ge(s_w, 4 * 16)
            for o in range(4):
                link(dve.tensor_reduce(w_top[:, o:o + 1], w32[:, o, :, :], axis=AX.XY, op=ALU.max, apply_absolute_value=True))
            spread_max(dve, "dve", w_top[:, :], 4, tops, acc[:, 0, :], ident, ones, s_pe0, s_top)
            power_scales(dve, link, w_scale[:, :], w_inv[:, :], acc[:, 0, P:P + 4])
            dve.tensor_scalar(factor[:, :], w_inv[:, 0:1], 1 / LN_SCALE, None, ALU.mult).then_inc(s_scale, 1)
            low_weights(0)
            low_parts(0, 0)
            layernorm(1, 1)
            low_weights(1)
            low_weights(2)
            low_weights(3)
            with dve.Fori(0, NCH // 2) as i:
                for c in range(2):
                    n = i * 2 + c
                    low_parts(n + 1, 1 - c)
                    layernorm(n + 2, c)
                    dve.wait_ge(s_c[c], i * 16 + 16)
                    dve.wait_ge(s_high, n + 1)
                    dve.tensor_reduce(high[:, 1:2], cx[:, c, :, :], axis=AX.XY, op=ALU.max, apply_absolute_value=True).then_inc(s_cmax, 1)
                    dve.wait_ge(s_q, n * G + G)
                    dve.tensor_reduce(high[:, 0:1], qo[:, 1 - c, :, :], axis=AX.XY, op=ALU.max, apply_absolute_value=True).then_inc(s_qmax, 1)
                    dve.wait_ge(s_cmax, n + 3)
                    dve.wait_ge(s_qmax, n + 2)
                    dve.tensor_tensor(high[:, 2:4], high[:, 2:4], high[:, 0:2], ALU.max).then_inc(s_high, 1)
            dve.wait_ge(s_q, NCH * G + G)
            dve.wait_ge(s_high, NCH + 1)
            link(dve.tensor_reduce(high[:, 0:1], qo[:, 1, :, :], axis=AX.XY, op=ALU.max, apply_absolute_value=True))
            dve.tensor_tensor(q_max[:, :], high[:, 2:3], high[:, 0:1], ALU.max).then_inc(s_high, 1)
            dve.tensor_copy(ctx_max[:, :], high[:, 3:4]).then_inc(s_high, 1)

        @block.scalar
        def _(act):
            act.sem_inc(s_q, G)
            for s_stored in s_qs:
                act.sem_inc(s_stored, 16)
            act.sem_inc(s_xn, CT)
            act.wait_ge(s_init, 4)

            def layernorm(n, c):
                act.wait_ge(s_var, n * CT + CT)
                act.activation(std[:, :], mv[:, :, 1], ACT.Sqrt, bias=eps[:, 0:1]).then_inc(s_std, 1)
                act.wait_ge(s_shift, n + 2)
                for t in range(CT):
                    act.activation(xn[:, c, t, :], xn[:, c, t, :], ACT.Identity, bias=shift[:, t:t + 1],
                                   scale=rstd[:, t:t + 1]).then_inc(s_xn, 1)

            def high_parts(n, c):
                act.wait_ge(s_acc, n * G + G)
                for k in range(KD):
                    act.wait_ge(s_tr, n * KD + (2 * KD + k + 1))
                    act.activation(hi[:, c, k, :], tr[:, k, :], ACT.Copy, scale=LN_SCALE).then_inc(s_hi, 1)

            def high_weights(o):
                act.activation(highs[o], w32[:, o, :, :], ACT.Identity, scale=w_scale[:, o:o + 1]).then_inc(s_wh, 1)

            layernorm(0, 0)
            act.wait_ge(s_k0, 2 * 16)
            act.wait_ge(s_scale, 1)
            high_weights(0)
            high_parts(0, 0)
            layernorm(1, 1)
            high_weights(1)
            high_weights(2)
            high_weights(3)
            with act.Fori(0, NCH // 2) as i:
                for c in range(2):
                    n = i * 2 + c
                    high_parts(n + 1, 1 - c)
                    layernorm(n + 2, c)
                    act.wait_ge(s_qs[c], i * 16 + 16)
                    act.wait_ge(s_qmax, n + 1)
                    for g in range(G):
                        act.wait_ge(s_acc, n * G + (2 * G + g + 1))
                        act.activation(qo[:, c, g, :], acc[:, g, :], ACT.Identity, bias=bias[:, g:g + 1], scale=factor[:, 0:1]).then_inc(s_q, 1)
                    act.wait_ge(s_q, n * G + 2 * G)
                    act.dma_start(qT_s[bass.ds(i * P, P), :, c * CH:(c + 1) * CH], qo[:, c, :, :]).then_inc(s_qs[c], 16)
            for s_stored in s_qs:
                act.wait_ge(s_stored, (NCH // 2 + 1) * 16)

        @block.tensor
        def _(pe):
            pe.sem_inc(s_tr, 2 * KD)
            pe.sem_inc(s_acc, 2 * G)
            pe.wait_ge(s_k0, 2 * 16)
            pe.wait_ge(s_init, 4)

            def transposes(n, c):
                pe.wait_ge(s_xn, n * CT + 2 * CT)
                for k in range(KD):
                    pe.wait_ge(s_lo, n * KD + k + 1)
                    for t in range(CT):
                        last = pe.transpose(tr[:, k, t * P:(t + 1) * P], xn[:, c, t, k * P:(k + 1) * P], ident[:, :])
                    last.then_inc(s_tr, 1)

            transposes(0, 0)
            pe.wait_ge(s_chain, 4)
            spread_max(pe, "pe", w_top[:, :], 4, tops, acc[:, 0, :], ident, ones, s_pe0, s_top)
            pe.wait_ge(s_chain, 5)
            pe.wait_ge(s_parts, 1)
            with pe.Fori(0, NCH // 2) as i:
                for c in range(2):
                    n = i * 2 + c
                    transposes(n + 1, 1 - c)
                    pe.wait_ge(s_lo, n * KD + 2 * KD)
                    for g in range(G):
                        pe.wait_ge(s_q, n * G + g + 1)
                        three_products(pe, acc[:, g, :], lambda part, k: part[:, 0, k, g * P:(g + 1) * P],
                                       lambda part, k: part[:, c, k, :], (w_hi, w_lo), (hi, lo)).then_inc(s_acc, 1)


def three_products(pe, bank, stationary, moving, left, right):
    pairs = ((left[0], right[0]), (left[0], right[1]), (left[1], right[0]))
    for k in range(KD):
        for n, (a, b) in enumerate(pairs):
            last = pe.matmul(bank, stationary(a, k), moving(b, k), start=(k == 0 and n == 0), stop=(k == KD - 1 and n == 2))
    return last


def quantise_tile(dve, w, out, high, top, scale, sem_step, first, sem_done):
    dve.tensor_reduce(top, w, axis=AX.X, op=ALU.max, apply_absolute_value=True).then_inc(sem_step, 1)
    dve.wait_ge(sem_step, first + 1)
    dve.tensor_scalar(top, top, 1e-8, None, ALU.max).then_inc(sem_step, 1)
    dve.wait_ge(sem_step, first + 2)
    dve.reciprocal(scale, top).then_inc(sem_step, 1)
    dve.tensor_scalar(high, top, 1e-8, None, ALU.max).then_inc(sem_step, 1)
    dve.wait_ge(sem_step, first + 4)
    dve.tensor_scalar(scale, scale, 127.0, None, ALU.mult).then_inc(sem_step, 1)
    dve.wait_ge(sem_step, first + 5)
    dve.tensor_scalar(w, w, scale, 127.0, ALU.mult, ALU.min).then_inc(sem_step, 1)
    dve.wait_ge(sem_step, first + 6)
    dve.tensor_scalar(w, w, -128.0, ROUND, ALU.max, ALU.add).then_inc(sem_step, 1)
    dve.wait_ge(sem_step, first + 7)
    dve.tensor_scalar(out, w, ROUND, None, ALU.subtract).then_inc(sem_done, 1)


def project_context(nc, s_mark, ctxT, bk, bv, w_inT, w_out, ident_in, ident16_in, kT_s, v_s, w_hi, w_lo, w_inv, ctx_max,
                    k_max, v_max, win16, win_high, wout16, wout_high):
    assert FT == NCH
    with ExitStack() as ctx:
        m = Space(nc, ctx, "p2")
        ident, ident16, ones = m.sb("ident", [P, P]), m.sb("ident16", [P, P], F16), m.sb("ones", [3, P])
        bias_k, bias_v = m.sb("bk", [P, G]), m.sb("bv", [P, D])
        cx = m.sb("ctx", [P, 2, KD, CH])
        hi, lo = (m.sb(n, [P, 2, KD, CH], F16) for n in ("hi", "lo"))
        ko, vo = m.sb("ko", [P, 2, G, CH]), m.sb("vo", [P, 2, CT, D])
        tops, sc = m.sb("tops", [3, 4]), m.sb("sc", [P, 4])
        wi, wo = m.sb("wi", [P, 2, D]), m.sb("wo", [P, 2, D])
        wi_int, row = m.sb("wi_int", [P, 2, D], F16), m.sb("row", [P, 4])
        high = m.sb("high", [P, 4])
        acc, acc_v, tr = m.ps("acc", [P, G, CH]), m.ps("acc_v", [P, 2, D]), m.ps("tr", [P, CH])

        s_c0, s_chain, s_pe0, s_top, s_init = m.sem("constants_in"), m.sem("chain"), m.sem("max_products"), m.sem("max_steps"), m.sem("initial_values")
        s_c, s_w = m.sems("ctx_in", 2), m.sems("w_in", 2)
        s_hi, s_scale = m.sem("hi"), m.sem("scales")
        s_step, s_wt, s_vmax = m.sem("rounding"), m.sem("w_transposed"), m.sem("v_read")
        s_lo = m.sem("lo")
        s_acc = m.sem("k_product")
        s_accv = m.sem("v_product")
        s_k, s_v = m.sem("k_evacuated"), m.sem("v_evacuated")
        s_kmax = m.sem("k_read")
        s_high = m.sem("high")
        s_wi, s_wo = m.sem("w_in_integers"), m.sem("w_out_integers")
        s_wd = m.sem("w_transpose_evacuated")
        s_ks, s_vs = m.sems("k_stored", 2), m.sems("v_stored", 2)
        block = ctx.enter_context(nc.Block())

        @block.sync
        def _(sync):
            for dst, src in ((ident, ident_in), (ident16, ident16_in), (bias_k, bk), (bias_v, bv)):
                sync.dma_start(dst[:, :], src).then_inc(s_c0, 16)

            def load(n, c):
                sync.wait_ge(s_lo, n + 1)
                sync.sem_inc(s_mark, 1)
                sync.dma_start(cx[:, c, :, :], ctxT.rearrange("(k p) t -> p k t", p=P)[:, :, bass.ds(n % NCH * CH, CH)]).then_inc(s_c[c], 16)

            load(0, 0)
            with sync.Fori(0, NCH // 2) as i:
                for c in range(2):
                    n = i * 2 + c
                    load(n + 1, 1 - c)
                    sync.wait_ge(s_wi, n + 1)
                    sync.sem_inc(s_mark, 1)
                    sync.dma_start(wi[:, c, :], w_inT[bass.ds(n * P, P), :]).then_inc(s_w[c], 16)
                    sync.wait_ge(s_wo, n + 1)
                    sync.sem_inc(s_mark, 1)
                    sync.dma_start(wo[:, c, :], w_out[bass.ds(n * P, P), :]).then_inc(s_w[c], 16)
            sync.wait_ge(s_c[0], (NCH // 2 + 1) * 16)

        @block.gpsimd
        def _(pool):
            pool.memset(ones[:, :], 1.0).then_inc(s_init, 1)
            pool.memset(high[:, :], 0.0).then_inc(s_init, 1)
            pool.memset(ko[:, 1, :, :], 0.0).then_inc(s_init, 1)

        @block.vector
        def _(dve):
            steps = [0]

            def link(ins):
                steps[0] += 1
                ins.then_inc(s_chain, 1)
                dve.wait_ge(s_chain, steps[0])

            def low_part(n, c):
                dve.wait_ge(s_hi, n + 1)
                dve.scalar_tensor_tensor(flat(lo[:, c, :, :]), flat(cx[:, c, :, :]), sc[:, 0:1],
                                         flat(hi[:, c, :, :]), ALU.mult, ALU.subtract).then_inc(s_lo, 1)

            dve.sem_inc(s_lo, 2)
            dve.sem_inc(s_v, 2)
            dve.sem_inc(s_wi, 2)
            dve.sem_inc(s_kmax, 1)
            dve.sem_inc(s_high, 1)
            dve.sem_inc(s_wo, 2)
            dve.wait_ge(s_init, 3)
            dve.wait_ge(s_c0, 4 * 16)
            spread_max(dve, "dve", ctx_max[:, :], 1, tops, acc[:, 0, :], ident, ones, s_pe0, s_top)
            power_scales(dve, link, sc[:, 0:1], sc[:, 1:2], acc[:, 0, P:P + 1])
            dve.tensor_scalar(sc[:, 2:4], w_inv[:, 1:3], sc[:, 1:2], None, ALU.mult).then_inc(s_scale, 1)
            low_part(0, 0)
            with dve.Fori(0, NCH // 2) as i:
                for c in range(2):
                    n = i * 2 + c
                    dve.wait_ge(s_vs[c], i * 16 + 16)
                    for t in range(CT):
                        dve.wait_ge(s_accv, n * CT + t + 1)
                        dve.scalar_tensor_tensor(vo[:, c, t, :], acc_v[:, t % 2, :], sc[:, 3:4], bias_v[:, :], ALU.mult, ALU.add).then_inc(s_v, 1)
                    low_part(n + 1, 1 - c)
                    dve.wait_ge(s_k, n * G + G)
                    dve.wait_ge(s_high, n + 1)
                    dve.tensor_reduce(high[:, 0:1], ko[:, 1 - c, :, :], axis=AX.XY, op=ALU.max, apply_absolute_value=True).then_inc(s_kmax, 1)
                    dve.wait_ge(s_v, n * CT + (CT + 2))
                    dve.tensor_reduce(high[:, 1:2], vo[:, c, :, :], axis=AX.XY, op=ALU.max, apply_absolute_value=True).then_inc(s_vmax, 1)
                    dve.wait_ge(s_kmax, n + 2)
                    dve.wait_ge(s_vmax, n + 1)
                    dve.tensor_tensor(high[:, 2:4], high[:, 2:4], high[:, 0:2], ALU.max).then_inc(s_high, 1)
                    dve.wait_ge(s_w[c], i * 32 + 32)
                    dve.wait_ge(s_wd, n + 1)
                    quantise_tile(dve, wi[:, c, :], wi_int[:, c, :], win_high[:, bass.ds(n, 1)], row[:, 0:1], row[:, 1:2], s_step, n * 14, s_wi)
                    quantise_tile(dve, wo[:, c, :], wout16[:, bass.ds(n, 1), :].rearrange("p a d -> p (a d)"), wout_high[:, bass.ds(n, 1)],
                                  row[:, 2:3], row[:, 3:4], s_step, n * 14 + 7, s_wo)
            dve.wait_ge(s_k, NCH * G + G)
            dve.wait_ge(s_high, NCH + 1)
            link(dve.tensor_reduce(high[:, 0:1], ko[:, 1, :, :], axis=AX.XY, op=ALU.max, apply_absolute_value=True))
            dve.tensor_tensor(k_max[:, :], high[:, 2:3], high[:, 0:1], ALU.max).then_inc(s_high, 1)
            dve.tensor_copy(v_max[:, :], high[:, 3:4]).then_inc(s_high, 1)

        @block.scalar
        def _(act):
            act.sem_inc(s_k, G)
            act.sem_inc(s_wd, 2)
            for s_stored in (*s_ks, *s_vs):
                act.sem_inc(s_stored, 16)

            def high_part(n, c):
                act.wait_ge(s_acc, n * G + G)
                act.wait_ge(s_c[c], (n - c) * 8 + 16)
                act.activation(hi[:, c, :, :], cx[:, c, :, :], ACT.Identity, scale=sc[:, 0:1]).then_inc(s_hi, 1)

            act.wait_ge(s_scale, 1)
            high_part(0, 0)
            with act.Fori(0, NCH // 2) as i:
                for c in range(2):
                    n = i * 2 + c
                    high_part(n + 1, 1 - c)
                    act.wait_ge(s_ks[c], i * 16 + 16)
                    act.wait_ge(s_kmax, n + 1)
                    for g in range(G):
                        act.wait_ge(s_acc, n * G + (2 * G + g + 1))
                        act.activation(ko[:, c, g, :], acc[:, g, :], ACT.Identity, bias=bias_k[:, g:g + 1], scale=sc[:, 2:3]).then_inc(s_k, 1)
                    act.wait_ge(s_v, n * CT + (CT + 2))
                    act.dma_start(v_s[bass.ds(i * P, P), c * CT:(c + 1) * CT, :], vo[:, c, :, :]).then_inc(s_vs[c], 16)
                    act.wait_ge(s_k, n * G + 2 * G)
                    act.dma_start(kT_s[bass.ds(i * P, P), :, c * CH:(c + 1) * CH], ko[:, c, :, :]).then_inc(s_ks[c], 16)
                    act.wait_ge(s_wt, n + 1)
                    act.activation(win16[:, :, bass.ds(n * P, P)], tr[:, :].bitcast(F16)[:, 0:KD * P].rearrange("p (k f) -> p k f", k=KD),
                                   ACT.Copy).then_inc(s_wd, 1)
            for s_stored in (*s_ks, *s_vs):
                act.wait_ge(s_stored, (NCH // 2 + 1) * 16)

        @block.tensor
        def _(pe):
            pe.sem_inc(s_acc, 2 * G)
            pe.wait_ge(s_c0, 4 * 16)
            pe.wait_ge(s_init, 3)
            spread_max(pe, "pe", ctx_max[:, :], 1, tops, acc[:, 0, :], ident, ones, s_pe0, s_top)
            pe.wait_ge(s_chain, 1)
            with pe.Fori(0, NCH // 2) as i:
                for c in range(2):
                    n = i * 2 + c
                    pe.wait_ge(s_lo, n + 3)
                    for t in range(CT):
                        pe.wait_ge(s_v, n * CT + t + 1)
                        three_products(pe, acc_v[:, t % 2, :], lambda part, k: part[:, c, k, t * P:(t + 1) * P],
                                       lambda part, k: part[:, 2, k, :], (hi, lo), (w_hi, w_lo)).then_inc(s_accv, 1)
                    for g in range(G):
                        pe.wait_ge(s_k, n * G + g + 1)
                        three_products(pe, acc[:, g, :], lambda part, k: part[:, 1, k, g * P:(g + 1) * P],
                                       lambda part, k: part[:, c, k, :], (w_hi, w_lo), (hi, lo)).then_inc(s_acc, 1)
                    pe.wait_ge(s_wi, n + 3)
                    pe.wait_ge(s_wd, n + 2)
                    for k in range(KD):
                        last = pe.transpose(tr[:, :].bitcast(F16)[:, k * P:(k + 1) * P], wi_int[:, c, k * P:(k + 1) * P], ident16[:, :])
                    last.then_inc(s_wt, 1)


def attend(nc, s_mark, qT_s, kT_s, v_s, qkv_max, o_inv, ident_in, ident16_in, diag_in, tri_in, step_q, step_k, oT_s):
    with ExitStack() as ctx:
        m = Space(nc, ctx, "p3")
        TURNS = B * G // 2
        NB = 4
        QK = 3 * HD
        ident, ident16, diag16, tri = m.sb("ident", [P, P]), m.sb("ident16", [P, P], F16), m.sb("diag16", [P, P], F16), m.sb("tri", [P, P], F16)
        qs, ks = ([m.sb(f"{n}{p}", [QK_ROWS, 4, S], F16) for p in range(2)] for n in ("qs", "ks"))
        raw, scaled = ([m.sb(f"{n}{o}", [P, S]) for o in range(2)] for n in ("raw", "scaled"))
        hi, lo = ([m.sb(f"{n}{o}", [P, S], F16) for o in range(2)] for n in ("hi", "lo"))
        v = [m.sb(f"v{p}", [P, KT, P]) for p in range(2)]
        probT = m.sb("probT", [P, 2, 4, 2, CH])
        pair_sum = m.sb("pair_sum", [P, 2, 4, CH])
        oT = m.sb("oT", [P, 2, S])
        pv_out, sum_out, recip = m.sb("pv_out", [P, CH]), m.sb("sum_out", [P, CH]), m.sb("recip", [P, CH])
        half_max, negmax = m.sb("half_max", [P, 2, 4, 2]), m.sb("negmax", [P, 4])
        max_parts = m.sb("max_parts", [P, 2, 4, 2], F16)
        sc, ones = m.sb("sc", [P, 16]), m.sb("ones", [P, P])
        tops = m.sb("tops", [3, 4])
        scoresT = m.ps("scoresT", [P, 2, 2, CH])
        scores = m.ps("scores", [P, 2, CH])
        acc, acc_sum = m.ps("acc", [P, CH]), m.ps("acc_sum", [P, CH])

        s_const, s_fill = m.sem("constants_in"), m.sem("step_rows_in")
        s_chain, s_pe0, s_top, s_scale = m.sem("chain"), m.sem("max_products"), m.sem("max_steps"), m.sem("scales")
        s_in, s_qk, s_v = m.sem("qk_in"), m.sems("qk_parts_in", 2), m.sems("v_in", 2)
        s_init = m.sem("initial_values")
        s_st, s_mx = m.sem("scoresT"), m.sem("scores")
        s_cmb, s_mp, s_rc = m.sem("max_combined"), m.sem("max_parts"), m.sem("max_rows_written")
        s_split = m.sem("split")
        s_lo = m.sem("lo")
        s_exp = m.sem("exp")
        s_pre = m.sem("pair_sum")
        s_pv, s_sum = m.sem("pv"), m.sem("sums")
        s_red = m.sem("reduced")
        s_rows = m.sem("max_rows")
        s_raw = m.sem("evacuated")
        s_rec = m.sem("reciprocal")
        s_out = m.sem("oT_written")
        s_o = m.sems("oT_stored", 2)
        block = ctx.enter_context(nc.Block())

        def bank_of(j, n):
            return (j + n + (n >= 2)) % 2

        def rows_bank(j):
            return j % 2

        def wait_apart(eng, sem, count):
            eng.wait_ge(sem, count)
            eng.sem_inc(s_mark, 1)

        @block.sync
        def _(sync):
            for dst, src in ((ident, ident_in), (ident16, ident16_in), (diag16, diag_in), (tri, tri_in)):
                sync.dma_start(dst[:, :], src).then_inc(s_const, 16)

            def load_raw(n, b, g):
                wait_apart(sync, s_split, n * 4 + 4)
                for buf, src in zip(raw, (kT_s, qT_s)):
                    sync.dma_start(buf[:, :].unsqueeze(1), src[bass.ds(b * P, P), bass.ds(g, 1), :]).then_inc(s_in, 16)

            def load_parts(n, par):
                wait_apart(sync, s_lo, n * 2 + 4)
                for o, (dst, parts) in enumerate(((ks[par], (hi, lo, hi)), (qs[par], (hi, hi, lo)))):
                    for r, part in enumerate(parts):
                        for j in range(4):
                            sync.dma_start(dst[r * HD:(r + 1) * HD, j, :],
                                           part[o][j * HD:(j + 1) * HD, :]).then_inc(s_qk[par], 16)

            def load_v(par, b, g):
                sync.dma_start(v[par][:, :, :], v_s[bass.ds(b * P, P), :, bass.ds(g * P, P)]).then_inc(s_v[par], 16)

            for par in range(2):
                load_raw(par, 0, par)
                if par == 0:
                    load_v(1, 0, 1)
                    load_v(0, 0, 0)
                    for q in qs:
                        sync.dma_start(q[QK + 2:QK_ROWS, :, :], step_q).then_inc(s_fill, 16)
                    for k in ks:
                        sync.dma_start(k[QK:QK_ROWS, :, :], step_k).then_inc(s_fill, 16)
                load_parts(par, par)
            load_raw(2, 0, 2)

            def turn(i, last):
                nxt, after = (i + 1) % TURNS, (i + 2) % TURNS
                for par in range(2):
                    b, g, n = nxt // 2, (nxt % 2) * 2 + par, i * 2 + (2 + par)
                    if par == 0 or not last:
                        wait_apart(sync, s_st, i * (16 * NB) + 32 * (par + 1))
                        load_parts(n, par)
                    if par == 0:
                        load_raw(n + 1, nxt // 2, (nxt % 2) * 2 + 1)
                    elif not last:
                        load_raw(n + 1, after // 2, (after % 2) * 2)
                    wait_apart(sync, s_out, i * NB + (2 * (par + 1) + 2))
                    sync.dma_start(oT_s[bass.ds(i // 2 * P, P), bass.ds((i % 2) * 2 + par, 1), :], oT[:, par:par + 1, :]).then_inc(s_o[par], 16)
                    if not last:
                        load_v(par, b, g)

            with sync.Fori(0, TURNS - 1) as i:
                turn(i, False)
            turn(TURNS - 1, True)
            sync.wait_ge(s_in, (2 * TURNS + 2) * 32)
            for par in range(2):
                sync.wait_ge(s_o[par], TURNS * 16 + 16)
                sync.wait_ge(s_v[par], TURNS * 16)
                sync.wait_ge(s_qk[par], (TURNS + 1 - par) * 24 * 16)

        @block.gpsimd
        def _(pool):
            pool.memset(ones[:, :], 1.0).then_inc(s_scale, 1)
            pool.sem_inc(s_lo, 2)
            pool.sem_inc(s_pre, 8)
            pool.sem_inc(s_out, 1)

            def low_part(n, o):
                pool.wait_ge(s_split, n * 4 + (2 * o + 6))
                pool.tensor_tensor(lo[o][:, :], scaled[o][:, :], hi[o][:, :], ALU.subtract).then_inc(s_lo, 1)

            low_part(0, 0)
            low_part(0, 1)
            pool.memset(probT[:, 1, :, :, :], 0.0).then_inc(s_init, 1)
            pool.memset(pair_sum[:, 1, :, :], 1.0).then_inc(s_init, 1)
            low_part(1, 0)
            low_part(1, 1)
            pool.wait_ge(s_init, 2)
            with pool.Fori(0, TURNS) as i:
                for t in range(NB):
                    blk = i * NB + t
                    for p in range(4):
                        for j in range(4):
                            pair, step = blk * 4 + p, p * 4 + j
                            if j == 0:
                                pool.wait_ge(s_sum, pair + 1)
                            pool.wait_ge(s_exp, blk * 16 + (step + 3))
                            pool.tensor_tensor(pair_sum[:, p % 2, j, :], probT[:, p % 2, j, 0, :], probT[:, p % 2, j, 1, :],
                                               ALU.add).then_inc(s_pre, 1)
                            if t % 2 == 1 and step in (8, 15):
                                low_part(i * 2 + (2 + t // 2), 0 if step == 8 else 1)
                            if step == 15:
                                par, half = (t - 1) // 2 % 2, (t - 1) % 2
                                if half == 0:
                                    pool.wait_ge(s_o[par], i * 16 + 16)
                                pool.wait_ge(s_rec, blk * 8 + 16)
                                pool.tensor_tensor(oT[:, par, half * CH:(half + 1) * CH], pv_out[:, :], recip[:, :],
                                                   ALU.mult).then_inc(s_out, 1)
            pool.wait_ge(s_rec, TURNS * NB * 8 + 16)
            pool.tensor_tensor(oT[:, 1, CH:2 * CH], pv_out[:, :], recip[:, :], ALU.mult).then_inc(s_out, 1)

        @block.vector
        def _(dve):
            dve.sem_inc(s_red, 2)
            dve.sem_inc(s_rec, 8)
            steps = [0]

            def link(ins):
                steps[0] += 1
                ins.then_inc(s_chain, 1)
                dve.wait_ge(s_chain, steps[0])

            spread_max(dve, "dve", qkv_max[:, :], 3, tops, acc, ident, ones, s_pe0, s_top)
            link(dve.tensor_scalar(sc[:, 0:2], acc[:, P:P + 2], 1e-18, 1e18, ALU.max, ALU.min))
            link(dve.reciprocal(sc[:, 2:3], sc[:, 1:2]))
            link(dve.tensor_scalar(sc[:, 3:4], sc[:, 0:1], sc[:, 2:3], math.sqrt(HD), ALU.mult, ALU.mult))
            bits = sc[:, :].bitcast(I32)
            link(dve.tensor_scalar(bits[:, 4:5], bits[:, 3:4], 24, 23, ALU.logical_shift_right, ALU.logical_shift_left))
            link(dve.tensor_scalar(bits[:, 5:6], bits[:, 4:5], 64 << 23, None, ALU.add))
            link(dve.tensor_scalar(bits[:, 8:9], bits[:, 5:6], -1, 254 << 23, ALU.mult, ALU.add))
            power_scales(dve, link, sc[:, 10:11], o_inv[:, :], acc[:, P + 2:P + 3])
            dve.tensor_scalar(sc[:, 9:10], sc[:, 5:6], 1 / math.sqrt(HD), None, ALU.mult).then_inc(s_scale, 1)

            def maxima(head, par, n):
                dve.wait_ge(s_mx, head * 8 + (n + 1))
                dve.tensor_reduce(half_max[:, par, n // 2, n % 2:n % 2 + 1], scores[:, bank_of(par, n), :], axis=AX.X, op=ALU.max,
                                  negate=True).then_inc(s_red, 1)

            def combine(head, par):
                dve.wait_ge(s_red, head * 8 + 10)
                dve.tensor_tensor(negmax[:, :], half_max[:, par, :, 0], half_max[:, par, :, 1], ALU.min).then_inc(s_cmb, 1)
                dve.wait_ge(s_rows, head + 1)
                dve.wait_ge(s_cmb, head * 2 + 1)
                dve.tensor_scalar(max_parts[:, par, :, 0], negmax[:, :], 1 / MAX_ROW, None, ALU.mult).then_inc(s_cmb, 1)
                dve.wait_ge(s_cmb, head * 2 + 2)
                dve.scalar_tensor_tensor(max_parts[:, par, :, 1], negmax[:, :], 1 / MAX_ROW, max_parts[:, par, :, 0],
                                         ALU.mult, ALU.subtract).then_inc(s_mp, 1)
                dve.wait_ge(s_mp, head + 1)

            def reciprocals(blk, e):
                if e == 0:
                    dve.wait_ge(s_raw, blk * 2 + 2)
                    dve.wait_ge(s_out, blk + 1)
                    dve.sem_inc(s_mark, 1)
                dve.reciprocal(recip[:, e * 64:(e + 1) * 64], sum_out[:, e * 64:(e + 1) * 64]).then_inc(s_rec, 1)

            for p in range(4):
                for n in range(8):
                    maxima(p, p % 2, n)
                    if n == 0 and p > 0:
                        combine(p - 1, (p - 1) % 2)
            with dve.Fori(0, TURNS) as i:
                for t in range(NB):
                    blk = i * NB + t
                    eighth = 0
                    for p in range(4):
                        for n in range(8):
                            maxima(blk * 4 + (4 + p), p % 2, n)
                            if n == 0:
                                combine(blk * 4 + (3 + p), (p + 3) % 2)
                            if p > 0 and n in (1, 3, 5) and eighth < 8:
                                reciprocals(blk, eighth)
                                eighth += 1
            for e in range(8):
                reciprocals(TURNS * NB, e)

        @block.scalar
        def _(act):
            act.sem_inc(s_split, 4)
            act.sem_inc(s_exp, 2)
            for par in range(2):
                act.sem_inc(s_o[par], 16)

            def split(n, o, part):
                out = (scaled, hi)[part][o]
                act.activation(out[:, :], raw[o][:, :], ACT.Identity, scale=sc[:, 8 + o:9 + o]).then_inc(s_split, 1)

            def write_max_rows(head, par, half, j):
                act.wait_ge(s_rows, head + 3)
                act.activation(qs[par][QK:QK + 2, j, half * CH:(half + 1) * CH], scores[QK:QK + 2, rows_bank(j + 1), :],
                               ACT.Copy).then_inc(s_rc, 1)

            def evacuate(blk, out, src, sem):
                act.wait_ge(sem, blk * 4 + 2)
                act.wait_ge(s_out, blk + 1)
                act.wait_ge(s_rec, blk * 8 + 8)
                scale = sc[:, 10:11] if out is pv_out else 1.0
                act.activation(out[:, :], src[:, :], ACT.Identity, scale=scale).then_inc(s_raw, 1)

            act.wait_ge(s_scale, 2)
            for n in range(2):
                act.wait_ge(s_in, n * 32 + 32)
                act.wait_ge(s_lo, n * 2 + 2)
                if n == 1:
                    act.wait_ge(s_qk[0], 24 * 16)
                for o in range(2):
                    split(n, o, 0)
                    split(n, o, 1)
            for head in range(3):
                write_max_rows(head, 0, 0, head)
            with act.Fori(0, TURNS) as i:
                for t in range(NB):
                    blk = i * NB + t
                    for p in range(4):
                        for j in range(4):
                            pair, step = blk * 4 + p, p * 4 + j
                            if j == 2:
                                other = (t + (p > 0)) % NB
                                write_max_rows(pair + 3, other // 2, other % 2, (p + 3) % 4)
                            if j == 0:
                                act.wait_ge(s_pv, pair + 1)
                            act.wait_ge(s_pre, blk * 16 + (step + 1))
                            act.wait_ge(s_st, blk * 16 + (step + 1))
                            act.activation(probT[:, p % 2, j, :, :], scoresT[:, j % 2, :, :], ACT.Exp).then_inc(s_exp, 1)
                            if step == 3:
                                evacuate(blk, pv_out, acc, s_pv)
                            if step == 4:
                                evacuate(blk, sum_out, acc_sum, s_sum)
                            if t % 2 == 1 and j == 2:
                                n, q = i * 2 + (2 + t // 2), t // 2
                                if p == 0:
                                    act.wait_ge(s_in, n * 32 + 32)
                                    act.wait_ge(s_lo, n * 2 + 2)
                                    act.wait_ge(s_qk[1 - q], (i + 1 + q) * (24 * 16))
                                    act.sem_inc(s_mark, 1)
                                split(n, p // 2, p % 2)
            evacuate(TURNS * NB, pv_out, acc, s_pv)
            evacuate(TURNS * NB, sum_out, acc_sum, s_sum)

        @block.tensor
        def _(pe):
            pe.sem_inc(s_pv, 1)
            pe.sem_inc(s_sum, 1)
            pe.sem_inc(s_rows, 2)
            pe.wait_ge(s_const, 4 * 16)
            pe.wait_ge(s_scale, 1)
            spread_max(pe, "pe", qkv_max[:, :], 3, tops, acc, ident, ones, s_pe0, s_top)

            def make_scores(head, t, p, n):
                par, qt, half = t // 2 % 2, t % 2 * 4 + n // 2, n % 2
                if n == 3:
                    if t > 0 or p > 0:
                        pe.wait_ge(s_rc, head)
                elif n == 2:
                    pe.wait_ge(s_red, head * 8 + 4)
                else:
                    pe.wait_ge(s_red, head * 8 + (n + 1))
                pe.matmul(scores[:, bank_of(p, n), :], qs[par][0:QK, p, qt * P:(qt + 1) * P],
                          ks[par][0:QK, p, half * CH:(half + 1) * CH], start=True, stop=True).then_inc(s_mx, 1)

            def make_max_rows(head, p):
                pe.wait_ge(s_mp, head + 1)
                pe.wait_ge(s_red, head * 8 + 11)
                for qt in range(4):
                    last = pe.matmul(scores[QK:QK + 2, rows_bank(p), qt * P:(qt + 1) * P], max_parts[:, (p - 1) % 2, qt, :],
                                     ident16[:, :], start=True, stop=True)
                last.then_inc(s_rows, 1)

            def make_scoresT(blk, t, p, j, tiles=(0, 1)):
                step = p * 4 + j
                par, half = t // 2, t % 2
                if 0 in tiles:
                    pe.wait_ge(s_exp, blk * 16 + (step + 1))
                    if p == 0:
                        pe.wait_ge(s_rc, blk * 4 + (j + 1))
                for k in tiles:
                    kt = 2 * p + k
                    bank = scoresT[:, j % 2, k, :]
                    diagonal = kt // 4 == half
                    last = pe.matmul(bank, ks[par][:, j, kt * P:(kt + 1) * P], qs[par][:, j, half * CH:(half + 1) * CH],
                                     start=True, stop=not diagonal)
                    if diagonal:
                        last = pe.matmul(bank[:, (kt % 4) * P:(kt % 4 + 1) * P], diag16[:, :], tri[:, :], start=False, stop=True)
                if 1 in tiles:
                    last.then_inc(s_st, 1)

            def pv(par, p, k):
                for j in range(4):
                    last = pe.matmul(acc[j * HD:(j + 1) * HD, :], v[par][:, 2 * p + k, j * HD:(j + 1) * HD],
                                     probT[:, p % 2, j, k, :], start=(p == 0 and k == 0), stop=(p == 3 and k == 1))
                return last

            def sums(p):
                for j in range(4):
                    last = pe.matmul(acc_sum[j * HD:(j + 1) * HD, :], ones[:, 0:HD], pair_sum[:, p % 2, j, :],
                                     start=(p == 0), stop=(p == 3))
                return last

            pe.wait_ge(s_qk[0], 24 * 16)
            for p in range(4):
                for n in range(8):
                    if p > 0 and n == 2:
                        make_max_rows(p - 1, p)
                    make_scores(p, 0, p, n)
            pe.wait_ge(s_fill, 4 * 16)
            pe.wait_ge(s_v[1], 16)
            pe.wait_ge(s_init, 2)
            for j in range(4):
                pe.matmul(acc[j * HD:(j + 1) * HD, :], v[1][:, 0, j * HD:(j + 1) * HD], probT[:, 1, j, 0, :], start=True, stop=False)
                pe.matmul(acc_sum[j * HD:(j + 1) * HD, :], ones[:, 0:HD], pair_sum[:, 1, j, :], start=True, stop=False)
            with pe.Fori(0, TURNS) as i:
                for t in range(NB):
                    blk = i * NB + t
                    for p in range(4):
                        pair, last_p = blk * 4 + p, (p + 3) % 4
                        v_par = (t - (p == 0)) // 2 % 2
                        if p == 0 and t == 1:
                            pe.wait_ge(s_qk[1], i * (24 * 16) + 24 * 16)
                        if p == 0 and t == NB - 1:
                            pe.wait_ge(s_qk[0], i * (24 * 16) + 48 * 16)

                        def tile(n):
                            make_scores(pair + 4, t + 1, p, n)

                        make_scoresT(blk, t, p, 0)
                        tile(0)
                        make_scoresT(blk, t, p, 1)
                        tile(1)
                        pe.wait_ge(s_exp, blk * 16 + (p * 4 + 2))
                        if p == 1:
                            pe.wait_ge(s_raw, blk * 2 + 1)
                            if t % 2 == 0:
                                pe.wait_ge(s_v[t // 2], i * 16 + 16)
                        pv(v_par, last_p, 0)
                        make_max_rows(pair + 3, p)
                        make_scoresT(blk, t, p, 2)
                        tile(2)
                        make_scoresT(blk, t, p, 3, (0,))
                        tile(3)
                        pv(v_par, last_p, 1).then_inc(s_pv, 1)
                        tile(4)
                        make_scoresT(blk, t, p, 3, (1,))
                        tile(5)
                        pe.wait_ge(s_pre, blk * 16 + (p * 4 + 8))
                        if p == 1:
                            pe.wait_ge(s_raw, blk * 2 + 2)
                        sums(last_p).then_inc(s_sum, 1)
                        tile(6)
                        tile(7)
            pe.wait_ge(s_exp, TURNS * NB * 16 + 2)
            pv(1, 3, 0)
            pv(1, 3, 1).then_inc(s_pv, 1)
            pe.wait_ge(s_pre, TURNS * NB * 16 + 8)
            sums(3).then_inc(s_sum, 1)


def merge(nc, s_mark, x, bo, oT_s, wo_hi, wo_lo, wo_inv, o_inv, x1_s, xnT_s, xn_max, ident_in):
    with ExitStack() as ctx:
        m = Space(nc, ctx, "p4")
        CPT = 4
        NT, TURNS = CPT * CT, NCH // CPT
        QUARTERS = ((0,), (1, 2), (3,), ())
        ident, bias, factor = m.sb("ident", [P, P]), m.sb("bo", [P, D]), m.sb("factor", [P, 1])
        oT = m.sb("oT", [P, 2, G, CH])
        hi, lo = (m.sb(n, [P, 2, G, CH], F16) for n in ("hi", "lo"))
        xs = m.sb("x", [P, NT, D])
        xn = m.sb("xn", [P, NT, D])
        xT = m.sb("xT", [P, 2, KD, CH])
        stats, mv = m.sb("stats", [P, NT, 6]), m.sb("mv", [P, NT, 2])
        std, rstd, shift, eps = m.sb("std", [P, NT]), m.sb("rstd", [P, NT]), m.sb("shift", [P, NT]), m.sb("eps", [P, 1])
        high = m.sb("high", [P, NT + 1])
        acc, tr = m.ps("acc", [P, 4, D]), m.ps("tr", [P, 2, CH])

        s_k0, s_x, s_oT = m.sem("constants_in"), m.sems("x_in", CPT), m.sems("oT_in", 2)
        s_eps, s_var, s_std, s_rstd, s_shift = m.sem("eps"), m.sem("var"), m.sem("std"), m.sem("rstd"), m.sem("shift")
        s_st, s_high = m.sem("stats"), m.sem("high")
        s_xb, s_hi = m.sem("bias_added"), m.sem("hi")
        s_lo = m.sem("lo")
        s_acc = m.sem("product")
        s_sum = m.sem("sum")
        s_tr = m.sem("transposed")
        s_xn = m.sem("xn")
        s_xt = m.sem("xT_evacuated")
        s_xs, s_xts = m.sems("x1_stored", CPT), m.sems("xT_stored", 2)
        block = ctx.enter_context(nc.Block())

        @block.sync
        def _(sync):
            def load_oT(n, c):
                sync.wait_ge(s_lo, n * G + G)
                sync.sem_inc(s_mark, 1)
                chunk = n % NCH
                for half in range(2):
                    sync.dma_start(oT[:, c, 2 * half:2 * half + 2, :],
                                   oT_s[bass.ds(chunk // 2 * P, P), 2 * half:2 * half + 2, c * CH:(c + 1) * CH]).then_inc(s_oT[c], 16)

            def load_x(n, q, turn):
                sync.wait_ge(s_xs[q], turn * 16 + 16)
                sync.sem_inc(s_mark, 1)
                sync.dma_start(xs[:, q * CT:(q + 1) * CT, :], x[bass.ds(n % NCH * CH, CH), :].rearrange("(t p) d -> p t d", p=P)).then_inc(s_x[q], 16)

            load_oT(0, 0)
            load_x(0, 0, 0)
            for dst, src in ((ident, ident_in), (bias, bo)):
                sync.dma_start(dst[:, :], src).then_inc(s_k0, 16)
            load_oT(1, 1)
            with sync.Fori(0, TURNS) as i:
                for q in range(CPT):
                    n = i * CPT + q
                    load_x(n + 1, (q + 1) % CPT, i + (q + 1) // CPT)
                    load_oT(n + 2, q % 2)
            for c in range(2):
                sync.wait_ge(s_oT[c], (NCH // 2 + 1) * 32)

        @block.gpsimd
        def _(pool):
            pool.sem_inc(s_lo, 2 * G)

            def low_part(n, c, g):
                pool.wait_ge(s_hi, n * G + (g + 1))
                pool.tensor_tensor(lo[:, c, g, :], oT[:, c, g, :], hi[:, c, g, :], ALU.subtract).then_inc(s_lo, 1)

            def add_bias(t, turn):
                if t % CT == 0:
                    pool.wait_ge(s_x[t // CT], turn * 16 + 16)
                pool.tensor_tensor(xs[:, t, :], xs[:, t, :], bias[:, :], ALU.add).then_inc(s_xb, 1)

            for g in range(G):
                low_part(0, 0, g)
            pool.wait_ge(s_k0, 2 * 16)
            for t in range(CT):
                add_bias(t, 0)
            with pool.Fori(0, TURNS) as i:
                for t in range(NT):
                    ahead = t + CT
                    add_bias(ahead % NT, i + ahead // NT)
                    for g in QUARTERS[t % CT]:
                        low_part(i * CPT + ahead // CT, ahead // CT % 2, g)

        @block.vector
        def _(dve):
            dve.memset(eps[:, :], EPS).then_inc(s_eps, 1)
            dve.tensor_scalar(factor[:, :], wo_inv, o_inv[:, :], None, ALU.mult).then_inc(s_eps, 1)
            dve.memset(high[:, :], 0.0).then_inc(s_high, 1)
            dve.sem_inc(s_sum, 4)
            dve.wait_ge(s_eps, 2)

            def magnitude(i, t):
                dve.wait_ge(s_xn, i * NT + (NT + t + 1))
                if t == 0:
                    dve.wait_ge(s_high, i * (NT + 1) + 1)
                dve.tensor_reduce(high[:, t:t + 1], xn[:, t, :], axis=AX.X, op=ALU.max, apply_absolute_value=True).then_inc(s_high, 1)

            with dve.Fori(0, TURNS) as i:
                for t in range(NT):
                    n = i * NT + t
                    dve.wait_ge(s_xb, n + 1)
                    dve.wait_ge(s_acc, n + (2 * CT + 1))
                    dve.scalar_tensor_tensor(xs[:, t, :], acc[:, t % 4, :], factor[:, 0:1], xs[:, t, :], ALU.mult, ALU.add).then_inc(s_sum, 1)
                    dve.wait_ge(s_sum, n + 5)
                    dve.bn_stats(stats[:, t, :], xs[:, t, :]).then_inc(s_st, 1)
                    dve.wait_ge(s_st, n + 1)
                    dve.sem_inc(s_mark, 1)
                    dve.bn_aggr(mv[:, t, :], stats[:, t, :]).then_inc(s_var, 1)
                    if t > 0:
                        magnitude(i, t - 1)
                    dve.wait_ge(s_std, n + 1)
                    dve.reciprocal(rstd[:, t:t + 1], std[:, t:t + 1]).then_inc(s_rstd, 1)
                    dve.wait_ge(s_rstd, n + 1)
                    dve.scalar_tensor_tensor(shift[:, t:t + 1], mv[:, t, 0:1], -1.0, rstd[:, t:t + 1], ALU.mult, ALU.mult).then_inc(s_shift, 1)
                magnitude(i, NT - 1)
                dve.wait_ge(s_high, i * (NT + 1) + (NT + 1))
                dve.tensor_reduce(high[:, NT:NT + 1], high[:, :], axis=AX.X, op=ALU.max).then_inc(s_high, 1)
            dve.wait_ge(s_high, TURNS * (NT + 1) + 1)
            dve.tensor_copy(xn_max[:, :], high[:, NT:NT + 1]).then_inc(s_high, 1)

        @block.scalar
        def _(act):
            act.sem_inc(s_xt, 2)
            act.sem_inc(s_xn, NT)
            for s_stored in (*s_xs, *s_xts):
                act.sem_inc(s_stored, 16)

            def high_part(n, c, g, count):
                act.wait_ge(s_oT[c], count)
                act.wait_ge(s_acc, n * CT + CT)
                act.activation(hi[:, c, g, :], oT[:, c, g, :], ACT.Copy).then_inc(s_hi, 1)

            def evacuate(i, t):
                q = t // CT
                if t % CT == 0:
                    act.wait_ge(s_xts[q % 2], i * 32 + (q // 2 * 16 + 16))
                act.wait_ge(s_tr, i * NT + (NT + t + 1))
                act.activation(xT[:, q % 2, :, (t % CT) * P:(t % CT + 1) * P], tr[:, t % 2, :], ACT.Copy).then_inc(s_xt, 1)
                if t % CT == CT - 1:
                    act.wait_ge(s_xt, i * NT + (t + 3))
                    act.dma_start(xnT_s[bass.ds((i * CPT + q) * P, P), :, :], xT[:, q % 2, :, :]).then_inc(s_xts[q % 2], 16)

            for g in range(G):
                high_part(0, 0, g, 32)
            act.wait_ge(s_eps, 1)
            with act.Fori(0, TURNS) as i:
                for t in range(NT):
                    q, g, n = t // CT, t % CT, i * NT + t
                    for quarter in QUARTERS[g]:
                        high_part(i * CPT + (q + 1), (q + 1) % 2, quarter, i * (CPT // 2 * 32) + ((q + 1) // 2 * 32 + 32))
                    act.wait_ge(s_var, n + 1)
                    act.activation(std[:, t:t + 1], mv[:, t, 1:2], ACT.Sqrt, bias=eps[:, 0:1]).then_inc(s_std, 1)
                    act.wait_ge(s_shift, n + 1)
                    act.wait_ge(s_tr, n + 1)
                    act.activation(xn[:, t, :], xs[:, t, :], ACT.Identity, bias=shift[:, t:t + 1], scale=rstd[:, t:t + 1]).then_inc(s_xn, 1)
                    if t > 0:
                        evacuate(i, t - 1)
                    if g == CT - 1:
                        act.wait_ge(s_xn, n + (NT + 1))
                        act.dma_start(x1_s[bass.ds((i * CPT + q) * P, P), :, :], xs[:, q * CT:(q + 1) * CT, :]).then_inc(s_xs[q], 16)
                evacuate(i, NT - 1)
            for s_stored in s_xs:
                act.wait_ge(s_stored, TURNS * 16 + 16)
            for s_stored in s_xts:
                act.wait_ge(s_stored, NCH // 2 * 16 + 16)

        @block.tensor
        def _(pe):
            pe.sem_inc(s_acc, 2 * CT)
            pe.sem_inc(s_tr, NT)
            pe.wait_ge(s_k0, 2 * 16)

            def transposes(i, t):
                pe.wait_ge(s_xn, i * NT + (NT + t + 1))
                pe.wait_ge(s_xt, i * NT + (t + 1))
                for k in range(KD):
                    last = pe.transpose(tr[:, t % 2, k * P:(k + 1) * P], xn[:, t, k * P:(k + 1) * P], ident[:, :])
                last.then_inc(s_tr, 1)

            with pe.Fori(0, TURNS) as i:
                for t in range(NT):
                    q, tile = t // CT, t % CT
                    if tile == 0:
                        pe.wait_ge(s_lo, (i * CPT + q) * G + 3 * G)
                    pe.wait_ge(s_sum, i * NT + t + 1)
                    three_products(pe, acc[:, t % 4, :], lambda part, k: part[:, q % 2, k, tile * P:(tile + 1) * P],
                                   lambda part, k: part[:, k, :], (hi, lo), (wo_hi, wo_lo)).then_inc(s_acc, 1)
                    if t > 1:
                        transposes(i, t - 2)
                transposes(i, NT - 2)
                transposes(i, NT - 1)


def expand(nc, s_mark, b_in, ident_in, win16, win_high, xnT_s, xn_max, h_s, h_max):
    with ExitStack() as ctx:
        m = Space(nc, ctx, "p5")
        HP = 4
        NP = 2 * FT // HP
        ident, bias, alpha = m.sb("ident", [P, P]), m.sb("b_in", [P, FT]), m.sb("alpha", [P, FT])
        scale_x, tops, ones = m.sb("scale_x", [P, 3]), m.sb("tops", [1, 2]), m.sb("ones", [1, P])
        raw = m.sb("raw", [P, 2, KD, CH])
        hi, lo = (m.sb(n, [P, 2, KD, CH], F16) for n in ("hi", "lo"))
        g = m.sb("g", [P, 4, HP, CH])
        high = m.sb("high", [P, NP + 1])
        acc = m.ps("acc", [P, 8, CH])

        s_k0, s_chain, s_pe0, s_top = m.sem("constants_in"), m.sem("chain"), m.sem("max_products"), m.sem("max_steps")
        s_x, s_int, s_hi, s_high, s_scale = m.sems("x_in", 2), m.sem("integers"), m.sem("x_hi"), m.sem("high"), m.sem("scales")
        s_lo = m.sem("x_lo")
        s_acc = m.sem("product")
        s_g = m.sem("gelu")
        s_read = m.sem("g_read")
        s_gs = m.sems("g_stored", 4)
        block = ctx.enter_context(nc.Block())

        @block.sync
        def _(sync):
            for dst, src in ((ident, ident_in), (bias, b_in)):
                sync.dma_start(dst[:, :], src).then_inc(s_k0, 16)

            def load(n, c):
                sync.wait_ge(s_lo, n + 1)
                sync.sem_inc(s_mark, 1)
                sync.dma_start(raw[:, c, :, :], xnT_s[bass.ds(n % NCH * P, P), :, :]).then_inc(s_x[c], 16)

            load(0, 0)
            with sync.Fori(0, NCH // 2) as i:
                load(i * 2 + 1, 1)
                for p in range(NP):
                    if p == 2:
                        load(i * 2 + 2, 0)
                    sync.wait_ge(s_g, i * (2 * FT) + (HP * (p + 1) + 8))
                    sync.sem_inc(s_mark, 1)
                    sync.dma_start(h_s[bass.ds((i * 2 + p // 4) * P, P), (p % 4) * HP:(p % 4 + 1) * HP, :], g[:, p % 4, :, :]).then_inc(s_gs[p % 4], 16)
            for s_stored in s_gs:
                sync.wait_ge(s_stored, NCH * 16 + 16)
            sync.wait_ge(s_x[0], (NCH // 2 + 1) * 16)

        @block.gpsimd
        def _(pool):
            pool.memset(ones[:, :], 1.0).then_inc(s_scale, 1)
            pool.sem_inc(s_lo, 2)

            def second_part(n, c):
                pool.wait_ge(s_acc, n * FT + FT)
                pool.wait_ge(s_hi, n + 1)
                pool.tensor_tensor(lo[:, c, :, :], raw[:, c, :, :], hi[:, c, :, :], ALU.subtract).then_inc(s_lo, 1)

            second_part(0, 0)
            with pool.Fori(0, NCH // 2) as i:
                second_part(i * 2 + 1, 1)
                second_part(i * 2 + 2, 0)

        @block.vector
        def _(dve):
            steps = [0]

            def link(ins):
                steps[0] += 1
                ins.then_inc(s_chain, 1)
                dve.wait_ge(s_chain, steps[0])

            dve.sem_inc(s_read, 4)
            dve.memset(high[:, :], 0.0).then_inc(s_high, 1)
            dve.wait_ge(s_k0, 2 * 16)
            spread_max(dve, "dve", xn_max[:, :], 1, tops, acc[:, 0, :], ident, ones, s_pe0, s_top)
            link(dve.tensor_scalar(scale_x[:, 0:1], acc[:, 0, P:P + 1], 1e-8, None, ALU.max))
            link(dve.reciprocal(scale_x[:, 1:2], scale_x[:, 0:1]))
            link(dve.tensor_scalar(scale_x[:, 2:3], scale_x[:, 1:2], 32767.0, None, ALU.mult))
            dve.tensor_scalar(alpha[:, :], win_high[:, :], scale_x[:, 0:1], 1 / (127.0 * 32767.0), ALU.mult, ALU.mult).then_inc(s_scale, 1)

            def integers(n, c):
                x = raw[:, c, :, :]
                dve.tensor_scalar(x, x, scale_x[:, 2:3], 32767.0, ALU.mult, ALU.min).then_inc(s_int, 1)
                dve.wait_ge(s_int, n * 3 + 1)
                dve.tensor_scalar(x, x, -32768.0, ROUND, ALU.max, ALU.add).then_inc(s_int, 1)
                dve.wait_ge(s_int, n * 3 + 2)
                dve.tensor_scalar(x, x, ROUND, None, ALU.subtract).then_inc(s_int, 1)

            dve.wait_ge(s_x[0], 16)
            integers(0, 0)
            with dve.Fori(0, NCH // 2) as i:
                for p in range(NP):
                    if p in (1, 5):
                        c = 1 if p == 1 else 0
                        n = i * 2 + 2 - c
                        dve.wait_ge(s_x[c], (i + 2 - c) * 16)
                        integers(n, c)
                    dve.wait_ge(s_g, i * (2 * FT) + (HP * (p + 1) + 8))
                    if p == 0:
                        dve.wait_ge(s_high, i * (NP + 1) + 1)
                    dve.tensor_reduce(high[:, p:p + 1], g[:, p % 4, :, :], axis=AX.XY, op=ALU.max,
                                      apply_absolute_value=True).then_inc(s_read, 1)
                dve.wait_ge(s_read, i * NP + (NP + 4))
                dve.tensor_reduce(high[:, NP:NP + 1], high[:, :], axis=AX.X, op=ALU.max).then_inc(s_high, NP + 1)
            dve.wait_ge(s_high, NCH // 2 * (NP + 1) + 1)
            dve.tensor_copy(h_max[:, :], high[:, NP:NP + 1]).then_inc(s_high, 1)

        @block.scalar
        def _(act):
            act.sem_inc(s_g, 8)
            for s_stored in s_gs:
                act.sem_inc(s_stored, 16)

            def first_part(n, c):
                act.wait_ge(s_acc, n * FT + FT)
                act.wait_ge(s_int, n * 3 + 3)
                act.activation(hi[:, c, :, :], raw[:, c, :, :], ACT.Copy).then_inc(s_hi, 1)

            first_part(0, 0)
            act.wait_ge(s_scale, 2)
            with act.Fori(0, NCH // 2) as i:
                for o in range(2 * FT):
                    f, p = o % FT, o // HP
                    if o == 6:
                        first_part(i * 2 + 1, 1)
                    if o == FT + 6:
                        first_part(i * 2 + 2, 0)
                    if o % HP == 0:
                        act.wait_ge(s_gs[p % 4], (i * 2 + p // 4) * 16 + 16)
                        act.wait_ge(s_read, i * NP + p + 1)
                    act.wait_ge(s_acc, i * (2 * FT) + (2 * FT + o + 1))
                    act.activation(g[:, p % 4, o % HP, :], acc[:, o % 8, :], ACT.Gelu, bias=bias[:, f:f + 1],
                                   scale=alpha[:, f:f + 1]).then_inc(s_g, 1)

        @block.tensor
        def _(pe):
            pe.sem_inc(s_acc, 2 * FT)
            pe.wait_ge(s_k0, 2 * 16)
            pe.wait_ge(s_scale, 1)
            spread_max(pe, "pe", xn_max[:, :], 1, tops, acc[:, 0, :], ident, ones, s_pe0, s_top)
            pe.wait_ge(s_chain, 1)
            with pe.Fori(0, NCH // 2) as i:
                for o in range(2 * FT):
                    c, f = o // FT, o % FT
                    if f == 0:
                        pe.wait_ge(s_lo, i * 2 + c + 3)
                    pe.wait_ge(s_g, i * (2 * FT) + o + 1)
                    for k in range(KD):
                        for part in (hi, lo):
                            last = pe.matmul(acc[:, o % 8, :], win16[:, k, f * P:(f + 1) * P], part[:, c, k, :],
                                             start=(k == 0 and part is hi), stop=(k == KD - 1 and part is lo))
                    last.then_inc(s_acc, 1)


def contract(nc, s_mark, b_out, ident_in, wout16, wout_high, h_s, h_max, x1_s, out):
    with ExitStack() as ctx:
        m = Space(nc, ctx, "p6")
        HP = 4
        NP = FT // HP
        ident, bias = m.sb("ident", [P, P]), m.sb("b_out", [P, D])
        rel = m.sb("rel", [P, FT])
        both, tops, ones, sc = m.sb("both", [P, 2]), m.sb("tops", [2, 3]), m.sb("ones", [2, P]), m.sb("sc", [P, 4])
        h = m.sb("h", [P, 8, HP, CH])
        hi, lo = (m.sb(n, [P, 4, HP, CH], F16) for n in ("hi", "lo"))
        x1, y = m.sb("x1", [P, 2, CT, D]), m.sb("y", [P, CT, D])
        acc = m.ps("acc", [P, 8, D])

        s_c, s_chain, s_pe0, s_top = m.sem("constants_in"), m.sem("chain"), m.sem("max_products"), m.sem("max_steps")
        s_ones = m.sem("ones")
        s_h = m.sems("h_in", 8)
        s_x = m.sems("x1_in", 2)
        s_int, s_hi, s_xb = m.sem("integers"), m.sem("h_hi"), m.sem("bias_added")
        s_lo = m.sem("h_lo")
        s_mm = m.sem("piece_product")
        s_y = m.sem("y")
        s_ys = m.sem("y_stored")
        block = ctx.enter_context(nc.Block())

        @block.sync
        def _(sync):
            for dst, src in ((ident, ident_in), (bias, b_out)):
                sync.dma_start(dst[:, :], src).then_inc(s_c, 16)

            def load(n, c):
                for p in range(NP):
                    slot = c * NP + p
                    sync.wait_ge(s_lo, n * NP + p + 1)
                    sync.sem_inc(s_mark, 1)
                    sync.dma_start(h[:, slot, :, :], h_s[bass.ds(n % NCH * P, P), p * HP:(p + 1) * HP, :]).then_inc(s_h[slot], 16)

            load(0, 0)
            with sync.Fori(0, NCH // 2) as i:
                for c in range(2):
                    n = i * 2 + c
                    sync.wait_ge(s_y, n * CT + CT)
                    sync.sem_inc(s_mark, 1)
                    sync.dma_start(x1[:, c, :, :], x1_s[bass.ds(n * P, P), :, :]).then_inc(s_x[c], 16)
                    load(n + 1, 1 - c)

        @block.gpsimd
        def _(pool):
            pool.memset(ones[:, :], 1.0).then_inc(s_ones, 1)
            pool.sem_inc(s_lo, 8)
            pool.wait_ge(s_c, 2 * 16)

            def low_parts(n, c):
                for p in range(NP):
                    pool.wait_ge(s_hi, n * NP + p + 1)
                    pool.wait_ge(s_mm, n * NP + p + 1)
                    pool.tensor_tensor(lo[:, p, :, :], h[:, c * NP + p, :, :], hi[:, p, :, :], ALU.subtract).then_inc(s_lo, 1)

            low_parts(0, 0)
            with pool.Fori(0, NCH // 2) as i:
                for c in range(2):
                    pool.wait_ge(s_x[c], i * 16 + 16)
                    for t in range(CT):
                        pool.tensor_tensor(x1[:, c, t, :], x1[:, c, t, :], bias[:, :], ALU.add).then_inc(s_xb, 1)
                    low_parts(i * 2 + (c + 1), 1 - c)

        @block.vector
        def _(dve):
            steps = [0]

            def link(ins):
                steps[0] += 1
                ins.then_inc(s_chain, 1)
                dve.wait_ge(s_chain, steps[0])

            dve.sem_inc(s_y, 2 * CT)
            link(dve.tensor_reduce(both[:, 0:1], wout_high[:, :], axis=AX.X, op=ALU.max))
            dve.tensor_scalar(both[:, 1:2], h_max[:, :], 1e-8, None, ALU.max).then_inc(s_ones, 1)
            dve.wait_ge(s_ones, 2)
            spread_max(dve, "dve", both[:, :], 2, tops, acc[:, 0, :], ident, ones, s_pe0, s_top)
            link(dve.tensor_copy(sc[:, 0:2], acc[:, 0, P:P + 2]))
            link(dve.reciprocal(sc[:, 2:4], sc[:, 0:2]))
            link(dve.tensor_scalar(rel[:, :], wout_high[:, :], sc[:, 2:3], None, ALU.mult))
            link(dve.tensor_scalar(sc[:, 3:4], sc[:, 3:4], 32767.0, None, ALU.mult))
            link(dve.tensor_scalar(sc[:, 2:3], sc[:, 0:1], sc[:, 1:2], 1 / (127.0 * 32767.0), ALU.mult, ALU.mult))

            def integers(chunk, c, turn):
                for p in range(NP):
                    slot = c * NP + p
                    n = chunk * NP + p
                    v = h[:, slot, :, :]
                    dve.wait_ge(s_h[slot], turn * 16 + 16)
                    dve.tensor_scalar(v, v, sc[:, 3:4], 32767.0, ALU.mult, ALU.min).then_inc(s_int, 1)
                    dve.wait_ge(s_int, n * (2 + HP) + 1)
                    dve.tensor_scalar(v, v, -32768.0, ROUND, ALU.max, ALU.add).then_inc(s_int, 1)
                    dve.wait_ge(s_int, n * (2 + HP) + 2)
                    for f in range(HP):
                        dve.tensor_scalar(h[:, slot, f, :], h[:, slot, f, :], ROUND, rel[:, p * HP + f:p * HP + f + 1],
                                          ALU.subtract, ALU.mult).then_inc(s_int, 1)

            integers(0, 0, 0)
            with dve.Fori(0, NCH // 2) as i:
                for c in range(2):
                    integers(i * 2 + (c + 1), 1 - c, i + c)
                    dve.wait_ge(s_mm, (i * 2 + c) * NP + (NP + 4))
                    dve.wait_ge(s_xb, (i * 2 + c) * CT + CT)
                    dve.wait_ge(s_ys, (i * 2 + c) * 16 + 16)
                    for t in range(CT):
                        dve.scalar_tensor_tensor(y[:, t, :], acc[:, c * 4 + t, :], sc[:, 2:3], x1[:, c, t, :], ALU.mult, ALU.add).then_inc(s_y, 1)

        @block.scalar
        def _(act):
            act.sem_inc(s_ys, 16)

            def high_parts(chunk, c):
                for p in range(NP):
                    n = chunk * NP + p
                    act.wait_ge(s_int, (n + 1) * (2 + HP))
                    act.wait_ge(s_mm, n + 1)
                    act.activation(hi[:, p, :, :], h[:, c * NP + p, :, :], ACT.Copy).then_inc(s_hi, 1)

            high_parts(0, 0)
            with act.Fori(0, NCH // 2) as i:
                for c in range(2):
                    high_parts(i * 2 + (c + 1), 1 - c)
                    act.wait_ge(s_y, (i * 2 + c) * CT + (3 * CT))
                    act.dma_start(out[bass.ds((i * 2 + c) * CH, CH), :].rearrange("(t p) d -> p t d", p=P), y[:, :, :]).then_inc(s_ys, 16)
            act.wait_ge(s_ys, NCH * 16 + 16)

        @block.tensor
        def _(pe):
            pe.sem_inc(s_mm, 4)
            pe.wait_ge(s_c, 2 * 16)
            pe.wait_ge(s_ones, 2)
            spread_max(pe, "pe", both[:, :], 2, tops, acc[:, 0, :], ident, ones, s_pe0, s_top)
            pe.wait_ge(s_chain, 2)
            with pe.Fori(0, NCH // 2) as i:
                for c in range(2):
                    pe.wait_ge(s_y, (i * 2 + c) * CT + CT)
                    for p in range(NP):
                        pe.wait_ge(s_lo, i * 8 + (c * NP + p) + 9)
                        for f in range(HP):
                            for part in (hi, lo):
                                for t in range(CT):
                                    last = pe.matmul(acc[:, c * 4 + t, :], part[:, p, f, t * P:(t + 1) * P], wout16[:, p * HP + f, :],
                                                     start=(p == 0 and f == 0 and part is hi),
                                                     stop=(p == NP - 1 and f == HP - 1 and part is lo))
                        last.then_inc(s_mm, 1)


def constants(np):
    left = np.arange(1024, 2048) / 1024
    right = (math.log(2.0) / left).astype(np.float16)
    best = np.argmin(np.abs(left * right.astype(np.float64) - math.log(2.0)))
    left, right = np.float16(left[best]), right[best]
    key, tile = np.arange(S)[None, :], np.arange(KT)[:, None]
    below = key < P * tile
    within = key // P == tile
    tri = np.arange(P)[:, None] <= np.arange(P)[None, :]
    zero = np.float16(0)
    return {
        "step_q": np.repeat(np.where(within, left, zero)[:, None, :], 4, axis=1),
        "step_k": np.repeat(np.concatenate([np.full((2, S), MAX_ROW, np.float16), np.where(below, right, zero)])[:, None, :], 4, axis=1),
        "tri": np.where(tri, left, zero),
        "diag16": np.where(np.eye(P, dtype=bool), right, zero),
        "ident": np.eye(P, dtype=np.float32),
        "ident16": np.eye(P, dtype=np.float16),
    }


def build(nc, a, out):
    def dram(name, shape, dt=F32):
        return nc.dram_tensor(name, shape, dt, kind="Internal").ap()

    qT_s, kT_s, oT_s = (dram(n, [B * P, G, S]) for n in ("qT_s", "kT_s", "oT_s"))
    v_s = dram("v_s", [B * P, KT, D])
    x1_s = dram("x1_s", [NCH * P, CT, D])
    xnT_s = dram("xnT_s", [NCH * P, KD, CH])
    h_s = dram("h_s", [NCH * P, FT, CH])
    with ExitStack() as ctx:
        m = Space(nc, ctx, "all")
        s_mark = m.sem("mark")
        qkv_max, xn_max, h_max = m.sb("qkv_max", [P, 3]), m.sb("xn_max", [P, 1]), m.sb("h_max", [P, 1])
        wo_hi, wo_lo = m.sb("wo_hi", [P, KD, D], F16), m.sb("wo_lo", [P, KD, D], F16)
        w_inv, o_inv = m.sb("w_inv", [P, 4]), m.sb("o_inv", [P, 1])
        win16, win_high = m.sb("win16", [P, KD, F], F16), m.sb("win_high", [P, FT])
        wout16, wout_high = m.sb("wout16", [P, FT, D], F16), m.sb("wout_high", [P, FT])
        with ExitStack() as ctx_qkv:
            m = Space(nc, ctx_qkv, "qkv")
            w_hi, w_lo = m.sb("w_hi", [P, 3, KD, D], F16), m.sb("w_lo", [P, 3, KD, D], F16)
            ctx_max = m.sb("ctx_max", [P, 1])
            project_queries(nc, s_mark, a["x"], a["ctxT"], a["wq"], a["wk"], a["wv"], a["wo"], a["bq"], a["ident"], qT_s,
                            w_hi, w_lo, wo_hi, wo_lo, w_inv, qkv_max[:, 1:2], ctx_max)
            project_context(nc, s_mark, a["ctxT"], a["bk"], a["bv"], a["w_inT"], a["w_out"], a["ident"], a["ident16"], kT_s, v_s,
                            w_hi, w_lo, w_inv, ctx_max, qkv_max[:, 0:1], qkv_max[:, 2:3], win16, win_high, wout16, wout_high)
        attend(nc, s_mark, qT_s, kT_s, v_s, qkv_max, o_inv, a["ident"], a["ident16"], a["diag16"], a["tri"], a["step_q"], a["step_k"], oT_s)
        merge(nc, s_mark, a["x"], a["bo"], oT_s, wo_hi, wo_lo, w_inv[:, 3:4], o_inv, x1_s, xnT_s, xn_max, a["ident"])
        expand(nc, s_mark, a["b_in"], a["ident"], win16, win_high, xnT_s, xn_max, h_s, h_max)
        contract(nc, s_mark, a["b_out"], a["ident"], wout16, wout_high, h_s, h_max, x1_s, out)


def kernel(x, ctx_1024, L0_xattn_Wq, L0_xattn_bq, L0_xattn_Wk, L0_xattn_bk, L0_xattn_Wv, L0_xattn_bv,
           L0_xattn_Wo, L0_xattn_bo, L0_ffn_W_in, L0_ffn_b_in, L0_ffn_W_out, L0_ffn_b_out):
    import numpy as np
    import concourse.bacc as bacc
    from concourse.bass_utils import run_bass_kernel_spmd

    def rows(v):
        return np.ascontiguousarray(np.broadcast_to(np.asarray(v)[None, :], (P, len(v))))

    def cols(v):
        return np.ascontiguousarray(np.asarray(v).reshape(-1, P).T)

    arrays = {
        "x": np.ascontiguousarray(np.asarray(x).reshape(B * S, D)),
        "ctxT": np.ascontiguousarray(np.asarray(ctx_1024).reshape(B * S, D).T),
        "wq": np.asarray(L0_xattn_Wq), "wk": np.asarray(L0_xattn_Wk), "wv": np.asarray(L0_xattn_Wv), "wo": np.asarray(L0_xattn_Wo),
        "bq": cols(L0_xattn_bq), "bk": cols(L0_xattn_bk), "bv": rows(L0_xattn_bv), "bo": rows(L0_xattn_bo),
        "w_inT": np.ascontiguousarray(np.asarray(L0_ffn_W_in).T), "b_in": cols(L0_ffn_b_in),
        "w_out": np.asarray(L0_ffn_W_out), "b_out": rows(L0_ffn_b_out),
        **constants(np),
    }
    nc = bacc.Bacc("TRN2", target_bir_lowering=False, num_devices=1)
    a = {n: nc.dram_tensor(n, v.shape, mybir.dt.from_np(v.dtype), kind="ExternalInput").ap() for n, v in arrays.items()}
    out = nc.dram_tensor("out", (B * S, D), F32, kind="ExternalOutput").ap()
    build(nc, a, out)
    r = run_bass_kernel_spmd(nc, [arrays], core_ids=[0])
    return r.results[0]["out"].reshape(B, S, D)
```
